# Optimizing a Trainium2 kernel written in Bass

```python
import numpy as np
import jax
import jax.numpy as jnp

def _softmax(x, axis=-1):
    return jax.nn.softmax(x, axis=axis)

def _gelu(x):
    return jax.nn.gelu(x, approximate=True)

def _silu(x):
    return jax.nn.silu(x)

def _sigmoid(x):
    return jax.nn.sigmoid(x)

def _layernorm(x, axis=-1, eps=1e-05):
    m = jnp.mean(x, axis=axis, keepdims=True)
    v = jnp.var(x, axis=axis, keepdims=True)
    return (x - m) / jnp.sqrt(v + eps)

def _scatter_add(tgt, idx, src, axis=0):
    return tgt.at[idx].add(src)

def _segment_sum(src, seg, n):
    return jax.ops.segment_sum(src, seg, n)
kernel_name = 'mk_early_fusion_d1_tok_img256_r4_7dc271'

def setup_inputs(seed: int=0):
    np.random.seed(seed)
    _w = jnp.asarray

    def _rec_inputs():
        import jax
        import jax.numpy as jnp
        _rk = jax.random.key(seed)
        x = -0.000596345 + 1.00056 * jax.random.normal(jax.random.fold_in(_rk, 1), (32, 64, 64, 3), jnp.float32)
        txt = 0.0279957 + 0.402868 * jax.random.normal(jax.random.fold_in(_rk, 2), (32, 77, 64), jnp.float32)
        return (x, txt)
    x, txt = _rec_inputs()

    def _L0_tok_setup():
        import jax, jax.numpy as jnp
        import numpy as np
        M1, M2, WIDTH, LAYERS = (16, 16, 64, 4)
        B, H, W = (16, 64, 64)
        EPS = 1e-05

        def _spectral_conv(h, w1, w2):
            xf = jnp.fft.rfft2(h)
            top = jnp.einsum('bixy,ioxy->boxy', xf[:, :, :M1, :M2], w1)
            bot = jnp.einsum('bixy,ioxy->boxy', xf[:, :, -M1:, :M2], w2)
            of = jnp.zeros(xf.shape, dtype=xf.dtype)
            of = of.at[:, :, :M1, :M2].set(top)
            of = of.at[:, :, -M1:, :M2].set(bot)
            return jnp.fft.irfft2(of, s=(h.shape[-2], h.shape[-1]))
        key = jax.random.key(seed)
        ks = jax.random.split(key, 16)
        scale = 1.0 / (WIDTH * WIDTH)
        inp = {'x': jax.random.normal(ks[0], (B, H, W, 3), dtype=jnp.float32), 'fc0_w': jax.random.normal(ks[1], (3, WIDTH), dtype=jnp.float32) * 0.3, 'fc0_b': jnp.zeros((WIDTH,), jnp.float32), 'w1r': jax.random.normal(ks[2], (LAYERS, WIDTH, WIDTH, M1, M2), dtype=jnp.float32) * scale, 'w1i': jax.random.normal(ks[3], (LAYERS, WIDTH, WIDTH, M1, M2), dtype=jnp.float32) * scale, 'w2r': jax.random.normal(ks[4], (LAYERS, WIDTH, WIDTH, M1, M2), dtype=jnp.float32) * scale, 'w2i': jax.random.normal(ks[5], (LAYERS, WIDTH, WIDTH, M1, M2), dtype=jnp.float32) * scale, 'pw_w': jax.random.normal(ks[6], (LAYERS, WIDTH, WIDTH), dtype=jnp.float32) * (1.0 / np.sqrt(WIDTH)), 'pw_b': jnp.zeros((LAYERS, WIDTH), jnp.float32), 'gamma': jnp.ones((LAYERS, WIDTH), jnp.float32), 'beta': jnp.zeros((LAYERS, WIDTH), jnp.float32), 'fc1_w': jax.random.normal(ks[7], (WIDTH, 128), dtype=jnp.float32) * (1.0 / np.sqrt(WIDTH)), 'fc1_b': jnp.zeros((128,), jnp.float32), 'fc2_w': jax.random.normal(ks[8], (128, 1), dtype=jnp.float32) * (1.0 / np.sqrt(128.0)), 'fc2_b': jnp.zeros((1,), jnp.float32)}
        return inp
    _L0_tok_all = _L0_tok_setup()
    _L0_tok_in = {k: v for k, v in _L0_tok_all.items() if k in ('fc0_w', 'fc0_b', 'w1r', 'w1i', 'w2r', 'w2i', 'pw_w', 'pw_b', 'gamma', 'beta', 'fc1_w', 'fc1_b', 'fc2_w', 'fc2_b')}
    del _L0_tok_all

    def _L0_attn_setup():
        import jax, jax.numpy as jnp
        import numpy as np
        B, N, D, H = (4, 256, 64, 8)
        key = jax.random.key(seed)
        k1, k2, k3 = jax.random.split(key, 3)
        x = jax.random.normal(k1, (B, N, D), dtype=jnp.float32)
        Wqkv = jax.random.normal(k2, (D, 3 * D * H), dtype=jnp.float32) * 0.02
        bqkv = jnp.zeros((3 * D * H,), dtype=jnp.float32)
        W0 = jax.random.normal(k3, (D * H, D), dtype=jnp.float32) * 0.02
        b0 = jnp.zeros((D,), dtype=jnp.float32)
        return {'x': x, 'Wqkv': Wqkv, 'bqkv': bqkv, 'W0': W0, 'b0': b0}
    _L0_attn_all = _L0_attn_setup()
    _L0_attn_in = {k: v for k, v in _L0_attn_all.items() if k in ('Wqkv', 'bqkv', 'W0', 'b0')}
    del _L0_attn_all

    def _L0_ffn_setup():
        import jax, jax.numpy as jnp
        import numpy as np
        D_MODEL = 64
        N_EXPERTS = 16
        HIDDEN = 128
        SCALE = 0.02
        key = jax.random.key(seed)
        ks = jax.random.split(key, 5)
        x = jax.random.normal(ks[0], (4, 2048, D_MODEL), dtype=jnp.float32)
        gate_w = jax.random.normal(ks[1], (D_MODEL, N_EXPERTS), dtype=jnp.float32) * SCALE
        gate_b = jnp.zeros((N_EXPERTS,), dtype=jnp.float32)
        w1 = jax.random.normal(ks[2], (N_EXPERTS, D_MODEL, HIDDEN), dtype=jnp.float32) * SCALE
        w2 = jax.random.normal(ks[3], (N_EXPERTS, D_MODEL, HIDDEN), dtype=jnp.float32) * SCALE
        w3 = jax.random.normal(ks[4], (N_EXPERTS, HIDDEN, D_MODEL), dtype=jnp.float32) * SCALE
        return {'x': x, 'gate_w': gate_w, 'gate_b': gate_b, 'w1': w1, 'w2': w2, 'w3': w3}
    _L0_ffn_all = _L0_ffn_setup()
    _L0_ffn_in = {k: v for k, v in _L0_ffn_all.items() if k in ('gate_w', 'gate_b', 'w1', 'w2', 'w3')}
    del _L0_ffn_all
    return {'x': x, 'txt': txt, 'L0_tok_fc0_w': _L0_tok_in['fc0_w'], 'L0_tok_fc0_b': _L0_tok_in['fc0_b'], 'L0_tok_w1r': _L0_tok_in['w1r'], 'L0_tok_w1i': _L0_tok_in['w1i'], 'L0_tok_w2r': _L0_tok_in['w2r'], 'L0_tok_w2i': _L0_tok_in['w2i'], 'L0_tok_pw_w': _L0_tok_in['pw_w'], 'L0_tok_pw_b': _L0_tok_in['pw_b'], 'L0_tok_gamma': _L0_tok_in['gamma'], 'L0_tok_beta': _L0_tok_in['beta'], 'L0_tok_fc1_w': _L0_tok_in['fc1_w'], 'L0_tok_fc1_b': _L0_tok_in['fc1_b'], 'L0_tok_fc2_w': _L0_tok_in['fc2_w'], 'L0_tok_fc2_b': _L0_tok_in['fc2_b'], 'L0_attn_Wqkv': _L0_attn_in['Wqkv'], 'L0_attn_bqkv': _L0_attn_in['bqkv'], 'L0_attn_W0': _L0_attn_in['W0'], 'L0_attn_b0': _L0_attn_in['b0'], 'L0_ffn_gate_w': _L0_ffn_in['gate_w'], 'L0_ffn_gate_b': _L0_ffn_in['gate_b'], 'L0_ffn_w1': _L0_ffn_in['w1'], 'L0_ffn_w2': _L0_ffn_in['w2'], 'L0_ffn_w3': _L0_ffn_in['w3']}

def reference(x, txt, L0_tok_fc0_w, L0_tok_fc0_b, L0_tok_w1r, L0_tok_w1i, L0_tok_w2r, L0_tok_w2i, L0_tok_pw_w, L0_tok_pw_b, L0_tok_gamma, L0_tok_beta, L0_tok_fc1_w, L0_tok_fc1_b, L0_tok_fc2_w, L0_tok_fc2_b, L0_attn_Wqkv, L0_attn_bqkv, L0_attn_W0, L0_attn_b0, L0_ffn_gate_w, L0_ffn_gate_b, L0_ffn_w1, L0_ffn_w2, L0_ffn_w3):
    import jax
    import jax.numpy as jnp

    def _L0_tok_ref(x, fc0_w, fc0_b, w1r, w1i, w2r, w2i, pw_w, pw_b, gamma, beta, fc1_w, fc1_b, fc2_w, fc2_b):
        import jax, jax.numpy as jnp
        import numpy as np
        M1, M2, WIDTH, LAYERS = (16, 16, 64, 4)
        B, H, W = (16, 64, 64)
        EPS = 1e-05

        def _spectral_conv(h, w1, w2):
            xf = jnp.fft.rfft2(h)
            top = jnp.einsum('bixy,ioxy->boxy', xf[:, :, :M1, :M2], w1)
            bot = jnp.einsum('bixy,ioxy->boxy', xf[:, :, -M1:, :M2], w2)
            of = jnp.zeros(xf.shape, dtype=xf.dtype)
            of = of.at[:, :, :M1, :M2].set(top)
            of = of.at[:, :, -M1:, :M2].set(bot)
            return jnp.fft.irfft2(of, s=(h.shape[-2], h.shape[-1]))
        h = jnp.einsum('bhwi,ic->bhwc', x, fc0_w) + fc0_b
        h = h.transpose(0, 3, 1, 2)
        for l in range(LAYERS):
            sc = _spectral_conv(h, w1r[l] + 1j * w1i[l], w2r[l] + 1j * w2i[l])
            pw = jnp.einsum('bihw,oi->bohw', h, pw_w[l]) + pw_b[l][None, :, None, None]
            y = sc + pw
            mean = y.mean(axis=(0, 2, 3), keepdims=True)
            var = y.var(axis=(0, 2, 3), keepdims=True)
            y = (y - mean) * jax.lax.rsqrt(var + EPS)
            y = y * gamma[l][None, :, None, None] + beta[l][None, :, None, None]
            h = jax.nn.gelu(y, approximate=False)
        h = h.transpose(0, 2, 3, 1)
        h = jax.nn.gelu(h @ fc1_w + fc1_b, approximate=False)
        out = (h @ fc2_w + fc2_b).squeeze(-1)
        return out

    def _L0_attn_ref(x, Wqkv, bqkv, W0, b0):
        import jax, jax.numpy as jnp
        import numpy as np
        B, N, D, H = (4, 256, 64, 8)
        b, n, d = x.shape
        h = Wqkv.shape[1] // (3 * d)
        qkv = x @ Wqkv + bqkv
        q, k, v = jnp.reshape(qkv, (3, b, n, d, h))
        score = jnp.einsum('bnqh,btqh->bnth', q, k) * d ** (-0.5)
        attn = jax.nn.softmax(score, axis=1)
        av = jnp.einsum('bnnh,bnqh->bnqh', attn, v)
        out = av.reshape(b, n, d * h) @ W0 + b0
        return out

    def _L0_ffn_ref(x, gate_w, gate_b, w1, w2, w3):
        import jax, jax.numpy as jnp
        import numpy as np
        D_MODEL = 64
        N_EXPERTS = 16
        HIDDEN = 128
        SCALE = 0.02
        n_experts = w1.shape[0]
        logits = jnp.einsum('bsd,de->bse', x, gate_w) + gate_b
        probs = jax.nn.softmax(logits, axis=-1)
        top_probs, top_idx = jax.lax.top_k(probs, 2)
        top_probs = top_probs / jnp.sum(top_probs, axis=-1, keepdims=True)
        dispatch = jnp.sum(jax.nn.one_hot(top_idx, n_experts, dtype=x.dtype) * top_probs[..., None], axis=-2)
        h1 = jnp.einsum('bsd,edh->bseh', x, w1)
        h2 = jnp.einsum('bsd,edh->bseh', x, w2)
        hidden = jax.nn.silu(h1) * h2
        expert_out = jnp.einsum('bseh,eho->bseo', hidden, w3)
        return jnp.einsum('bseo,bse->bso', expert_out, dispatch)
    h = _L0_tok_ref(x, L0_tok_fc0_w, L0_tok_fc0_b, L0_tok_w1r, L0_tok_w1i, L0_tok_w2r, L0_tok_w2i, L0_tok_pw_w, L0_tok_pw_b, L0_tok_gamma, L0_tok_beta, L0_tok_fc1_w, L0_tok_fc1_b, L0_tok_fc2_w, L0_tok_fc2_b)
    h = jnp.concatenate([h, txt], axis=1)
    h = h + _L0_attn_ref(_layernorm(h, axis=-1), L0_attn_Wqkv, L0_attn_bqkv, L0_attn_W0, L0_attn_b0)
    h = h + _L0_ffn_ref(_layernorm(h, axis=-1), L0_ffn_gate_w, L0_ffn_gate_b, L0_ffn_w1, L0_ffn_w2, L0_ffn_w3)
    return h

_drawn_inputs = setup_inputs


def setup_inputs(seed=0):
    import zlib

    import numpy as np

    out = dict(_drawn_inputs(seed))
    spreads = {'L0_tok_fc0_b': (0.0, 0.8),
     'L0_tok_pw_b': (0.0, 0.8),
     'L0_tok_gamma': (1.0, 0.2),
     'L0_tok_beta': (0.0, 0.1),
     'L0_tok_fc1_b': (0.0, 0.1),
     'L0_attn_bqkv': (0.0, 0.8),
     'L0_attn_b0': (0.0, 0.1),
     'L0_ffn_gate_b': (0.0, 0.8)}
    factors = {'L0_tok_w1r': 8.0,
     'L0_tok_w1i': 8.0,
     'L0_tok_w2r': 8.0,
     'L0_tok_w2i': 8.0,
     'L0_attn_Wqkv': 8.0,
     'L0_attn_W0': 8.0,
     'L0_ffn_gate_w': 8.0,
     'L0_ffn_w1': 8.0,
     'L0_ffn_w2': 8.0,
     'L0_ffn_w3': 8.0}
    for name, (base, spread) in spreads.items():
        noise = np.random.default_rng([zlib.crc32(name.encode()), seed]).standard_normal(out[name].shape)
        drawn = base * np.exp(spread * noise) if base else spread * noise
        out[name] = jnp.asarray(drawn.astype(out[name].dtype))
    for name, factor in factors.items():
        out[name] = (out[name] * factor).astype(out[name].dtype)
    return out
```

```python
import numpy as np
import concourse.bass as bass
from concourse import mybir
from contextlib import ExitStack

IMG, SIDE, CH, WIDTH, LAYERS = 32, 64, 3, 64, 4
M1, M2 = 16, 16
PAIRS = IMG // 2
PX = SIDE * SIDE
KY, KX = 2 * M1, M2
MODES = KY * KX
CHUNKS = 4
CM = MODES // CHUNKS
HIDDEN1 = 128
TXT, D = 77, 64
SEQ = SIDE + TXT
TOK = IMG * SEQ
EPS = 1e-5


def dft_constants():
    w = 2 * np.pi / SIDE
    pos, kx = np.arange(SIDE), np.arange(KX)
    ky = np.concatenate([np.arange(M1), np.arange(SIDE - M1, SIDE)])
    ident = np.eye(128)
    f1 = np.zeros((2, SIDE, 2, KX, 2))
    for r in range(2):
        f1[r, :, r, :, 0] = np.cos(w * np.outer(pos, kx))
        f1[r, :, r, :, 1] = -np.sin(w * np.outer(pos, kx))
    f2 = np.zeros((2, SIDE, 2, KY))
    c, s = np.cos(w * np.outer(pos, ky)), np.sin(w * np.outer(pos, ky))
    f2[0, :, 0], f2[1, :, 0], f2[0, :, 1], f2[1, :, 1] = c, s, -s, c
    i1 = np.zeros((2, 2, KY, 2, SIDE))
    i1[:, 0, :, 0], i1[:, 1, :, 0], i1[:, 0, :, 1], i1[:, 1, :, 1] = c.T, -s.T, s.T, c.T
    i2 = np.zeros((4, KX, 2, 4, SIDE))
    g = np.where(kx == 0, 1.0, 2.0)[:, None] / PX
    for r in range(4):
        i2[r, :, 0, r] = g * np.cos(w * np.outer(kx, pos))
        i2[r, :, 1, r] = -g * np.sin(w * np.outer(kx, pos))
    avg = (np.arange(128)[:, None] % 64 == np.arange(128)[None] % 64) * 0.5
    parts = [ident, f1.reshape(128, 64), f2.reshape(128, 64), i1.reshape(128, 128), i2.reshape(128, 256), avg]
    return np.concatenate(parts, axis=1).astype(np.float32)


NCONST = 128 + 64 + 64 + 128 + 256 + 128


def build_fno(nc, small, x6, fc0, fc0T, fc0b, wmix, pwT, pwb, gamma, beta, consts, z_d, X_d, G_d, layers=LAYERS):
    f32 = mybir.dt.float32
    ALU, ACT, AX = mybir.AluOpType, mybir.ActivationFunctionType, mybir.AxisListType
    ctx = ExitStack()
    with ctx:
        def sb(name, shape):
            return ctx.enter_context(nc.sbuf_tensor(name, shape, f32))

        def sem(name):
            return ctx.enter_context(nc.semaphore(name))

        W = sb("W", [128, CHUNKS, CM * WIDTH])
        work = sb("work", [128, 18432])
        cst = sb("cst", [128, NCONST])
        wbd = sb("wbd", [128, 128])
        wc6 = sb("wc6", [6, 128])
        P = [ctx.enter_context(nc.psum_tensor(f"P{i}", [128, 512], f32)) for i in range(8)]
        ident, f1r, f2r = cst[:, 0:128], cst[:, 128:192], cst[:, 192:256]
        i1r, i2r, avg = cst[:, 256:384], cst[:, 384:640], cst[:, 640:768]

        def part(off, n):
            return work[:, off:off + n]
        zbuf = [part(0, 4096), part(4096, 4096)]
        hT = [part(8192, 1024), part(9216, 1024)]
        hT2 = [part(10240, 512), part(10752, 512)]
        A1 = [part(11264, 2048), part(13312, 2048)]
        Xs = [part(15360, 1536), part(16896, 1536)]
        XM = [part(0, 8192), part(8192, 8192)]
        Gs = [part(16384, 1024), part(17408, 1024)]
        Ai = [part(8192, 2048), part(10240, 2048)]
        AT = [part(12288, 512), part(12800, 512)]
        Gt = part(13312, 2048)
        ybuf = [part(15360, 1024), part(16384, 1024)]
        stats = part(17408, 768)
        xall = work[0:96, 0:4096]
        sel0 = work[0:96, 4096:6144]
        Xx = work[0:96, 6144:7168]
        fc0Tbd = small[:, 16:22]
        fc0b_c, pwb_c, gam_c, bet_c = (small[:, i:i + 1] for i in range(4))
        bias0, mv, e2, st2 = small[:, 4:5], small[:, 6:8], small[:, 8:9], small[:, 10:12]
        bsc, bbi = small[:, 12:13], small[:, 13:14]
        rstd, std = small[:, 14:15], small[:, 15:16]
        fc0b4k = small[:, 24:25]
        tmp = small[:, 26:28]
        eps_c, minus = small[:, 28:29], small[:, 29:30]

        S = {n: sem(n) for n in (
            "s_const", "s_zero", "s_w0", "s_par", "s_parload",
            "a0_pe", "a0_ev", "a0_mx", "a0_re", "a0_im", "a0_dc", "a0_neg",
            "z_gelu", "pT1", "pF1", "pT2", "pF2", "eT1", "eF1", "eT2", "eF2", "neg",
            "pM", "eMd", "eMa",
            "pI1", "pT3", "pY", "eI1", "eT3", "eY", "eS", "z_gelu_c",
            "pe_phase", "act_phase", "dve_phase", "pool_phase", "chain", "pStat", "eStat", "sAggr", "sVar", "sRstd",
            "x0_load", "dbg")}
        zl = [[sem(f"zl{u}{q}") for q in range(4)] for u in range(2)]
        wl = [sem(f"wl{c}") for c in range(CHUNKS)]
        xl = [sem(f"xl{u}") for u in range(2)]
        gl = [sem(f"gl{u}") for u in range(2)]
        xst = [sem(f"xst{u}") for u in range(2)]
        gst = [sem(f"gst{u}") for u in range(2)]
        yst = [sem(f"yst{u}") for u in range(2)]

        z_q = z_d.rearrange("(t u) p (q n) -> t u p q n", u=2, q=4)
        x6_q = x6.rearrange("(t u) p (q n) -> t u p q n", u=2, q=4)
        X_s = X_d.rearrange("r k c (h t u) m -> t u h c (r k) m", h=2, u=2)
        G_s = G_d.rearrange("(h t u) r y (k o) -> h t u (r y) k o", h=2, u=2, o=WIDTH)
        G_w = G_d.rearrange("i r k n -> k r i n")

        def wait(eng, s, v):
            if not isinstance(v, int) or v > 0:
                eng.wait_ge(S[s] if isinstance(s, str) else s, v)

        class At:
            def __init__(self, t, u, q, lag):
                d = q - lag
                back, self.q = -(d // 4), d % 4
                self.par = (u - back) % 2
                self.t = t + (u - back) // 2
                self.pair = self.t * 2 + self.par
                self.s = self.pair * 4 + self.q
                self.ok = not isinstance(self.pair, int) or 0 <= self.pair < PAIRS

        def over_steps(eng, body, last=PAIRS // 2 + 1):
            for u in range(2):
                for q in range(4):
                    body(0, u, q)
            with eng.Fori(1, PAIRS // 2) as t:
                for u in range(2):
                    for q in range(4):
                        body(t, u, q)
            for u in range(2):
                for q in range(4):
                    body(PAIRS // 2, u, q)

        OTHERS = {"pe": "act dve pool", "act": "pe dve pool", "dve": "pe act pool", "pool": "pe act dve", "sp": "pe act dve pool"}

        def enter(eng, who, n):
            for o in OTHERS[who].split():
                eng.wait_ge(S[o + "_phase"], n)

        def leave(eng, who):
            eng.drain().then_inc(S[who + "_phase"], 1)

        block = ctx.enter_context(nc.Block())

        @block.sync
        def _(sp):
            sp.dma_start(cst[:, :], consts).then_inc(S["s_const"], 16)
            sp.dma_start(xall, x6.rearrange("b p n -> (b p) n")).then_inc(S["x0_load"], 16)
            for c in range(CHUNKS):
                sp.dma_start(W[:, c, :], wmix[0, c]).then_inc(wl[c], 16)
            sp.wait_ge(S["s_zero"], 2)
            for b in range(PAIRS):
                for h in range(2):
                    r = b * 6 + h * 3
                    sp.dma_start(sel0[r:r + 3, b * 128 + h * 64:b * 128 + h * 64 + 64], fc0).then_inc(S["s_w0"], 16)
            for h in range(2):
                o = slice(h * 64, h * 64 + 64)
                sp.dma_start(fc0Tbd[o, h * 3:h * 3 + 3], fc0T).then_inc(S["s_w0"], 16)
                sp.dma_start(fc0b_c[o, :], fc0b).then_inc(S["s_w0"], 16)

            def layer_parameters(l):
                for h in range(2):
                    o = slice(h * 64, h * 64 + 64)
                    sp.dma_start(wbd[o, o], pwT[l]).then_inc(S["s_parload"], 16)
                    for dst, src in ((pwb_c, pwb), (gam_c, gamma), (bet_c, beta)):
                        sp.dma_start(dst[o, :], src[l]).then_inc(S["s_parload"], 16)

            def mix_loads(l):
                enter(sp, "sp", 3 * l + 1)

                def xm(c):
                    if c >= 2:
                        sp.wait_ge(S["pM"], l * 64 + 16 * (c - 1))
                    for v, h, plane in ((0, 0, 0), (0, 1, 2), (1, 0, 1), (1, 1, 0)):
                        sp.dma_start(XM[c % 2][h * 64:h * 64 + 64, v * 4096:v * 4096 + 4096],
                                     X_d[plane, c].rearrange("c i m -> c (i m)")).then_inc(xl[c % 2], 16)
                layer_parameters(l)
                xm(0)
                xm(1)
                for c in range(CHUNKS):
                    if c + 2 < CHUNKS:
                        xm(c + 2)
                    if not isinstance(l, int) or l + 1 < LAYERS:
                        sp.wait_ge(S["pM"], l * 64 + 16 * (c + 1))
                        sp.dma_start(W[:, c, :], wmix[l + 1, c]).then_inc(wl[c], 16)

            def inv_loads(l, first):
                enter(sp, "sp", 3 * l + 2)

                def step(t, u, q):
                    a = At(t, u, q, 0)
                    if not a.ok:
                        return
                    inner = not isinstance(a.pair, int)
                    if q == 0:
                        if inner:
                            sp.wait_ge(S["pI1"], l * 64 + a.pair * 4 - 4)
                        for h in range(2):
                            sp.dma_start(Gt[u * 64:u * 64 + 64, :].rearrange("p (k h o) -> p h k o", h=2, o=WIDTH)[:, h], G_s[h, a.t, u]).then_inc(gl[u], 16)
                    if inner:
                        sp.wait_ge(S["pY"], l * 128 + a.s * 2 - 14)
                    o = slice(q * 1024, q * 1024 + 1024)
                    if first:
                        sp.dma_start(zbuf[u][0:6, o], x6_q[a.t, u, :, q]).then_inc(zl[u][q], 16)
                    else:
                        sp.dma_start(zbuf[u][:, o], z_q[a.t, u, :, q]).then_inc(zl[u][q], 16)
                over_steps(sp, step)

            def fwd_loads(l):
                enter(sp, "sp", 3 * l)

                def step(t, u, q):
                    a = At(t, u, q, 0)
                    if not a.ok:
                        return
                    if not isinstance(a.pair, int):
                        sp.wait_ge(S["pT1"], (l - 1) * 128 + a.s * 2 - 14)
                    o = slice(q * 1024, q * 1024 + 1024)
                    sp.dma_start(zbuf[u][:, o], z_q[a.t, u, :, q]).then_inc(zl[u][q], 16)
                over_steps(sp, step)
            mix_loads(0)
            inv_loads(0, True)
            for l in range(1, layers):
                fwd_loads(l)
                mix_loads(l)
                inv_loads(l, False)

        def z_loads_before(l, phase):
            return (l * 2 - 1 if phase == "A" else l * 2) * 8 * 16

        @block.gpsimd
        def _(pool):
            nc.gpsimd.memset(sel0, 0.0)
            nc.gpsimd.memset(small[:, :], 0.0)
            nc.gpsimd.memset(wbd[:, :], 0.0).then_inc(S["s_zero"], 1)
            pool.wait_ge(S["s_zero"], 1)
            nc.gpsimd.memset(eps_c, EPS)
            nc.gpsimd.memset(minus, -1.0).then_inc(S["s_zero"], 1)
            pool.wait_ge(S["s_zero"], 2)

            def negate_and_store(a, negs, n_before, t, u):
                Xu = Xs[u]
                nc.gpsimd.tensor_tensor(Xu[:, 1024:1536], Xu[:, 512:1024], minus.broadcast_to([128, 512]), ALU.mult).then_inc(S[negs], 1)
                pool.wait_ge(S[negs], n_before + 1)
                for h in range(2):
                    pool.dma_start(X_s[t, u, h], Xu[h * 64:h * 64 + 64, :].rearrange("p (k m) -> p k m", m=CM)).then_inc(xst[u], 16)

            for b in range(PAIRS):
                pool.wait_ge(S["a0_im"], b + 1)
                pool.wait_ge(S["a0_dc"], b + 1)
                negate_and_store(None, "a0_neg", b, b // 2, b % 2)
            for u in range(2):
                pool.wait_ge(xst[u], 8 * 32)
            leave(pool, "pool")

            def mix(l):
                enter(pool, "pool", 3 * l + 1)
                for k in range(KY):
                    pool.wait_ge(S["eMd"], l * 32 + k + 1)
                    pool.wait_ge(S["eMa"], l * 32 + k + 1)
                    pool.dma_start(G_w[k], Gs[k % 2][0:64, :]).then_inc(gst[k % 2], 16)
                for u in range(2):
                    pool.wait_ge(gst[u], (l + 1) * 16 * 16)
                leave(pool, "pool")

            def inv(l):
                enter(pool, "pool", 3 * l + 2)

                def step(t, u, q):
                    a = At(t, u, q, 6)
                    if not a.ok:
                        return
                    pool.wait_ge(S["eY"], l * 128 + a.s * 2 + 2)
                    pool.dma_start(z_q[a.t, a.par, :, a.q], ybuf[a.q % 2]).then_inc(yst[a.q % 2], 16)
                over_steps(pool, step)
                for u in range(2):
                    pool.wait_ge(yst[u], (l + 1) * 32 * 16)
                leave(pool, "pool")

            def fwd(l):
                enter(pool, "pool", 3 * l)

                def step(t, u, q):
                    a = At(t, u, q, 8)
                    if not a.ok or a.q != 3:
                        return
                    pool.wait_ge(S["eF2"], (l - 1) * 32 + a.pair * 2 + 4)
                    negate_and_store(a, "neg", (l - 1) * 16 + a.pair, a.t, a.par)
                over_steps(pool, step)
                for u in range(2):
                    pool.wait_ge(xst[u], (l + 1) * 8 * 32)
                leave(pool, "pool")
            mix(0)
            inv(0)
            for l in range(1, layers):
                fwd(l)
                mix(l)
                inv(l)

        @block.tensor
        def _(pe):
            nc.tensor.nop().then_inc(S["pF2"], 1)
            pe.wait_ge(S["s_const"], 16)
            pe.wait_ge(S["x0_load"], 16)

            def tr(out, in_):
                n = in_.shape[0]
                return nc.tensor.matmul(out, in_, ident[0:n, 0:n], start=True, stop=True, is_transpose=True)

            n = 0
            for g in range(4):
                for h in range(2):
                    for i in range(4):
                        last = tr(P[h][:, i * 128:i * 128 + 96], xall[:, g * 1024 + h * 512 + i * 128:g * 1024 + h * 512 + i * 128 + 128])
                    last.then_inc(S["a0_pe"], 1)
                    n += 1
                    pe.wait_ge(S["a0_ev"], n)
                for i in range(8):
                    last = nc.tensor.matmul(P[3][0:96, i * 64:i * 64 + 64], hT[0][:, i * 128:i * 128 + 96], f1r, start=True, stop=True)
                last.then_inc(S["a0_pe"], 1)
                n += 1
                pe.wait_ge(S["a0_ev"], n)
            for g in range(4):
                for i in range(4):
                    last = tr(P[0][:, i * 128:i * 128 + 96], A1[0][0:96, (4 * g + i) * 128:(4 * g + i) * 128 + 128])
                last.then_inc(S["a0_pe"], 1)
                n += 1
                pe.wait_ge(S["a0_ev"], n)
                for i in range(4):
                    last = nc.tensor.matmul(P[1][0:96, i * 64:i * 64 + 64], hT2[0][:, i * 128:i * 128 + 96], f2r, start=True, stop=True)
                last.then_inc(S["a0_pe"], 1)
                n += 1
                pe.wait_ge(S["a0_ev"], n)
            pe.wait_ge(S["s_w0"], 36 * 16)
            for b in range(PAIRS):
                if b >= 2:
                    pe.wait_ge(S["a0_re"], b - 1)
                    pe.wait_ge(S["a0_im"], b - 1)
                for r in range(2):
                    last = nc.tensor.matmul(P[2 * (b % 2) + r][:, :], sel0[:, b * 128:b * 128 + 128], Xx[:, r * 512:r * 512 + 512], start=True, stop=True)
                last.then_inc(S["a0_mx"], 1)
            leave(pe, "pe")

            def mix(l):
                enter(pe, "pe", 3 * l + 1)
                for n in range(64):
                    c, g = n // 16, n % 16
                    if g == 0:
                        pe.wait_ge(wl[c], (l + 1) * 16)
                        pe.wait_ge(xl[c % 2], (l * 2 + c // 2 + 1) * 64)
                    if n >= 4:
                        pe.wait_ge(S["eMd" if n % 2 == 0 else "eMa"], l * 32 + (n - 4) // 2 + 1)
                    xm = XM[c % 2].rearrange("p (i m) -> p i m", m=CM)
                    for i in range(8):
                        m = g * 8 + i
                        last = nc.tensor.matmul(P[n % 4][0:64, i * 64:i * 64 + 64], xm[:, :, m], W[:, c, m * 64:m * 64 + 64], start=True, stop=True)
                    last.then_inc(S["pM"], 1)
                leave(pe, "pe")

            def inv(l, first):
                enter(pe, "pe", 3 * l + 2)
                pe.wait_ge(S["s_parload"], (l + 1) * 128)
                if first:
                    nc.tensor.matmul(P[7][0:6, 0:128], fc0Tbd, wbd[:, :], start=True, stop=True)
                    nc.tensor.matmul(P[6][:, 0:1], wbd[:, :], fc0b_c, start=True, stop=True).then_inc(S["pStat"], 1)
                    pe.wait_ge(S["eStat"], 1)

                def step(t, u, q):
                    a = At(t, u, q, 5)
                    if a.ok:
                        wait(pe, "eI1", l * 64 + a.pair * 4 + 4)
                        wait(pe, "eT3", l * 64 + a.s - 1 if not first or not isinstance(a.s, int) else a.s - 1)
                        for i in range(4):
                            j = 4 * a.q + i
                            last = tr(P[2 + a.q % 2][:, i * 128:i * 128 + 128], Ai[a.par][:, j * 128:j * 128 + 128])
                        last.then_inc(S["pT3"], 1)
                    a = At(t, u, q, 0)
                    if a.ok:
                        wait(pe, gl[a.par], l * 256 + a.t * 32 + 32)
                        wait(pe, "eI1", l * 64 + a.s - 1)
                        half = slice(a.par * 64, a.par * 64 + 64)
                        for i in range(4):
                            last = nc.tensor.matmul(P[a.q % 2][:, i * 128:i * 128 + 128], Gt[half, (4 * a.q + i) * 128:(4 * a.q + i) * 128 + 128], i1r[half, :], start=True, stop=True)
                        last.then_inc(S["pI1"], 1)
                    a = At(t, u, q, 6)
                    if a.ok:
                        if first:
                            wait(pe, zl[a.par][a.q], a.t * 16 + 16)
                        else:
                            wait(pe, "z_gelu_c", (l - 1) * 64 + a.s + 1)
                        wait(pe, "eT3", l * 64 + a.s + 1)
                        for h in range(2):
                            bank = P[4 + 2 * (a.q % 2) + h]
                            wait(pe, "eY", l * 128 + a.s * 2 + h - 3)
                            o = slice(a.q * 1024 + h * 512, a.q * 1024 + h * 512 + 512)
                            if first:
                                nc.tensor.matmul(bank[:, :], wc6[:, :], zbuf[a.par][0:6, o], start=True, stop=False)
                            else:
                                nc.tensor.matmul(bank[:, :], wbd[:, :], zbuf[a.par][:, o], start=True, stop=False)
                            for i in range(2):
                                last = nc.tensor.matmul(bank[:, i * 256:i * 256 + 256], AT[a.q % 2][:, (2 * h + i) * 128:(2 * h + i) * 128 + 128], i2r, start=False, stop=i == 1)
                            last.then_inc(S["pY"], 1)
                over_steps(pe, step)
                pe.wait_ge(S["sAggr"], l + 1)
                nc.tensor.matmul(P[0][:, 0:2], avg, st2, start=True, stop=True).then_inc(S["pStat"], 1)
                leave(pe, "pe")

            def fwd(l):
                enter(pe, "pe", 3 * l)

                def step(t, u, q):
                    a = At(t, u, q, 2)
                    if a.ok:
                        wait(pe, "z_gelu", (l - 1) * 64 + a.s + 1)
                        for h in range(2):
                            wait(pe, "eT1", (l - 1) * 128 + a.s * 2 + h - 1)
                            for i in range(4):
                                o = a.q * 1024 + h * 512 + i * 128
                                last = tr(P[h][:, i * 128:i * 128 + 128], zbuf[a.par][:, o:o + 128])
                            last.then_inc(S["pT1"], 1)
                    a = At(t, u, q, 8)
                    if a.ok:
                        wait(pe, "eT2", (l - 1) * 64 + a.s + 1)
                        if a.q % 2 == 0:
                            wait(pe, "eF2", (l - 1) * 32 + a.pair * 2 + a.q // 2 + 1)
                        for i in range(4):
                            o = ((a.q % 2) * 4 + i) * 64
                            last = nc.tensor.matmul(P[5 + a.q // 2][:, o:o + 64], hT2[a.q % 2][:, i * 128:i * 128 + 128], f2r, start=True, stop=True)
                        last.then_inc(S["pF2"], 1)
                    a = At(t, u, q, 7)
                    if a.ok:
                        wait(pe, "eF1", (l - 1) * 64 + a.pair * 4 + 4)
                        wait(pe, "eT2", (l - 1) * 64 + a.s)
                        for i in range(4):
                            last = tr(P[2][:, i * 128:i * 128 + 128], A1[a.par][:, (4 * a.q + i) * 128:(4 * a.q + i) * 128 + 128])
                        last.then_inc(S["pT2"], 1)
                    a = At(t, u, q, 3)
                    if a.ok:
                        wait(pe, "eT1", (l - 1) * 128 + a.s * 2 + 2)
                        wait(pe, "eF1", (l - 1) * 64 + a.s - 1)
                        for i in range(8):
                            last = nc.tensor.matmul(P[3 + a.q % 2][:, i * 64:i * 64 + 64], hT[a.q % 2][:, i * 128:i * 128 + 128], f1r, start=True, stop=True)
                        last.then_inc(S["pF1"], 1)
                over_steps(pe, step)
                leave(pe, "pe")
            mix(0)
            inv(0, True)
            for l in range(1, layers):
                fwd(l)
                mix(l)
                inv(l, False)

        @block.scalar
        def _(act):
            act.wait_ge(S["s_w0"], 36 * 16)
            for b in range(PAIRS):
                act.wait_ge(S["a0_mx"], b + 1)
                if b >= 2:
                    act.wait_ge(xst[b % 2], 32 * (b // 2))
                nc.scalar.activation(Xs[b % 2][:, 0:512], P[2 * (b % 2)][:, :], ACT.Copy).then_inc(S["a0_re"], 1)
            leave(act, "act")

            def mix(l):
                enter(act, "act", 3 * l + 1)
                for k in range(KY):
                    n = 2 * k + 1
                    act.wait_ge(S["pM"], l * 64 + n + 1)
                    v = l * 256 + 16 * (k // 2)
                    wait(act, gst[k % 2], v if k >= 2 else 0)
                    nc.scalar.activation(Gs[k % 2][0:64, 512:1024], P[n % 4][0:64, :], ACT.Copy).then_inc(S["eMa"], 1)
                leave(act, "act")

            def inv(l, first):
                enter(act, "act", 3 * l + 2)

                def step(t, u, q):
                    a = At(t, u, q, 4)
                    if a.ok and not first:
                        wait(act, zl[a.par][a.q], z_loads_before(l, "C") + a.t * 16 + 16)
                        o = slice(a.q * 1024, a.q * 1024 + 1024)
                        nc.scalar.activation(zbuf[a.par][:, o], zbuf[a.par][:, o], ACT.Gelu, bias=bbi, scale=bsc).then_inc(S["z_gelu_c"], 1)
                    a = At(t, u, q, 6)
                    if a.ok:
                        for h in range(2):
                            act.wait_ge(S["pY"], l * 128 + a.s * 2 + h + 1)
                            if h == 0:
                                wait(act, yst[a.q % 2], stores_waited(l, a))
                                wait(act, "eS", l * 128 + a.s * 2 - 2)
                            nc.scalar.activation(ybuf[a.q % 2][:, h * 512:h * 512 + 512], P[4 + 2 * (a.q % 2) + h][:, :], ACT.Identity, bias=bias0 if first else pwb_c).then_inc(S["eY"], 1)
                if first:
                    act.wait_ge(S["eStat"], 1)
                act.wait_ge(S["s_parload"], (l + 1) * 128)
                over_steps(act, step)
                act.wait_ge(S["sVar"], l + 1)
                nc.scalar.activation(std, e2, ACT.Sqrt, bias=eps_c).then_inc(S["sRstd"], 1)
                leave(act, "act")

            def stores_waited(l, a):
                return l * 32 * 16 + (a.pair * 2 + a.q // 2) * 16 if not isinstance(a.pair, int) or a.s >= 2 else 0

            def fwd(l):
                enter(act, "act", 3 * l)

                def step(t, u, q):
                    a = At(t, u, q, 0)
                    if a.ok:
                        wait(act, zl[a.par][a.q], z_loads_before(l, "A") + a.t * 16 + 16)
                        o = slice(a.q * 1024, a.q * 1024 + 1024)
                        nc.scalar.activation(zbuf[a.par][:, o], zbuf[a.par][:, o], ACT.Gelu, bias=bbi, scale=bsc).then_inc(S["z_gelu"], 1)
                    a = At(t, u, q, 3)
                    if a.ok:
                        act.wait_ge(S["pF1"], (l - 1) * 64 + a.s + 1)
                        nc.scalar.activation(A1[a.par].rearrange("p (k y) -> p y k", y=SIDE)[:, 16 * a.q:16 * a.q + 16],
                                             P[3 + a.q % 2][:, :].rearrange("p (y k) -> p y k", k=2 * KX), ACT.Copy).then_inc(S["eF1"], 1)
                    a = At(t, u, q, 8)
                    if a.ok and a.q % 2 == 1:
                        g = a.q // 2
                        act.wait_ge(S["pF2"], (l - 1) * 64 + a.s + 2)
                        if g == 0 and (not isinstance(a.pair, int) or a.pair >= 2):
                            wait(act, xst[a.par], l * 256 + a.t * 32)
                        out = Xs[a.par][:, 0:1024].rearrange("p (r y k) -> p k r y", r=2, k=KX)[:, 8 * g:8 * g + 8]
                        nc.scalar.activation(out, P[5 + g][:, :].rearrange("p (k r y) -> p k r y", k=8, r=2), ACT.Copy).then_inc(S["eF2"], 1)
                over_steps(act, step)
                leave(act, "act")
            mix(0)
            inv(0, True)
            for l in range(1, layers):
                fwd(l)
                mix(l)
                inv(l, False)

        @block.vector
        def _(dve):
            chained = [0]

            def link(ins):
                chained[0] += 1
                ins.then_inc(S["chain"], 1)
                dve.wait_ge(S["chain"], chained[0])
            nc.vector.nop().then_inc(S["eF2"], 2)
            n = 0
            for g in range(4):
                for h in range(2):
                    n += 1
                    dve.wait_ge(S["a0_pe"], n)
                    nc.vector.tensor_copy(hT[0][:, h * 512:h * 512 + 512].rearrange("p (i c) -> p i c", c=128)[:, :, 0:96],
                                          P[h][:, :].rearrange("p (i c) -> p i c", c=128)[:, :, 0:96]).then_inc(S["a0_ev"], 1)
                n += 1
                dve.wait_ge(S["a0_pe"], n)
                nc.vector.tensor_copy(A1[0][0:96, :].rearrange("p (k y) -> p y k", y=SIDE)[:, 16 * g:16 * g + 16],
                                      P[3][0:96, :].rearrange("p (y k) -> p y k", k=2 * KX)).then_inc(S["a0_ev"], 1)
            for g in range(4):
                n += 1
                dve.wait_ge(S["a0_pe"], n)
                nc.vector.tensor_copy(hT2[0][:, 0:512].rearrange("p (i c) -> p i c", c=128)[:, :, 0:96],
                                      P[0][:, :].rearrange("p (i c) -> p i c", c=128)[:, :, 0:96]).then_inc(S["a0_ev"], 1)
                n += 1
                dve.wait_ge(S["a0_pe"], n)
                nc.vector.tensor_copy(Xx.rearrange("p (r y k) -> p k r y", r=2, k=KX)[:, 4 * g:4 * g + 4],
                                      P[1][0:96, 0:256].rearrange("p (k r y) -> p k r y", k=4, r=2)).then_inc(S["a0_ev"], 1)
            dve.wait_ge(S["s_w0"], 36 * 16)
            link(nc.vector.tensor_scalar(fc0b4k, fc0b_c, float(PX), None, ALU.mult))
            for b in range(PAIRS):
                dve.wait_ge(S["a0_mx"], b + 1)
                if b >= 2:
                    dve.wait_ge(xst[b % 2], 32 * (b // 2))
                nc.vector.tensor_copy(Xs[b % 2][:, 512:1024], P[2 * (b % 2) + 1][:, :]).then_inc(S["a0_im"], 1)
                dve.wait_ge(S["a0_re"], b + 1)
                nc.vector.tensor_tensor(Xs[b % 2][:, 0:1], Xs[b % 2][:, 0:1], fc0b4k, ALU.add).then_inc(S["a0_dc"], 1)
            leave(dve, "dve")

            def mix(l):
                enter(dve, "dve", 3 * l + 1)
                for k in range(KY):
                    n = 2 * k
                    dve.wait_ge(S["pM"], l * 64 + n + 1)
                    wait(dve, gst[k % 2], l * 256 + 16 * (k // 2) if k >= 2 else 0)
                    nc.vector.tensor_copy(Gs[k % 2][0:64, 0:512], P[n % 4][0:64, :]).then_inc(S["eMd"], 1)
                leave(dve, "dve")

            def inv(l, first):
                enter(dve, "dve", 3 * l + 2)
                if first:
                    dve.wait_ge(S["pStat"], 1)
                    nc.vector.tensor_copy(wc6[:, :], P[7][0:6, 0:128])
                    dve.wait_ge(S["s_parload"], (l + 1) * 128)
                    nc.vector.tensor_tensor(bias0, P[6][:, 0:1], pwb_c, ALU.add).then_inc(S["eStat"], 1)

                def step(t, u, q):
                    a = At(t, u, q, 5)
                    if a.ok:
                        dve.wait_ge(S["pT3"], l * 64 + a.s + 1)
                        wait(dve, "pY", l * 128 + a.s * 2 - 2)
                        nc.vector.tensor_copy(AT[a.q % 2], P[2 + a.q % 2][:, :]).then_inc(S["eT3"], 1)
                    a = At(t, u, q, 0)
                    if a.ok:
                        dve.wait_ge(S["pI1"], l * 64 + a.s + 1)
                        nc.vector.tensor_copy(Ai[a.par].rearrange("p (y k) -> p k y", k=2 * KX)[:, 8 * a.q:8 * a.q + 8],
                                              P[a.q % 2][:, :].rearrange("p (k y) -> p k y", y=SIDE)).then_inc(S["eI1"], 1)
                    a = At(t, u, q, 6)
                    if a.ok:
                        for h in range(2):
                            dve.wait_ge(S["eY"], l * 128 + a.s * 2 + h + 1)
                            so = stats.rearrange("p (t c) -> p t c", c=96)[:, a.t, a.par * 48 + (a.q * 2 + h) * 6:a.par * 48 + (a.q * 2 + h) * 6 + 6]
                            nc.vector.bn_stats(so, ybuf[a.q % 2][:, h * 512:h * 512 + 512]).then_inc(S["eS"], 1)
                over_steps(dve, step)
                dve.wait_ge(S["eS"], (l + 1) * 128)
                link(nc.vector.bn_aggr(mv, stats))
                link(nc.vector.tensor_copy(st2[:, 0:1], mv[:, 0:1]))
                link(nc.vector.tensor_tensor(e2, mv[:, 0:1], mv[:, 0:1], ALU.mult))
                nc.vector.tensor_tensor(st2[:, 1:2], mv[:, 1:2], e2, ALU.add).then_inc(S["sAggr"], 1)
                dve.wait_ge(S["pStat"], l + 2)
                link(nc.vector.tensor_copy(tmp, P[0][:, 0:2]))
                link(nc.vector.tensor_tensor(e2, tmp[:, 0:1], tmp[:, 0:1], ALU.mult))
                nc.vector.tensor_tensor(e2, tmp[:, 1:2], e2, ALU.subtract).then_inc(S["sVar"], 1)
                dve.wait_ge(S["sRstd"], l + 1)
                link(nc.vector.reciprocal(rstd, std))
                link(nc.vector.tensor_tensor(bsc, rstd, gam_c, ALU.mult))
                link(nc.vector.tensor_tensor(e2, tmp[:, 0:1], bsc, ALU.mult))
                link(nc.vector.tensor_tensor(bbi, bet_c, e2, ALU.subtract))
                leave(dve, "dve")

            def fwd(l):
                enter(dve, "dve", 3 * l)

                def step(t, u, q):
                    a = At(t, u, q, 2)
                    if a.ok:
                        for h in range(2):
                            dve.wait_ge(S["pT1"], (l - 1) * 128 + a.s * 2 + h + 1)
                            if h == 0:
                                wait(dve, "pF1", (l - 1) * 64 + a.s - 1)
                            nc.vector.tensor_copy(hT[a.q % 2][:, h * 512:h * 512 + 512], P[h][:, :]).then_inc(S["eT1"], 1)
                    a = At(t, u, q, 7)
                    if a.ok:
                        dve.wait_ge(S["pT2"], (l - 1) * 64 + a.s + 1)
                        wait(dve, "pF2", (l - 1) * 64 + a.s)
                        nc.vector.tensor_copy(hT2[a.q % 2], P[2][:, :]).then_inc(S["eT2"], 1)
                over_steps(dve, step)
                leave(dve, "dve")
            mix(0)
            inv(0, True)
            for l in range(1, layers):
                fwd(l)
                mix(l)
                inv(l, False)
ROWS = 96
PER = TOK // ROWS
HEADS = 8
HP = HEADS // 2
THIRD = TOK // 3
NT = 376
EXPERTS, HID = 16, 128


def attention_constants():
    h, t = np.arange(96) // 48, np.arange(96) % 48
    mask = (t[:, None] == np.arange(PER)[None]) * 1.0
    spread = (h[:, None] == (np.arange(128) // 64)[None]) * 1.0
    order = np.tile(np.arange(EXPERTS, dtype=np.float64), (96, 1))
    ident = np.eye(128)[0:96]
    return np.concatenate([mask, spread, order, ident], axis=1).astype(np.float32)


NACONST = PER + 128 + EXPERTS + 128


def over_pairs_steps(eng, body):
    for u in range(2):
        for q in range(4):
            body(0, u, q)
    with eng.Fori(1, PAIRS // 2) as t:
        for u in range(2):
            for q in range(4):
                body(t, u, q)
    for u in range(2):
        for q in range(4):
            body(PAIRS // 2, u, q)


class At:
    def __init__(self, t, u, q, lag):
        d = q - lag
        back, self.q = -(d // 4), d % 4
        self.par = (u - back) % 2
        self.t = t + (u - back) // 2
        self.pair = self.t * 2 + self.par
        self.s = self.pair * 4 + self.q
        self.ok = not isinstance(self.pair, int) or 0 <= self.pair < PAIRS


def build_head(nc, bsc, bbi, z_d, H_d, txt, fc1, fc1b, fc2, fc2b):
    f32 = mybir.dt.float32
    ALU, ACT = mybir.AluOpType, mybir.ActivationFunctionType
    ctx = ExitStack()
    with ctx:
        sb = lambda name, shape: ctx.enter_context(nc.sbuf_tensor(name, shape, f32))
        sem = lambda name: ctx.enter_context(nc.semaphore(name))
        zbuf = sb("hz", [128, 2, 4096])
        g = sb("hg", [128, 2, 4, 512])
        f1 = sb("hf1", [128, 2, 128])
        fz = sb("hfz", [128, 63])
        bia = sb("hb", [128, 2])
        ob = sb("hob", [32, 512])
        P = [ctx.enter_context(nc.psum_tensor(f"HP{i}", [128, 512], f32)) for i in range(8)]
        zeroed, params, text = sem("h_zeroed"), sem("h_params"), sem("h_text")
        z_in = [[sem(f"h_z{u}{q}") for q in range(4)] for u in range(2)]
        h_ready, hid_done, g_ready, out_done, ob_ready, stored = (sem(n) for n in ("h_ready", "hid_done", "g_ready", "out_done", "ob_ready", "h_stored"))
        z_q = z_d.rearrange("(t u) p (q n) -> t u p q n", u=2, q=4)
        H_i = H_d.rearrange("(h t u) n -> h t u n", h=2, u=2)

        def wait(eng, s, v):
            if not isinstance(v, int) or v > 0:
                eng.wait_ge(s, v)
        block = ctx.enter_context(nc.Block())

        @block.sync
        def _(sp):
            sp.dma_start(H_d[:, PX:], txt).then_inc(text, 16)
            sp.dma_start(bia[:, 0:1], fc1b).then_inc(params, 16)
            sp.dma_start(bia[0:32, 1:2], fc2b.broadcast_to([32, 1])).then_inc(params, 16)
            sp.wait_ge(zeroed, 1)
            for h in range(2):
                sp.dma_start(f1[h * 64:h * 64 + 64, h, :], fc1).then_inc(params, 16)
            sp.dma_start(fz[:, 31:32], fc2).then_inc(params, 16)

            def step(t, u, q):
                a = At(t, u, q, 0)
                if a.ok:
                    if not isinstance(a.pair, int):
                        sp.wait_ge(hid_done, (a.s - 8) * 4 + 4)
                    sp.dma_start(zbuf[:, u, q * 1024:q * 1024 + 1024], z_q[a.t, u, :, q]).then_inc(z_in[u][q], 16)
                a = At(t, u, q, 3)
                if a.ok and a.par == 1 and a.q == 3:
                    sp.wait_ge(ob_ready, a.t + 1)
                    for h in range(2):
                        for v in range(2):
                            sp.dma_start(H_i[h, a.t, v, 0:PX].rearrange("(c n) -> c n", n=512), ob[h * 16 + v * 8:h * 16 + v * 8 + 8, :]).then_inc(stored, 16)
            over_pairs_steps(sp, step)
            sp.wait_ge(stored, 8 * 64)
            sp.wait_ge(text, 16)

        @block.gpsimd
        def _(pool):
            nc.gpsimd.memset(f1[:, :, :], 0.0)
            nc.gpsimd.memset(fz[:, :], 0.0).then_inc(zeroed, 1)

        @block.scalar
        def _(act):
            act.wait_ge(params, 80)

            def step(t, u, q):
                a = At(t, u, q, 0)
                if a.ok:
                    act.wait_ge(z_in[a.par][a.q], a.t * 16 + 16)
                    z = zbuf[:, a.par, a.q * 1024:a.q * 1024 + 1024]
                    nc.scalar.activation(z, z, ACT.Gelu, bias=bbi, scale=bsc).then_inc(h_ready, 1)
                a = At(t, u, q, 1)
                if a.ok:
                    wait(act, out_done, a.s - 1)
                    for k in range(4):
                        act.wait_ge(hid_done, a.s * 4 + k + 1)
                        nc.scalar.activation(g[:, a.q % 2, k, :], P[k][:, :], ACT.Gelu, bias=bia[:, 0:1]).then_inc(g_ready, 1)
            over_pairs_steps(act, step)

        @block.tensor
        def _(pe):
            pe.wait_ge(params, 80)

            def step(t, u, q):
                a = At(t, u, q, 1)
                if a.ok:
                    pe.wait_ge(h_ready, a.s + 1)
                    for k in range(4):
                        h, o = k // 2, a.q * 1024 + (k % 2) * 512
                        wait(pe, g_ready, a.s * 4 + k - 3)
                        nc.tensor.matmul(P[k][:, :], f1[:, h, :], zbuf[:, a.par, o:o + 512], start=True, stop=True).then_inc(hid_done, 1)
                a = At(t, u, q, 2)
                if a.ok:
                    if a.par == 0 and a.q == 0:
                        wait(pe, ob_ready, a.t)
                    for k in range(4):
                        j = (k // 2) * 16 + a.par * 8 + a.q * 2 + k % 2
                        pe.wait_ge(g_ready, a.s * 4 + k + 1)
                        last = nc.tensor.matmul(P[4][0:32, :], fz[:, 31 - j:63 - j], g[:, a.q % 2, k, :],
                                                start=a.par == 0 and a.q == 0 and k == 0, stop=a.par == 1 and a.q == 3 and k == 3)
                    last.then_inc(out_done, 1)
            over_pairs_steps(pe, step)

        @block.vector
        def _(dve):
            dve.wait_ge(params, 80)

            def body(t):
                dve.wait_ge(out_done, t * 8 + 8)
                wait(dve, stored, t * 64)
                nc.vector.tensor_scalar(ob[:, :], P[4][0:32, :], bia[0:32, 1:2], None, ALU.add).then_inc(ob_ready, 1)
            body(0)
            with dve.Fori(1, PAIRS // 2) as t:
                body(t)


def layernorm(nc, ALU, AX, link, dve, act_sqrt, H, xn, stat, n=PER):
    mean, var, rstd = stat[:, 0:n], stat[:, n:2 * n], stat[:, 2 * n:3 * n]
    Hv = H.rearrange("p (j d) -> p j d", d=D)
    first, second = xn[:, :, 0:D], xn[:, :, D:2 * D]

    def over_d(x):
        return x.rearrange("p (j o) -> p j o", o=1).broadcast_to([ROWS, n, D])
    link(nc.vector.tensor_reduce(mean, Hv, axis=AX.X, op=ALU.add))
    link(nc.vector.tensor_scalar(mean, mean, 1.0 / D, None, ALU.mult))
    link(nc.vector.tensor_tensor(first, Hv, over_d(mean), ALU.subtract))
    link(nc.vector.tensor_tensor(second, first, first, ALU.mult))
    link(nc.vector.tensor_reduce(var, second, axis=AX.X, op=ALU.add))
    act_sqrt(var, rstd)
    link(nc.vector.reciprocal(rstd, rstd))
    link(nc.vector.tensor_tensor(first, first, over_d(rstd), ALU.mult))
    return nc.vector.tensor_copy(second, first)


def build_attention(nc, H, H_d, wqkv, bqkv, w0, b0, aconst):
    f32, f32r = mybir.dt.float32, mybir.dt.float32r
    ALU, ACT, AX = mybir.AluOpType, mybir.ActivationFunctionType, mybir.AxisListType
    ctx = ExitStack()
    with ctx:
        sb = lambda name, shape, dt=f32: ctx.enter_context(nc.sbuf_tensor(name, shape, dt))
        sem = lambda name: ctx.enter_context(nc.semaphore(name))
        cst = sb("ac", [96, NACONST])
        mask, spread, ident = cst[:, 0:PER], cst[:, PER:PER + 128], cst[:, PER + 128 + EXPERTS:]
        xT = sb("axT", [128, TOK], f32r)
        whi, wlo = sb("awh", [128, 12, 128], f32r), sb("awl", [128, 12, 128], f32r)
        bias = sb("ab", [128, 24])
        VT = sb("aV", [128, HP, TOK])
        QT, KT = sb("aQ", [128, TOK]), sb("aK", [128, TOK])
        KZ = sb("aKZ", [128, ROWS, 2, 48])
        w0s, b0s = sb("aw0", [128, HP, D]), sb("ab0", [D, 1])
        E = sb("aE", [96, 2, 3 * SEQ])
        nmax, sums = sb("am", [96, ROWS]), sb("as", [96, ROWS])
        stat = sb("ast", [96, 3 * PER + 1])
        wraw = QT[:, 0:12 * 128].rearrange("p (c m) -> p c m", c=12)
        xn = VT[0:96, 0:2, :].rearrange("p a n -> p (a n)")[:, 0:PER * 128].rearrange("p (j d) -> p j d", d=128)
        Dg = KT[0:96, :].rearrange("p (b c) -> p b c", c=PER)
        oT = QT[0:D, :]
        P = [ctx.enter_context(nc.psum_tensor(f"AP{i}", [128, 512], f32)) for i in range(8)]
        S = {n: sem("at_" + n) for n in ("h", "par", "chain", "var", "rstd", "xn", "tr", "xT", "zero", "qkv", "evA", "evD", "kz", "sc", "max", "exp", "diag", "norm", "sp", "av", "o", "oA", "ot", "done", "whi", "wready")}
        block = ctx.enter_context(nc.Block())
        EV = HP * 36 // 2

        def groups(hp):
            for x in (1, 0, 2):
                for s in range(3):
                    for r in range(4):
                        yield x, s, r

        @block.sync
        def _(sp):
            sp.dma_start(H, H_d.rearrange("i n -> (i n)").rearrange("(p n) -> p n", p=ROWS)).then_inc(S["h"], 16)
            sp.dma_start(cst[:, :], aconst).then_inc(S["par"], 16)
            for h in range(2):
                sp.dma_start(wraw[h * 64:h * 64 + 64], wqkv).then_inc(S["par"], 16)
            sp.dma_start(bias[:, 0:12], bqkv).then_inc(S["par"], 16)
            sp.dma_start(w0s[:, :, :], w0).then_inc(S["par"], 16)
            sp.dma_start(b0s[:, :], b0).then_inc(S["par"], 16)

        @block.gpsimd
        def _(pool):
            nc.gpsimd.memset(KZ[:, :, :, :], 0.0).then_inc(S["zero"], 1)
            for hp in range(HP):
                pool.wait_ge(S["evA"], hp * 18 + 6)
                pool.wait_ge(S["evD"], hp * 18 + 6)
                if hp:
                    pool.wait_ge(S["sc"], hp * IMG)
                else:
                    pool.wait_ge(S["zero"], 1)
                for h in range(2):
                    o = slice(h * 64, h * 64 + 64)
                    nc.gpsimd.tensor_copy(KZ[o, :, h, 0:PER], KT[o, :].rearrange("p (b c) -> p b c", c=PER)).then_inc(S["kz"], 1)
                pool.wait_ge(S["kz"], hp * 2 + 2)
                for b in range(IMG):
                    pool.wait_ge(S["exp"], hp * ROWS + b * 3 + 3)
                    blocks = E[:, b % 2, :].rearrange("p (k n) -> p k n", k=3)
                    for k in range(3):
                        last = nc.gpsimd.tensor_tensor(Dg[:, b * 3 + k, :], blocks[:, k, k * PER:k * PER + PER], mask, ALU.mult)
                    last.then_inc(S["diag"], 1)

        @block.tensor
        def _(pe):
            pe.wait_ge(S["par"], 96)
            pe.wait_ge(S["xn"], 1)
            for j in range(PER):
                if j >= 8 and j % 4 == 0:
                    pe.wait_ge(S["xT"], j // 4 - 1)
                last = nc.tensor.matmul(P[(j // 4) % 2][:, (j % 4) * 96:(j % 4) * 96 + 96], xn[:, j, :], ident[:, 0:96], start=True, stop=True, is_transpose=True)
                if j % 4 == 3 or j == PER - 1:
                    last.then_inc(S["tr"], 1)
            pe.wait_ge(S["xT"], 12)
            pe.wait_ge(S["wready"], 1)
            n = 0
            for hp in range(HP):
                for x, s, r in groups(hp):
                    if n >= 2:
                        pe.wait_ge(S["evA" if n % 2 == 0 else "evD"], n // 2)
                    rows = xT[:, x * THIRD + r * NT:x * THIRD + r * NT + NT]
                    nc.tensor.matmul(P[n % 2][:, 0:NT], whi[:, s * HP + hp, :], rows, start=True, stop=False)
                    nc.tensor.matmul(P[n % 2][:, 0:NT], wlo[:, s * HP + hp, :], rows, start=False, stop=True).then_inc(S["qkv"], 1)
                    n += 1
                pe.wait_ge(S["kz"], hp * 2 + 2)
                pe.wait_ge(S["evA"], hp * 18 + 12)
                pe.wait_ge(S["evD"], hp * 18 + 12)
                for b in range(IMG):
                    m = hp * IMG + b
                    if m >= 4:
                        pe.wait_ge(S["exp"], (m - 4) * 3 + 3)
                    for k in range(3):
                        last = nc.tensor.matmul(P[2 + m % 4][0:96, k * SEQ:k * SEQ + SEQ], KZ[:, b * 3 + k, :, :].rearrange("p h c -> p (h c)"), QT[:, b * SEQ:b * SEQ + SEQ], start=True, stop=True)
                    last.then_inc(S["sc"], 1)
                for i in range(12):
                    m = hp * 12 + i
                    pe.wait_ge(S["norm"], m + 1)
                    if m >= 2:
                        pe.wait_ge(S["av"], m - 1)
                    nc.tensor.matmul(P[6 + m % 2][:, 0:NT], spread, Dg[:, i * 8:i * 8 + 8, :].rearrange("p b c -> p (b c)"), start=True, stop=True).then_inc(S["sp"], 1)
            for i in range(12):
                pe.wait_ge(S["av"], 36 + i + 1)
                if i >= 2:
                    pe.wait_ge(S["oA"], i - 1)
                for hp in range(HP):
                    last = nc.tensor.matmul(P[i % 2][0:D, 0:NT], w0s[:, hp, :], VT[:, hp, i * NT:i * NT + NT], start=hp == 0, stop=hp == HP - 1)
                last.then_inc(S["o"], 1)
            pe.wait_ge(S["oA"], 12)
            for g in range(6):
                if g >= 2:
                    pe.wait_ge(S["done"], g - 1)
                js = range(g * 8, min(g * 8 + 8, PER))
                for j in js:
                    last = nc.tensor.matmul(P[2 + g % 2][0:96, (j - g * 8) * D:(j - g * 8) * D + D], oT[:, j:j + 1 + PER * 95:PER], ident[0:D, 0:D], start=True, stop=True, is_transpose=True)
                last.then_inc(S["ot"], 1)

        @block.scalar
        def _(act):
            act.wait_ge(S["var"], 1)
            nc.scalar.activation(stat[:, 2 * PER:3 * PER], stat[:, PER:2 * PER], ACT.Sqrt, bias=stat[:, 3 * PER:3 * PER + 1], scale=1.0 / D).then_inc(S["rstd"], 1)
            act.wait_ge(S["wready"], 1)
            n = 0
            for hp in range(HP):
                for x, s, r in groups(hp):
                    if n % 2 == 0:
                        act.wait_ge(S["qkv"], n + 1)
                        if hp and n % 36 == 0:
                            act.wait_ge(S["sp"], hp * 12)
                        if x == 0 and s == 0 and r == 0 and hp:
                            act.wait_ge(S["sc"], hp * IMG)
                        dst = (QT[:, :], KT[:, :], VT[:, hp, :])[x].rearrange("p (r s) -> p s r", s=3)[:, s, r * NT:r * NT + NT]
                        c = s * HP + hp + (12 if x == 0 else 0)
                        nc.scalar.activation(dst, P[n % 2][:, 0:NT], ACT.Identity, bias=bias[:, c:c + 1], scale=0.125 if x == 0 else 1.0).then_inc(S["evA"], 1)
                    n += 1
                for b in range(IMG):
                    m = hp * IMG + b
                    act.wait_ge(S["max"], m + 1)
                    if m >= 2:
                        act.wait_ge(S["diag"], m - 1)
                    for k in range(3):
                        c = b * 3 + k
                        nc.scalar.activation(E[:, b % 2, k * SEQ:k * SEQ + SEQ], P[2 + m % 4][0:96, k * SEQ:k * SEQ + SEQ], ACT.Exp, bias=nmax[:, c:c + 1], accum_out=sums[:, c:c + 1]).then_inc(S["exp"], 1)
            for i in range(12):
                act.wait_ge(S["o"], i + 1)
                nc.scalar.activation(oT[:, i * NT:i * NT + NT], P[i % 2][0:D, 0:NT], ACT.Identity, bias=b0s[:, :]).then_inc(S["oA"], 1)

        @block.vector
        def _(dve):
            chained = [0]

            def link(ins):
                chained[0] += 1
                ins.then_inc(S["chain"], 1)
                dve.wait_ge(S["chain"], chained[0])
            dve.wait_ge(S["h"], 16)
            link(nc.vector.memset(stat[:, 3 * PER:], EPS))

            def act_sqrt(var, rstd):
                link(nc.vector.tensor_copy(var, var)) if False else None
                nc.vector.nop().then_inc(S["var"], 1)
                dve.wait_ge(S["rstd"], 1)
            layernorm(nc, ALU, AX, link, dve, act_sqrt, H, xn, stat).then_inc(S["xn"], 1)
            dve.wait_ge(S["par"], 96)
            link(nc.vector.tensor_copy(whi[:, :, :], wraw))
            link(nc.vector.tensor_scalar(bias[:, 12:24], bias[:, 0:12], 0.125, None, ALU.mult))
            link(nc.vector.tensor_tensor(wlo[:, :, :], wraw, whi[:, :, :], ALU.subtract))
            dve.wait_ge(S["chain"], chained[0])
            nc.vector.nop().then_inc(S["wready"], 1)
            xv = xT[:, :].rearrange("d (p j) -> d j p", j=PER)
            for g in range(12):
                dve.wait_ge(S["tr"], g + 1)
                k = min(4, PER - 4 * g)
                src = P[g % 2][:, 0:k * 96].rearrange("d (j p) -> d j p", p=96)
                link(nc.vector.tensor_copy(xv[:, 4 * g:4 * g + k], src))
                nc.vector.tensor_tensor(xv[64:128, 4 * g:4 * g + k], src[64:128], xv[64:128, 4 * g:4 * g + k], ALU.subtract).then_inc(S["xT"], 1)
            n = 0
            for hp in range(HP):
                for x, s, r in groups(hp):
                    if n % 2 == 1:
                        dve.wait_ge(S["qkv"], n + 1)
                        if hp and n % 36 == 1:
                            dve.wait_ge(S["sp"], hp * 12)
                        if x == 0 and s == 0 and r == 1 and hp:
                            dve.wait_ge(S["sc"], hp * IMG)
                        dst = (QT[:, :], KT[:, :], VT[:, hp, :])[x].rearrange("p (r s) -> p s r", s=3)[:, s, r * NT:r * NT + NT]
                        c = s * HP + hp
                        nc.vector.tensor_scalar(dst, P[n % 2][:, 0:NT], bias[:, c:c + 1], 0.125 if x == 0 else 1.0, ALU.add, ALU.mult).then_inc(S["evD"], 1)
                    n += 1
                for b in range(IMG):
                    m = hp * IMG + b
                    dve.wait_ge(S["sc"], m + 1)
                    nc.vector.tensor_reduce(nmax[:, b * 3:b * 3 + 3], P[2 + m % 4][0:96, 0:3 * SEQ].rearrange("p (k n) -> p k n", k=3), axis=AX.X, op=ALU.max, negate=True).then_inc(S["max"], 1)
                dve.wait_ge(S["exp"], (hp + 1) * ROWS)
                dve.wait_ge(S["evA"], (hp + 1) * 18)
                link(nc.vector.reciprocal(sums[:, :], sums[:, :]))
                for i in range(12):
                    m = hp * 12 + i
                    dve.wait_ge(S["diag"], hp * IMG + (i * 8 + 7) // 3 + 1)
                    dd = Dg[:, i * 8:i * 8 + 8, :]
                    nc.vector.tensor_tensor(dd, dd, sums[:, i * 8:i * 8 + 8].rearrange("p (b o) -> p b o", o=1).broadcast_to([96, 8, PER]), ALU.mult).then_inc(S["norm"], 1)
                for i in range(12):
                    m = hp * 12 + i
                    dve.wait_ge(S["sp"], m + 1)
                    v = VT[:, hp, i * NT:i * NT + NT]
                    nc.vector.tensor_tensor(v, P[6 + m % 2][:, 0:NT], v, ALU.mult).then_inc(S["av"], 1)
            for g in range(6):
                dve.wait_ge(S["ot"], g + 1)
                k = min(8, PER - g * 8)
                h = H[:, g * 512:g * 512 + k * D]
                nc.vector.tensor_tensor(h, P[2 + g % 2][0:96, 0:k * D], h, ALU.add).then_inc(S["done"], 1)


def build_moe(nc, H, out, dT_d, gate, gateb, w12, w3, aconst):
    f32, f32r = mybir.dt.float32, mybir.dt.float32r
    ALU, ACT, AX = mybir.AluOpType, mybir.ActivationFunctionType, mybir.AxisListType
    ctx = ExitStack()
    with ctx:
        sb = lambda name, shape, dt=f32: ctx.enter_context(nc.sbuf_tensor(name, shape, dt))
        sem = lambda name: ctx.enter_context(nc.semaphore(name))
        cst = sb("mc", [96, NACONST])
        order, ident = cst[:, PER + 128:PER + 128 + EXPERTS], cst[:, PER + 128 + EXPERTS:]
        xT = sb("mxT", [128, TOK], f32r)
        whi, wlo = sb("mwh", [128, EXPERTS, 2 * HID], f32r), sb("mwl", [128, EXPERTS, 2 * HID], f32r)
        ghi = sb("mg", [128, 2 * EXPERTS], f32r)
        w3s = sb("mw3", [128, EXPERTS, D])
        scr = sb("mscr", [128, 8 * PER * EXPERTS])
        xn = sb("mxn", [96, PER, 128])
        disp = sb("mdisp", [96, PER, EXPERTS])
        dTs = sb("mdT", [EXPERTS, TOK])
        oT = dTs
        acc = sb("macc", [D, TOK])
        dB = sb("mdB", [128, 2, EXPERTS // 4, NT])
        s1 = sb("ms1", [128, 2, NT])
        hid = sb("mhid", [128, 3, NT])
        stat = sb("mst", [96, 3 * PER + 1])
        small = sb("msm", [96, 4 * PER])
        gb = sb("mgb", [96, EXPERTS])
        wraw = scr[:, 0:EXPERTS * 2 * HID].rearrange("p (e m) -> p e m", e=EXPERTS)
        graw = scr[:, EXPERTS * 2 * HID:EXPERTS * 2 * HID + EXPERTS]
        P = [ctx.enter_context(nc.psum_tensor(f"MP{i}", [128, 512], f32)) for i in range(8)]
        S = {n: sem("m_" + n) for n in ("par", "chain", "var", "rstd", "xn", "tr", "xT", "w", "lg", "lgd", "rt", "dt", "dte", "dst", "h", "silu", "prod", "hid", "acc", "accd", "ot", "fin", "st")}
        dbs = [sem(f"m_db{u}") for u in range(2)]
        block = ctx.enter_context(nc.Block())
        STEPS = 12 * EXPERTS
        QE = EXPERTS // 4

        @block.sync
        def _(sp):
            sp.dma_start(cst[:, :], aconst).then_inc(S["par"], 16)
            for h in range(2):
                sp.dma_start(wraw[h * 64:h * 64 + 64], w12).then_inc(S["par"], 16)
                sp.dma_start(graw[h * 64:h * 64 + 64, :], gate).then_inc(S["par"], 16)
            sp.dma_start(w3s[:, :, :], w3).then_inc(S["par"], 16)
            sp.dma_start(gb[:, :], gateb.broadcast_to([96, EXPERTS])).then_inc(S["par"], 16)
            sp.wait_ge(S["dte"], 12)
            sp.dma_start(dT_d, dTs[:, :]).then_inc(S["dst"], 16)
            sp.wait_ge(S["dst"], 16)
            for n in range(12 * 4):
                t, c = n // 4, n % 4
                if n >= 2:
                    sp.wait_ge(S["hid"], (n - 2) * QE + QE)
                src = dT_d[c * QE:c * QE + QE, t * NT:t * NT + NT].rearrange("(o e) n -> o e n", o=1).broadcast_to([128, QE, NT])
                sp.dma_start(dB[:, n % 2], src).then_inc(dbs[n % 2], 16)
            for g in range(6):
                sp.wait_ge(S["fin"], g + 1)
                k = min(8, PER - g * 8)
                sp.dma_start(out.rearrange("i n -> (i n)").rearrange("(p n) -> p n", p=ROWS)[:, g * 512:g * 512 + k * D], H[:, g * 512:g * 512 + k * D]).then_inc(S["st"], 16)
            sp.wait_ge(S["st"], 96)

        @block.gpsimd
        def _(pool):
            for n in range(STEPS):
                q = n // QE
                pool.wait_ge(S["prod"], n + 1)
                if n % QE == 0:
                    pool.wait_ge(dbs[q % 2], (q // 2 + 1) * 16)
                nc.gpsimd.tensor_tensor(hid[:, n % 3, :], hid[:, n % 3, :], dB[:, q % 2, n % QE, :], ALU.mult).then_inc(S["hid"], 1)

        @block.tensor
        def _(pe):
            pe.wait_ge(S["par"], 112)
            pe.wait_ge(S["xn"], 1)
            for j in range(PER):
                if j >= 8 and j % 4 == 0:
                    pe.wait_ge(S["xT"], j // 4 - 1)
                last = nc.tensor.matmul(P[(j // 4) % 2][:, (j % 4) * 96:(j % 4) * 96 + 96], xn[:, j, :], ident[:, 0:96], start=True, stop=True, is_transpose=True)
                if j % 4 == 3 or j == PER - 1:
                    last.then_inc(S["tr"], 1)
            pe.wait_ge(S["xT"], 12)
            pe.wait_ge(S["w"], 1)
            for j in range(PER):
                last = nc.tensor.matmul(P[2 + j // 16][0:96, (j % 16) * 32:(j % 16) * 32 + 32], xT[:, j:j + 1 + PER * 95:PER], ghi[:, :], start=True, stop=True)
            last.then_inc(S["lg"], 1)
            pe.wait_ge(S["rt"], 1)
            for g in range(12):
                if g >= 2:
                    pe.wait_ge(S["dte"], g - 1)
                k = min(4, PER - 4 * g)
                for i in range(k):
                    last = nc.tensor.matmul(P[5 + g % 2][0:EXPERTS, i * 96:i * 96 + 96], disp[:, 4 * g + i, :], ident[:, 0:96], start=True, stop=True, is_transpose=True)
                last.then_inc(S["dt"], 1)
            for n in range(STEPS + 3):
                if n < STEPS:
                    t, e = n // EXPERTS, n % EXPERTS
                    x = xT[:, t * NT:t * NT + NT]
                    if n >= 2:
                        pe.wait_ge(S["prod"], n - 1)
                    for k in range(2):
                        o = slice(k * HID, k * HID + HID)
                        nc.tensor.matmul(P[2 * k + n % 2][:, 0:NT], whi[:, e, o], x, start=True, stop=False)
                        nc.tensor.matmul(P[2 * k + n % 2][:, 0:NT], wlo[:, e, o], x, start=False, stop=True).then_inc(S["h"], 1)
                m = n - 3
                if m >= 0:
                    t, e = m // EXPERTS, m % EXPERTS
                    pe.wait_ge(S["hid"], m + 1)
                    if e == 0 and t >= 2:
                        pe.wait_ge(S["accd"], t - 1)
                    last = nc.tensor.matmul(P[4 + t % 2][0:D, 0:NT], w3s[:, e, :], hid[:, m % 3, :], start=e == 0, stop=e == EXPERTS - 1)
                    last.then_inc(S["acc"], 1)
            pe.wait_ge(S["accd"], 12)
            for g in range(6):
                if g >= 2:
                    pe.wait_ge(S["fin"], g - 1)
                for j in range(g * 8, min(g * 8 + 8, PER)):
                    last = nc.tensor.matmul(P[6 + g % 2][0:96, (j - g * 8) * D:(j - g * 8) * D + D], acc[:, j:j + 1 + PER * 95:PER], ident[0:D, 0:D], start=True, stop=True, is_transpose=True)
                last.then_inc(S["ot"], 1)

        @block.scalar
        def _(act):
            act.wait_ge(S["var"], 1)
            nc.scalar.activation(stat[:, 2 * PER:3 * PER], stat[:, PER:2 * PER], ACT.Sqrt, bias=stat[:, 3 * PER:3 * PER + 1], scale=1.0 / D).then_inc(S["rstd"], 1)
            act.wait_ge(S["lgd"], 1)
            lg = scr[0:96, 0:PER * EXPERTS]
            nc.scalar.activation(lg, lg, ACT.Exp).then_inc(S["lgd"], 1)
            for n in range(STEPS):
                t, e = n // EXPERTS, n % EXPERTS
                act.wait_ge(S["h"], 2 * n + 1)
                if n >= 2:
                    act.wait_ge(S["prod"], n - 1)
                nc.scalar.activation(s1[:, n % 2, :], P[n % 2][:, 0:NT], ACT.Silu).then_inc(S["silu"], 1)
                if e == 2 and t >= 1:
                    pass
                if e == 6 and t >= 1:
                    act.wait_ge(S["acc"], t * EXPERTS)
                    nc.scalar.activation(acc[:, (t - 1) * NT:t * NT], P[4 + (t - 1) % 2][0:D, 0:NT], ACT.Copy).then_inc(S["accd"], 1)
            act.wait_ge(S["acc"], 12 * EXPERTS)
            nc.scalar.activation(acc[:, 11 * NT:12 * NT], P[5][0:D, 0:NT], ACT.Copy).then_inc(S["accd"], 1)

        @block.vector
        def _(dve):
            chained = [0]

            def link(ins):
                chained[0] += 1
                ins.then_inc(S["chain"], 1)
                dve.wait_ge(S["chain"], chained[0])
            link(nc.vector.memset(stat[:, 3 * PER:], EPS))

            def act_sqrt(var, rstd):
                nc.vector.nop().then_inc(S["var"], 1)
                dve.wait_ge(S["rstd"], 1)
            layernorm(nc, ALU, AX, link, dve, act_sqrt, H, xn[:, :, :], stat).then_inc(S["xn"], 1)
            dve.wait_ge(S["par"], 112)
            link(nc.vector.tensor_copy(whi[:, :, :], wraw))
            link(nc.vector.tensor_tensor(wlo[:, :, :], wraw, whi[:, :, :], ALU.subtract))
            link(nc.vector.tensor_copy(ghi[:, 0:EXPERTS], graw))
            link(nc.vector.tensor_tensor(ghi[:, EXPERTS:], graw, ghi[:, 0:EXPERTS], ALU.subtract))
            nc.vector.nop().then_inc(S["w"], 1)
            xv = xT[:, :].rearrange("d (p j) -> d j p", j=PER)
            for g in range(12):
                dve.wait_ge(S["tr"], g + 1)
                k = min(4, PER - 4 * g)
                src = P[g % 2][:, 0:k * 96].rearrange("d (j p) -> d j p", p=96)
                link(nc.vector.tensor_copy(xv[:, 4 * g:4 * g + k], src))
                nc.vector.tensor_tensor(xv[64:128, 4 * g:4 * g + k], src[64:128], xv[64:128, 4 * g:4 * g + k], ALU.subtract).then_inc(S["xT"], 1)
            n, E_ = PER * EXPERTS, EXPERTS
            arr = [scr[0:96, i * n:i * n + n].rearrange("p (j e) -> p j e", e=E_) for i in range(8)]
            lg, pr, hit, idx, one1, one2, rest, tmp = arr
            cols = [small[:, i * PER:i * PER + PER] for i in range(4)]

            def over_e(x):
                return x.rearrange("p (j o) -> p j o", o=1).broadcast_to([ROWS, PER, E_])

            def over_j(x):
                return x.rearrange("p (o e) -> p o e", o=1).broadcast_to([ROWS, PER, E_])
            dve.wait_ge(S["lg"], 1)
            for b in range(3):
                k = min(16, PER - 16 * b)
                src = P[2 + b][0:96, 0:k * 32].rearrange("p (j w e) -> p j w e", w=2, e=E_)
                link(nc.vector.tensor_copy(lg[:, 16 * b:16 * b + k], src[:, :, 1]))
                link(nc.vector.tensor_tensor(lg[:, 16 * b:16 * b + k], src[:, :, 0], lg[:, 16 * b:16 * b + k], ALU.add))
            link(nc.vector.tensor_tensor(lg, lg, over_j(gb[:, :]), ALU.add))
            link(nc.vector.tensor_reduce(cols[0], lg, axis=AX.X, op=ALU.max))
            nc.vector.tensor_tensor(lg, lg, over_e(cols[0]), ALU.subtract).then_inc(S["lgd"], 1)
            dve.wait_ge(S["lgd"], 2)
            link(nc.vector.tensor_reduce(cols[0], lg, axis=AX.X, op=ALU.add))
            link(nc.vector.reciprocal(cols[0], cols[0]))
            link(nc.vector.tensor_tensor(pr, lg, over_e(cols[0]), ALU.mult))
            link(nc.vector.tensor_copy(rest, pr))
            for top, one in ((cols[1], one1), (cols[2], one2)):
                link(nc.vector.tensor_reduce(top, rest, axis=AX.X, op=ALU.max))
                link(nc.vector.tensor_tensor(hit, rest, over_e(top), ALU.is_equal))
                link(nc.vector.tensor_scalar(idx, hit, -float(E_), float(E_), ALU.mult, ALU.add))
                link(nc.vector.tensor_tensor(idx, idx, over_j(order), ALU.add))
                link(nc.vector.tensor_reduce(cols[3], idx, axis=AX.X, op=ALU.min))
                link(nc.vector.tensor_tensor(one, idx, over_e(cols[3]), ALU.is_equal))
                link(nc.vector.tensor_scalar(tmp, one, -2.0, None, ALU.mult))
                link(nc.vector.tensor_tensor(rest, rest, tmp, ALU.add))
            link(nc.vector.tensor_tensor(cols[1], cols[1], cols[2], ALU.add))
            link(nc.vector.reciprocal(cols[1], cols[1]))
            link(nc.vector.tensor_tensor(one1, one1, one2, ALU.add))
            link(nc.vector.tensor_tensor(pr, pr, one1, ALU.mult))
            nc.vector.tensor_tensor(disp[:, :, :], pr, over_e(cols[1]), ALU.mult).then_inc(S["rt"], 1)
            dv = dTs[:, :].rearrange("e (p j) -> e j p", j=PER)
            for g in range(12):
                dve.wait_ge(S["dt"], g + 1)
                k = min(4, PER - 4 * g)
                nc.vector.tensor_copy(dv[:, 4 * g:4 * g + k], P[5 + g % 2][0:EXPERTS, 0:k * 96].rearrange("e (j p) -> e j p", p=96)).then_inc(S["dte"], 1)
            for m in range(STEPS):
                dve.wait_ge(S["h"], 2 * m + 2)
                dve.wait_ge(S["silu"], m + 1)
                if m >= 3:
                    dve.wait_ge(S["acc"], m - 2)
                nc.vector.tensor_tensor(hid[:, m % 3, :], P[2 + m % 2][:, 0:NT], s1[:, m % 2, :], ALU.mult).then_inc(S["prod"], 1)
            for g in range(6):
                dve.wait_ge(S["ot"], g + 1)
                k = min(8, PER - g * 8)
                h = H[:, g * 512:g * 512 + k * D]
                nc.vector.tensor_tensor(h, P[6 + g % 2][0:96, 0:k * D], h, ALU.add).then_inc(S["fin"], 1)


def build(nc, a, out):
    f32 = mybir.dt.float32
    z_d = nc.dram_tensor("z_d", (PAIRS, 128, PX), f32).ap()
    X_d = nc.dram_tensor("X_d", (3, CHUNKS, WIDTH, IMG, CM), f32).ap()
    G_d = nc.dram_tensor("G_d", (IMG, 2, KY, KX * WIDTH), f32).ap()
    H_d = nc.dram_tensor("H_d", (IMG, SEQ * D), f32).ap()
    dT_d = nc.dram_tensor("dT_d", (EXPERTS, TOK), f32).ap()
    with ExitStack() as ctx:
        small = ctx.enter_context(nc.sbuf_tensor("small", [128, 64], f32))
        build_fno(nc, small, a["x6"], a["fc0"], a["fc0T"], a["fc0b"], a["wmix"], a["pwT"], a["pwb"], a["gamma"], a["beta"], a["consts"], z_d, X_d, G_d)
        build_head(nc, small[:, 12:13], small[:, 13:14], z_d, H_d, a["txt"], a["fc1"], a["fc1b"], a["fc2"], a["fc2b"])
        H = ctx.enter_context(nc.sbuf_tensor("H", [ROWS, PER * D], f32))
        build_attention(nc, H[:, :], H_d, a["wqkv"], a["bqkv"], a["w0"], a["b0"], a["aconst"])
        build_moe(nc, H[:, :], out, dT_d, a["gate"], a["gateb"], a["w12"], a["w3"], a["aconst"])


def kernel(**inputs):
    import numpy as _np
    import concourse.bacc as _bacc
    from concourse import mybir as _mybir
    from concourse.bass_utils import run_bass_kernel_spmd as _run

    d = {k: _np.asarray(v) for k, v in inputs.items()}
    f = {k[3:]: v for k, v in d.items() if k.startswith("L0_")}
    wr = _np.stack([f["tok_w1r"], f["tok_w2r"]], axis=1)
    wi = _np.stack([f["tok_w1i"], f["tok_w2i"]], axis=1)
    wmix = _np.stack([wr, wi], axis=2).reshape(LAYERS, 2, 128, WIDTH, 2, CM).transpose(0, 1, 4, 2, 5, 3)
    wqkv = f["attn_Wqkv"].reshape(D, 3, D, HEADS).transpose(0, 1, 3, 2)
    bqkv = f["attn_bqkv"].reshape(3, D, HEADS).transpose(2, 1, 0).reshape(HP, 128, 3).transpose(1, 2, 0)
    host = {
        "x6": d["x"].reshape(2, PAIRS, PX, CH).transpose(1, 0, 3, 2).reshape(PAIRS, 2 * CH, PX),
        "txt": d["txt"].reshape(IMG, TXT * D),
        "fc0": f["tok_fc0_w"], "fc0T": f["tok_fc0_w"].T, "fc0b": f["tok_fc0_b"].reshape(WIDTH, 1),
        "wmix": wmix.reshape(LAYERS, CHUNKS, 128, CM * WIDTH),
        "pwT": f["tok_pw_w"].transpose(0, 2, 1),
        "pwb": f["tok_pw_b"].reshape(LAYERS, WIDTH, 1),
        "gamma": f["tok_gamma"].reshape(LAYERS, WIDTH, 1), "beta": f["tok_beta"].reshape(LAYERS, WIDTH, 1),
        "fc1": f["tok_fc1_w"], "fc1b": f["tok_fc1_b"].reshape(HIDDEN1, 1),
        "fc2": f["tok_fc2_w"], "fc2b": f["tok_fc2_b"].reshape(1, 1),
        "wqkv": wqkv.reshape(D, 12, 128), "bqkv": bqkv.reshape(128, 12),
        "w0": f["attn_W0"].reshape(D, HEADS, D).transpose(1, 0, 2).reshape(HP, 128, D).transpose(1, 0, 2),
        "b0": f["attn_b0"].reshape(D, 1),
        "gate": f["ffn_gate_w"], "gateb": f["ffn_gate_b"].reshape(1, EXPERTS),
        "w12": _np.concatenate([f["ffn_w1"], f["ffn_w2"]], axis=2).transpose(1, 0, 2),
        "w3": f["ffn_w3"].transpose(1, 0, 2),
        "consts": dft_constants(), "aconst": attention_constants(),
    }
    nc = _bacc.Bacc("TRN2", target_bir_lowering=False, num_devices=1)
    arrays, aps = {}, {}
    for name, value in host.items():
        value = _np.ascontiguousarray(value)
        arrays[f"in_{name}"] = value
        aps[name] = nc.dram_tensor(f"in_{name}", value.shape, _mybir.dt.from_np(value.dtype), kind="ExternalInput").ap()
    out = nc.dram_tensor("out_0", (IMG, SEQ * D), _mybir.dt.float32, kind="ExternalOutput").ap()
    build(nc, aps, out)
    r = _run(nc, [arrays], core_ids=[0])
    return r.results[0]["out_0"].reshape(IMG, SEQ, D)
```

```python
import numpy as np
import concourse.bass as bass
from concourse import mybir
from contextlib import ExitStack

IMG, SIDE, CH, WIDTH, LAYERS = 32, 64, 3, 64, 4
M1, M2 = 16, 16
PAIRS = IMG // 2
PX = SIDE * SIDE
KY, KX = 2 * M1, M2
MODES = KY * KX
CHUNKS = 4
CM = MODES // CHUNKS
WP = MODES // 16
HIDDEN1 = 128
TXT, D = 77, 64
SEQ = SIDE + TXT
TOK = IMG * SEQ
EPS = 1e-5


def dft_constants():
    w = 2 * np.pi / SIDE
    pos, kx = np.arange(SIDE), np.arange(KX)
    ky = np.concatenate([np.arange(M1), np.arange(SIDE - M1, SIDE)])
    ident = np.eye(128)
    f1 = np.zeros((2, SIDE, 2, KX, 2))
    for r in range(2):
        f1[r, :, r, :, 0] = np.cos(w * np.outer(pos, kx))
        f1[r, :, r, :, 1] = -np.sin(w * np.outer(pos, kx))
    f2 = np.zeros((2, SIDE, 2, KY))
    c, s = np.cos(w * np.outer(pos, ky)), np.sin(w * np.outer(pos, ky))
    f2[0, :, 0], f2[1, :, 0], f2[0, :, 1], f2[1, :, 1] = c, s, -s, c
    i1 = np.kron(np.eye(2), np.block([[c.T, s.T], [-s.T, c.T]]))
    i2 = np.zeros((4, KX, 2, 4, SIDE))
    g = np.where(kx == 0, 1.0, 2.0)[:, None] / PX
    for r in range(4):
        i2[r, :, 0, r] = g * np.cos(w * np.outer(kx, pos))
        i2[r, :, 1, r] = -g * np.sin(w * np.outer(kx, pos))
    avg = (np.arange(128)[:, None] % 64 == np.arange(128)[None] % 64) * 0.5
    none = np.zeros((128, 64))
    parts = [ident, f1.reshape(128, 64), none, f2.reshape(128, 64), none, i1, avg, i2.reshape(128, 256)]
    return np.concatenate(parts, axis=1).astype(np.float32)


NCONST = 128 + 128 + 128 + 256 + 128 + 256


def build_fno(nc, small, x6, fc0, fc0T, fc0b, wmix, pwT, pwb, gamma, beta, consts, z_d, X_d, G_d, layers=LAYERS):
    f32, f32r = mybir.dt.float32, mybir.dt.float32r
    ALU, ACT, AX = mybir.AluOpType, mybir.ActivationFunctionType, mybir.AxisListType
    ctx = ExitStack()
    with ctx:
        def sb(name, shape, dt=f32):
            return ctx.enter_context(nc.sbuf_tensor(name, shape, dt))

        def sem(name):
            return ctx.enter_context(nc.semaphore(name))

        with ExitStack() as under:
            zparts = under.enter_context(nc.sbuf_tensor("zparts", [128, 2, 2, 1024], f32r))
            ATr = under.enter_context(nc.sbuf_tensor("ATr", [128, 2, 2, 512], f32r))
        W = sb("W", [128, WP, 1024])
        work = sb("work", [128, 18432])
        i2h, i2l = sb("i2h", [128, 256], f32r), sb("i2l", [128, 256], f32r)
        pwh, pwl = sb("pwh", [128, 128], f32r), sb("pwl", [128, 128], f32r)
        cst = sb("cst", [128, NCONST - 256])
        wbd = sb("wbd", [128, 128])
        wc6 = sb("wc6", [96, 128])
        P = [ctx.enter_context(nc.psum_tensor(f"P{i}", [128, 512], f32)) for i in range(8)]
        ident, f1r, f2r = cst[:, 0:128], cst[:, 128:256], cst[:, 256:384]
        i1r, avg = cst[:, 384:640], cst[:, 640:768]

        def part(off, n):
            return work[:, off:off + n]
        zbuf = [part(0, 4096), part(4096, 4096)]
        hT = [part(8192, 1024), part(9216, 1024)]
        hT2 = [part(10240, 512), part(10752, 512)]
        A1 = [part(11264, 2048), part(13312, 2048)]
        Xs = [part(15360, 1536), part(16896, 1536)]
        XM = [part(0, 8192), part(8192, 8192)]
        Gs = [part(16384, 1024), part(17408, 1024)]
        Ai = [part(8192, 2048), part(10240, 2048)]
        Gt = [part(14336, 1024), part(15360, 1024)]
        ybuf = [part(16384, 1024), part(17408, 1024)]
        stats = W[:, WP - 1, 0:768]
        xall = work[0:96, 0:4096]
        sel0 = work[0:96, 4096:6144]
        Xx = work[0:96, 6144:7168]
        i2r = part(7168, 256)
        fc0Tbd = small[:, 16:22]
        fc0b_c, pwb_c, gam_c, bet_c = (small[:, i:i + 1] for i in range(4))
        bias0, mv, e2, st2 = small[:, 4:5], small[:, 6:8], small[:, 8:9], small[:, 10:12]
        bsc, bbi = small[:, 12:13], small[:, 13:14]
        rstd, std = small[:, 14:15], small[:, 15:16]
        fc0b4k = small[:, 24:25]
        tmp = small[:, 26:28]
        eps_c, minus = small[:, 28:29], small[:, 29:30]

        S = {n: sem(n) for n in (
            "s_const", "w_loaded", "z_zero", "sp_phase", "s_zero", "s_w0", "s_par", "s_parload",
            "a0_pe", "a0_ev", "a0_mx", "a0_re", "a0_im", "a0_dc", "a0_neg",
            "z_gelu", "pT1", "pF1", "pT2", "pF2", "eT1", "eF1", "eT2", "eF2",
            "pM", "eMd", "eMa",
            "pI1", "pT3", "pY", "eI1", "eT3", "eY", "eS", "z_gelu_c", "z_hi", "z_split", "eT3h", "pw_hi", "pw_split",
            "pe_phase", "act_phase", "dve_phase", "pool_phase", "chain", "pStat", "eStat", "sAggr", "sVar", "sRstd",
            "x0_load", "dbg")}
        zl = [[sem(f"zl{u}{q}") for q in range(4)] for u in range(2)]
        xl = [sem(f"xl{u}") for u in range(2)]
        gl = [sem(f"gl{u}") for u in range(2)]
        xst = [sem(f"xst{u}") for u in range(2)]
        gst = [sem(f"gst{u}") for u in range(2)]
        yst = [sem(f"yst{u}") for u in range(2)]

        z_q = z_d.rearrange("(t u) p (q n) -> t u p q n", u=2, q=4)
        x6_q = x6.rearrange("(t u) p (q n) -> t u p q n", u=2, q=4)
        X_s = X_d.rearrange("r k c (h t u) m -> t u h c (r k) m", h=2, u=2)
        G_s = G_d.rearrange("(h t u) r y (k v o) -> h t u (r y) k v o", h=2, u=2, v=2, o=WIDTH)
        W_t = W[:, :, :].rearrange("p (t w) n -> p t w n", w=4)
        G_w = G_d.rearrange("i r k n -> k r i n")

        def wait(eng, s, v):
            if not isinstance(v, int) or v > 0:
                eng.wait_ge(S[s] if isinstance(s, str) else s, v)

        class At:
            def __init__(self, t, u, q, lag):
                d = q - lag
                back, self.q = -(d // 4), d % 4
                self.par = (u - back) % 2
                self.t = t + (u - back) // 2
                self.pair = self.t * 2 + self.par
                self.s = self.pair * 4 + self.q
                self.ok = not isinstance(self.pair, int) or 0 <= self.pair < PAIRS

        def over_steps(eng, body, last=PAIRS // 2 + 1):
            for u in range(2):
                for q in range(4):
                    body(0, u, q)
            with eng.Fori(1, PAIRS // 2) as t:
                for u in range(2):
                    for q in range(4):
                        body(t, u, q)
            for u in range(2):
                for q in range(4):
                    body(PAIRS // 2, u, q)

        OTHERS = {"pe": "act dve pool sp", "act": "pe dve pool sp", "dve": "pe act pool sp", "pool": "pe act dve sp", "sp": "pe act dve pool"}

        def enter(eng, who, n):
            for o in OTHERS[who].split():
                eng.wait_ge(S[o + "_phase"], n)

        def leave(eng, who):
            eng.drain().then_inc(S[who + "_phase"], 1)

        def store_spectra(eng, t, u):
            for h in range(2):
                eng.dma_start(X_s[t, u, h], Xs[u][h * 64:h * 64 + 64, :].rearrange("p (k m) -> p k m", m=CM)).then_inc(xst[u], 16)

        block = ctx.enter_context(nc.Block())

        @block.sync
        def _(sp):
            sp.dma_start(cst[:, :], consts[:, 0:NCONST - 256]).then_inc(S["s_const"], 16)
            sp.dma_start(i2r, consts[:, NCONST - 256:]).then_inc(S["s_const"], 16)
            sp.dma_start(xall, x6.rearrange("b p n -> (b p) n")).then_inc(S["x0_load"], 16)
            sp.wait_ge(S["s_zero"], 2)
            for b in range(PAIRS):
                for h in range(2):
                    r = b * 6 + h * 3
                    sp.dma_start(sel0[r:r + 3, b * 128 + h * 64:b * 128 + h * 64 + 64], fc0).then_inc(S["s_w0"], 16)
            for h in range(2):
                o = slice(h * 64, h * 64 + 64)
                sp.dma_start(fc0Tbd[o, h * 3:h * 3 + 3], fc0T).then_inc(S["s_w0"], 16)
                sp.dma_start(fc0b_c[o, :], fc0b).then_inc(S["s_w0"], 16)
            sp.dma_start(W[:, :, :], wmix[0].rearrange("w p n -> p w n")).then_inc(S["w_loaded"], 16)

            for b in range(PAIRS):
                sp.wait_ge(S["a0_dc"], b + 1)
                sp.wait_ge(S["a0_neg"], b + 1)
                store_spectra(sp, b // 2, b % 2)
            for u in range(2):
                sp.wait_ge(xst[u], 8 * 32)
            leave(sp, "sp")

            def layer_parameters(l):
                for h in range(2):
                    o = slice(h * 64, h * 64 + 64)
                    sp.dma_start(wbd[o, o], pwT[l]).then_inc(S["s_parload"], 16)
                    for dst, src in ((pwb_c, pwb), (gam_c, gamma), (bet_c, beta)):
                        sp.dma_start(dst[o, :], src[l]).then_inc(S["s_parload"], 16)

            def mix_loads(l):
                enter(sp, "sp", 3 * l + 1)

                def xm(c):
                    if c >= 2:
                        sp.wait_ge(S["pM"], l * 64 + 16 * (c - 1))
                    for v, h, plane in ((0, 0, 0), (0, 1, 2), (1, 0, 1), (1, 1, 0)):
                        sp.dma_start(XM[c % 2][h * 64:h * 64 + 64, v * 4096:v * 4096 + 4096],
                                     X_d[plane, c].rearrange("c i m -> c (i m)")).then_inc(xl[c % 2], 16)
                layer_parameters(l)
                xm(0)
                xm(1)
                for k in range(KY):
                    sp.wait_ge(S["eMd"], l * 32 + k + 1)
                    sp.wait_ge(S["eMa"], l * 32 + k + 1)
                    sp.dma_start(G_w[k], Gs[k % 2][0:64, :]).then_inc(gst[k % 2], 16)
                    if k % 8 == 7 and k < 16:
                        xm(k // 8 + 2)
                for u in range(2):
                    sp.wait_ge(gst[u], (l + 1) * 16 * 16)
                leave(sp, "sp")

            def inv_loads(l, first):
                enter(sp, "sp", 3 * l + 2)
                if first:
                    sp.wait_ge(S["z_zero"], 1)

                def step(t, u, q):
                    a = At(t, u, q, 0)
                    inner = not isinstance(a.pair, int)
                    if q == 0 and a.ok:
                        if inner:
                            sp.wait_ge(S["pI1"], l * 64 + a.pair * 4 - 4)
                        for v in range(2):
                            for h in range(2):
                                dst = Gt[u][v * 64:v * 64 + 64, :].rearrange("p (k h o) -> p h k o", h=2, o=WIDTH)[:, h]
                                sp.dma_start(dst, G_s[h, a.t, u, :, :, v]).then_inc(gl[u], 16)
                    b = At(t, u, q, 8)
                    if b.ok:
                        sp.wait_ge(S["eY"], l * 128 + b.s * 2 + 2)
                        sp.dma_start(z_q[b.t, b.par, :, b.q], ybuf[b.q % 2]).then_inc(yst[b.q % 2], 16)
                    if not a.ok:
                        return
                    if inner:
                        sp.wait_ge(S["z_split"], l * 64 + a.s - 7)
                    o = slice(q * 1024, q * 1024 + 1024)
                    if first:
                        sp.dma_start(zbuf[u][0:6, o], x6_q[a.t, u, :, q]).then_inc(zl[u][q], 16)
                    else:
                        sp.dma_start(zbuf[u][:, o], z_q[a.t, u, :, q]).then_inc(zl[u][q], 16)
                over_steps(sp, step)
                for u in range(2):
                    sp.wait_ge(yst[u], (l + 1) * 32 * 16)
                leave(sp, "sp")

            def fwd_loads(l):
                enter(sp, "sp", 3 * l)

                def step(t, u, q):
                    a = At(t, u, q, 0)
                    if not a.ok:
                        return
                    if not isinstance(a.pair, int):
                        sp.wait_ge(S["pT1"], (l - 1) * 128 + a.s * 2 - 14)
                    o = slice(q * 1024, q * 1024 + 1024)
                    sp.dma_start(zbuf[u][:, o], z_q[a.t, u, :, q]).then_inc(zl[u][q], 16)
                    if q % 2 == 1:
                        w = u * 2 + q // 2
                        sp.dma_start(W_t[:, a.t, w], wmix[l].rearrange("(t w) p n -> p t w n", w=4)[:, a.t, w]).then_inc(S["w_loaded"], 16)
                over_steps(sp, step)
                for u in range(2):
                    sp.wait_ge(xst[u], (l + 1) * 8 * 32)
                leave(sp, "sp")
            mix_loads(0)
            inv_loads(0, True)
            for l in range(1, layers):
                fwd_loads(l)
                mix_loads(l)
                inv_loads(l, False)

        def z_loads_before(l, phase):
            return (l * 2 - 1 if phase == "A" else l * 2) * 8 * 16

        @block.gpsimd
        def _(pool):
            nc.gpsimd.memset(sel0, 0.0)
            nc.gpsimd.memset(small[:, :], 0.0)
            nc.gpsimd.memset(wc6[:, :], 0.0)
            nc.gpsimd.memset(wbd[:, :], 0.0).then_inc(S["s_zero"], 1)
            pool.wait_ge(S["s_zero"], 1)
            nc.gpsimd.memset(eps_c, EPS)
            nc.gpsimd.memset(minus, -1.0).then_inc(S["s_zero"], 1)
            pool.wait_ge(S["s_zero"], 2)

            def negate(negs, u):
                nc.gpsimd.tensor_tensor(Xs[u][:, 1024:1536], Xs[u][:, 512:1024], minus.broadcast_to([128, 512]), ALU.mult).then_inc(S[negs], 1)

            for b in range(PAIRS):
                pool.wait_ge(S["a0_im"], b + 1)
                if b >= 2:
                    pool.wait_ge(xst[b % 2], 32 * (b // 2))
                negate("a0_neg", b % 2)
            leave(pool, "pool")
            enter(pool, "pool", 1)
            leave(pool, "pool")

            def inv(l, rows):
                enter(pool, "pool", 3 * l + 2)

                def step(t, u, q):
                    a = At(t, u, q, 4)
                    if a.ok:
                        pool.wait_ge(S["z_hi"], l * 64 + a.s + 1)
                        nc.gpsimd.tensor_tensor(zparts[0:rows, a.q % 2, 1, :], zbuf[a.par][0:rows, a.q * 1024:a.q * 1024 + 1024],
                                                zparts[0:rows, a.q % 2, 0, :], ALU.subtract).then_inc(S["z_split"], 1)
                over_steps(pool, step)
                leave(pool, "pool")
            inv(0, 96)
            for l in range(1, layers):
                for n in range(3 * l, 3 * l + 2):
                    enter(pool, "pool", n)
                    leave(pool, "pool")
                inv(l, 128)

        @block.tensor
        def _(pe):
            nc.tensor.nop().then_inc(S["pF2"], 1)
            pe.wait_ge(S["s_const"], 32)
            pe.wait_ge(S["x0_load"], 16)

            def tr(out, in_):
                n = in_.shape[0]
                return nc.tensor.matmul(out, in_, ident[0:n, 0:n], start=True, stop=True, is_transpose=True)

            n = 0
            for g in range(4):
                for h in range(2):
                    for i in range(4):
                        last = tr(P[h][:, i * 128:i * 128 + 96], xall[:, g * 1024 + h * 512 + i * 128:g * 1024 + h * 512 + i * 128 + 128])
                    last.then_inc(S["a0_pe"], 1)
                    n += 1
                    pe.wait_ge(S["a0_ev"], n)
                for i in range(8):
                    last = nc.tensor.matmul(P[3][0:96, i * 64:i * 64 + 64], hT[0][:, i * 128:i * 128 + 96], f1r[:, 0:64], start=True, stop=True)
                last.then_inc(S["a0_pe"], 1)
                n += 1
                pe.wait_ge(S["a0_ev"], n)
            for g in range(4):
                for i in range(4):
                    last = tr(P[0][:, i * 128:i * 128 + 96], A1[0][0:96, (4 * g + i) * 128:(4 * g + i) * 128 + 128])
                last.then_inc(S["a0_pe"], 1)
                n += 1
                pe.wait_ge(S["a0_ev"], n)
                for i in range(4):
                    last = nc.tensor.matmul(P[1][0:96, i * 64:i * 64 + 64], hT2[0][:, i * 128:i * 128 + 96], f2r[:, 0:64], start=True, stop=True)
                last.then_inc(S["a0_pe"], 1)
                n += 1
                pe.wait_ge(S["a0_ev"], n)
            pe.wait_ge(S["s_w0"], 36 * 16)
            for b in range(PAIRS):
                if b >= 2:
                    pe.wait_ge(S["a0_re"], b - 1)
                    pe.wait_ge(S["a0_im"], b - 1)
                for r in range(2):
                    last = nc.tensor.matmul(P[2 * (b % 2) + r][:, :], sel0[:, b * 128:b * 128 + 128], Xx[:, r * 512:r * 512 + 512], start=True, stop=True)
                last.then_inc(S["a0_mx"], 1)
            leave(pe, "pe")

            def mix(l):
                enter(pe, "pe", 3 * l + 1)
                for n in range(64):
                    c, g = n // 16, n % 16
                    if n == 0:
                        pe.wait_ge(S["w_loaded"], 16 + l * WP * 16)
                    if g == 0:
                        pe.wait_ge(xl[c % 2], (l * 2 + c // 2 + 1) * 64)
                    if n >= 4:
                        pe.wait_ge(S["eMd" if n % 2 == 0 else "eMa"], l * 32 + (n - 4) // 2 + 1)
                    xm = XM[c % 2].rearrange("p (i m) -> p i m", m=CM)
                    for i in range(8):
                        m = g * 8 + i
                        last = nc.tensor.matmul(P[n % 4][0:64, i * 64:i * 64 + 64], xm[:, :, m], W[:, (c * CM + m) // 16, (m % 16) * 64:(m % 16) * 64 + 64], start=True, stop=True)
                    last.then_inc(S["pM"], 1)
                leave(pe, "pe")

            def inv(l, first):
                enter(pe, "pe", 3 * l + 2)
                pe.wait_ge(S["s_parload"], (l + 1) * 128)
                if first:
                    nc.tensor.matmul(P[7][0:6, 0:128], fc0Tbd, wbd[:, :], start=True, stop=True)
                    nc.tensor.matmul(P[6][:, 0:1], wbd[:, :], fc0b_c, start=True, stop=True).then_inc(S["pStat"], 1)
                    pe.wait_ge(S["eStat"], 1)
                pe.wait_ge(S["pw_split"], l + 1)
                rows = 96 if first else 128

                def step(t, u, q):
                    a = At(t, u, q, 5)
                    if a.ok:
                        wait(pe, "eI1", l * 64 + a.pair * 4 + 4)
                        wait(pe, "eT3", l * 64 + a.s - 1 if not first or not isinstance(a.s, int) else a.s - 1)
                        for i in range(4):
                            j = 4 * a.q + i
                            last = tr(P[2 + a.q % 2][:, i * 128:i * 128 + 128], Ai[a.par][:, j * 128:j * 128 + 128])
                        last.then_inc(S["pT3"], 1)
                    a = At(t, u, q, 0)
                    if a.ok:
                        wait(pe, gl[a.par], l * 512 + a.t * 64 + 64)
                        wait(pe, "eI1", l * 64 + a.s - 1)
                        for i in range(2):
                            m = 2 * a.q + i
                            last = nc.tensor.matmul(P[a.q % 2][:, i * 256:i * 256 + 256], Gt[a.par][:, m * 128:m * 128 + 128], i1r, start=True, stop=True)
                        last.then_inc(S["pI1"], 1)
                    a = At(t, u, q, 6)
                    if a.ok:
                        pe.wait_ge(S["z_split"], l * 64 + a.s + 1)
                        pe.wait_ge(S["eT3"], l * 64 + a.s + 1)
                        for h in range(2):
                            bank = P[4 + 2 * (a.q % 2) + h]
                            wait(pe, "eY", l * 128 + a.s * 2 + h - 3)
                            zh, zlow = (zparts[0:rows, a.q % 2, part, h * 512:h * 512 + 512] for part in range(2))
                            nc.tensor.matmul(bank[:, :], pwh[0:rows, :], zh, start=True, stop=False)
                            nc.tensor.matmul(bank[:, :], pwl[0:rows, :], zh, start=False, stop=False)
                            nc.tensor.matmul(bank[:, :], pwh[0:rows, :], zlow, start=False, stop=False)
                            for i in range(2):
                                half = bank[:, i * 256:i * 256 + 256]
                                ath, atl = (ATr[:, a.q % 2, part, (2 * h + i) * 128:(2 * h + i) * 128 + 128] for part in range(2))
                                nc.tensor.matmul(half, ath, i2h[:, :], start=False, stop=False)
                                nc.tensor.matmul(half, ath, i2l[:, :], start=False, stop=False)
                                last = nc.tensor.matmul(half, atl, i2h[:, :], start=False, stop=i == 1)
                            last.then_inc(S["pY"], 1)
                over_steps(pe, step)
                pe.wait_ge(S["sAggr"], l + 1)
                nc.tensor.matmul(P[0][:, 0:2], avg, st2, start=True, stop=True).then_inc(S["pStat"], 1)
                leave(pe, "pe")

            def fwd(l):
                enter(pe, "pe", 3 * l)

                def step(t, u, q):
                    a = At(t, u, q, 2)
                    if a.ok:
                        wait(pe, "z_gelu", (l - 1) * 64 + a.s + 1)
                        for h in range(2):
                            wait(pe, "eT1", (l - 1) * 128 + a.s * 2 + h - 1)
                            for i in range(4):
                                o = a.q * 1024 + h * 512 + i * 128
                                last = tr(P[h][:, i * 128:i * 128 + 128], zbuf[a.par][:, o:o + 128])
                            last.then_inc(S["pT1"], 1)
                    a = At(t, u, q, 8)
                    if a.ok:
                        wait(pe, "eT2", (l - 1) * 64 + a.s + 1)
                        if a.q % 2 == 0:
                            wait(pe, "eF2", (l - 1) * 32 + a.pair * 2 + a.q // 2 + 1)
                        for i in range(4):
                            m = (a.q % 2) * 4 + i
                            n = 128 if m < 7 else 64
                            last = nc.tensor.matmul(P[5 + a.q // 2][:, m * 64:m * 64 + n], hT2[a.q % 2][:, i * 128:i * 128 + 128], f2r[:, 0:n], start=True, stop=True)
                        last.then_inc(S["pF2"], 1)
                    a = At(t, u, q, 7)
                    if a.ok:
                        wait(pe, "eF1", (l - 1) * 64 + a.pair * 4 + 4)
                        wait(pe, "eT2", (l - 1) * 64 + a.s)
                        for i in range(4):
                            last = tr(P[2][:, i * 128:i * 128 + 128], A1[a.par][:, (4 * a.q + i) * 128:(4 * a.q + i) * 128 + 128])
                        last.then_inc(S["pT2"], 1)
                    a = At(t, u, q, 3)
                    if a.ok:
                        wait(pe, "eT1", (l - 1) * 128 + a.s * 2 + 2)
                        wait(pe, "eF1", (l - 1) * 64 + a.s - 1)
                        for i in range(8):
                            n = 128 if i < 7 else 64
                            last = nc.tensor.matmul(P[3 + a.q % 2][:, i * 64:i * 64 + n], hT[a.q % 2][:, i * 128:i * 128 + 128], f1r[:, 0:n], start=True, stop=True)
                        last.then_inc(S["pF1"], 1)
                over_steps(pe, step)
                leave(pe, "pe")
            mix(0)
            inv(0, True)
            for l in range(1, layers):
                fwd(l)
                mix(l)
                inv(l, False)

        @block.scalar
        def _(act):
            act.wait_ge(S["s_w0"], 36 * 16)
            for b in range(PAIRS):
                act.wait_ge(S["a0_mx"], b + 1)
                if b >= 2:
                    act.wait_ge(xst[b % 2], 32 * (b // 2))
                nc.scalar.activation(Xs[b % 2][:, 0:512], P[2 * (b % 2)][:, :], ACT.Copy).then_inc(S["a0_re"], 1)
            leave(act, "act")

            def mix(l):
                enter(act, "act", 3 * l + 1)
                for k in range(KY):
                    n = 2 * k + 1
                    act.wait_ge(S["pM"], l * 64 + n + 1)
                    v = l * 256 + 16 * (k // 2)
                    wait(act, gst[k % 2], v if k >= 2 else 0)
                    nc.scalar.activation(Gs[k % 2][0:64, 512:1024], P[n % 4][0:64, :], ACT.Copy).then_inc(S["eMa"], 1)
                leave(act, "act")

            def inv(l, first):
                enter(act, "act", 3 * l + 2)

                def step(t, u, q):
                    c = At(t, u, q, 4)
                    z = zbuf[c.par][0:rows, c.q * 1024:c.q * 1024 + 1024]
                    if c.ok and not first:
                        wait(act, zl[c.par][c.q], z_loads_before(l, "C") + c.t * 16 + 16)
                        nc.scalar.activation(z, z, ACT.Gelu, bias=bbi, scale=bsc).then_inc(S["z_gelu_c"], 1)
                    a = At(t, u, q, 6)
                    if a.ok:
                        for h in range(2):
                            act.wait_ge(S["pY"], l * 128 + a.s * 2 + h + 1)
                            if h == 0:
                                wait(act, yst[a.q % 2], stores_waited(l, a))
                                wait(act, "eS", l * 128 + a.s * 2 - 2)
                            nc.scalar.activation(ybuf[a.q % 2][:, h * 512:h * 512 + 512], P[4 + 2 * (a.q % 2) + h][:, :], ACT.Identity, bias=bias0 if first else pwb_c).then_inc(S["eY"], 1)
                    if c.ok:
                        if first:
                            act.wait_ge(zl[c.par][c.q], c.t * 16 + 16)
                        else:
                            act.wait_ge(S["z_gelu_c"], (l - 1) * 64 + c.s + 1)
                        wait(act, "pY", l * 128 + c.s * 2 - 2)
                        nc.scalar.activation(zparts[0:rows, c.q % 2, 0, :], z, ACT.Copy).then_inc(S["z_hi"], 1)
                if first:
                    act.wait_ge(S["eStat"], 1)
                    act.wait_ge(S["z_zero"], 1)
                rows = 96 if first else 128
                act.wait_ge(S["s_parload"], (l + 1) * 128)
                over_steps(act, step)
                act.wait_ge(S["sVar"], l + 1)
                nc.scalar.activation(std, e2, ACT.Sqrt, bias=eps_c).then_inc(S["sRstd"], 1)
                leave(act, "act")

            def stores_waited(l, a):
                return l * 32 * 16 + (a.pair * 2 + a.q // 2) * 16 if not isinstance(a.pair, int) or a.s >= 2 else 0

            def fwd(l):
                enter(act, "act", 3 * l)

                def step(t, u, q):
                    a = At(t, u, q, 0)
                    if a.ok:
                        wait(act, zl[a.par][a.q], z_loads_before(l, "A") + a.t * 16 + 16)
                        o = slice(a.q * 1024, a.q * 1024 + 1024)
                        nc.scalar.activation(zbuf[a.par][:, o], zbuf[a.par][:, o], ACT.Gelu, bias=bbi, scale=bsc).then_inc(S["z_gelu"], 1)
                    a = At(t, u, q, 3)
                    if a.ok:
                        act.wait_ge(S["pF1"], (l - 1) * 64 + a.s + 1)
                        nc.scalar.activation(A1[a.par].rearrange("p (k y) -> p y k", y=SIDE)[:, 16 * a.q:16 * a.q + 16],
                                             P[3 + a.q % 2][:, :].rearrange("p (y k) -> p y k", k=2 * KX), ACT.Copy).then_inc(S["eF1"], 1)
                    a = At(t, u, q, 8)
                    if a.ok and a.q % 2 == 1:
                        g = a.q // 2
                        act.wait_ge(S["pF2"], (l - 1) * 64 + a.s + 2)
                        if g == 0 and (not isinstance(a.pair, int) or a.pair >= 2):
                            wait(act, xst[a.par], l * 256 + a.t * 32)
                        out = Xs[a.par][:, 0:1024].rearrange("p (r y k) -> p k r y", r=2, k=KX)[:, 8 * g:8 * g + 8]
                        nc.scalar.activation(out, P[5 + g][:, :].rearrange("p (k r y) -> p k r y", k=8, r=2), ACT.Copy)
                        out = Xs[a.par][:, 1024:1536].rearrange("p (y k) -> p k y", k=KX)[:, 8 * g:8 * g + 8]
                        nc.scalar.activation(out, P[5 + g][:, :].rearrange("p (k r y) -> p k r y", k=8, r=2)[:, :, 1], ACT.Copy, scale=-1.0).then_inc(S["eF2"], 1)
                        if g == 1:
                            act.wait_ge(S["eF2"], (l - 1) * 32 + a.pair * 2 + 4)
                            store_spectra(act, a.t, a.par)
                over_steps(act, step)
                leave(act, "act")
            mix(0)
            inv(0, True)
            for l in range(1, layers):
                fwd(l)
                mix(l)
                inv(l, False)

        @block.vector
        def _(dve):
            chained = [0]

            def link(ins):
                chained[0] += 1
                ins.then_inc(S["chain"], 1)
                dve.wait_ge(S["chain"], chained[0])
            dve.wait_ge(S["s_const"], 32)
            link(nc.vector.tensor_copy(i2h[:, :], i2r))
            link(nc.vector.tensor_tensor(i2l[:, :], i2r, i2h[:, :], ALU.subtract))
            nc.vector.nop().then_inc(S["eF2"], 2)
            n = 0
            for g in range(4):
                for h in range(2):
                    n += 1
                    dve.wait_ge(S["a0_pe"], n)
                    nc.vector.tensor_copy(hT[0][:, h * 512:h * 512 + 512].rearrange("p (i c) -> p i c", c=128)[:, :, 0:96],
                                          P[h][:, :].rearrange("p (i c) -> p i c", c=128)[:, :, 0:96]).then_inc(S["a0_ev"], 1)
                n += 1
                dve.wait_ge(S["a0_pe"], n)
                nc.vector.tensor_copy(A1[0][0:96, :].rearrange("p (k y) -> p y k", y=SIDE)[:, 16 * g:16 * g + 16],
                                      P[3][0:96, :].rearrange("p (y k) -> p y k", k=2 * KX)).then_inc(S["a0_ev"], 1)
            for g in range(4):
                n += 1
                dve.wait_ge(S["a0_pe"], n)
                nc.vector.tensor_copy(hT2[0][:, 0:512].rearrange("p (i c) -> p i c", c=128)[:, :, 0:96],
                                      P[0][:, :].rearrange("p (i c) -> p i c", c=128)[:, :, 0:96]).then_inc(S["a0_ev"], 1)
                n += 1
                dve.wait_ge(S["a0_pe"], n)
                nc.vector.tensor_copy(Xx.rearrange("p (r y k) -> p k r y", r=2, k=KX)[:, 4 * g:4 * g + 4],
                                      P[1][0:96, 0:256].rearrange("p (k r y) -> p k r y", k=4, r=2)).then_inc(S["a0_ev"], 1)
            dve.wait_ge(S["s_w0"], 36 * 16)
            link(nc.vector.tensor_scalar(fc0b4k, fc0b_c, float(PX), None, ALU.mult))
            for b in range(PAIRS):
                dve.wait_ge(S["a0_mx"], b + 1)
                if b >= 2:
                    dve.wait_ge(xst[b % 2], 32 * (b // 2))
                nc.vector.tensor_copy(Xs[b % 2][:, 512:1024], P[2 * (b % 2) + 1][:, :]).then_inc(S["a0_im"], 1)
                dve.wait_ge(S["a0_re"], b + 1)
                nc.vector.tensor_tensor(Xs[b % 2][:, 0:1], Xs[b % 2][:, 0:1], fc0b4k, ALU.add).then_inc(S["a0_dc"], 1)
            leave(dve, "dve")

            def mix(l):
                enter(dve, "dve", 3 * l + 1)
                for k in range(KY):
                    n = 2 * k
                    dve.wait_ge(S["pM"], l * 64 + n + 1)
                    wait(dve, gst[k % 2], l * 256 + 16 * (k // 2) if k >= 2 else 0)
                    nc.vector.tensor_copy(Gs[k % 2][0:64, 0:512], P[n % 4][0:64, :]).then_inc(S["eMd"], 1)
                leave(dve, "dve")

            def inv(l, first):
                enter(dve, "dve", 3 * l + 2)
                if first:
                    dve.wait_ge(S["pStat"], 1)
                    nc.vector.memset(work[0:96, 0:8192], 0.0).then_inc(S["z_zero"], 1)
                    dve.wait_ge(S["s_zero"], 2)
                    link(nc.vector.tensor_copy(wc6[0:6, :], P[7][0:6, 0:128]))
                dve.wait_ge(S["s_parload"], (l + 1) * 128)
                if first:
                    nc.vector.tensor_tensor(bias0, P[6][:, 0:1], pwb_c, ALU.add).then_inc(S["eStat"], 1)
                rows, pw = (96, wc6[:, :]) if first else (128, wbd[:, :])
                nc.vector.tensor_copy(pwh[0:rows, :], pw).then_inc(S["pw_hi"], 1)
                dve.wait_ge(S["pw_hi"], l + 1)
                nc.vector.tensor_tensor(pwl[0:rows, :], pw, pwh[0:rows, :], ALU.subtract).then_inc(S["pw_split"], 1)

                def step(t, u, q):
                    a = At(t, u, q, 5)
                    if a.ok:
                        dve.wait_ge(S["pT3"], l * 64 + a.s + 1)
                        wait(dve, "pY", l * 128 + a.s * 2 - 2)
                        ath, atl = ATr[:, a.q % 2, 0, :], ATr[:, a.q % 2, 1, :]
                        nc.vector.tensor_copy(ath, P[2 + a.q % 2][:, :]).then_inc(S["eT3h"], 1)
                        dve.wait_ge(S["eT3h"], l * 64 + a.s + 1)
                        nc.vector.tensor_tensor(atl, P[2 + a.q % 2][:, :], ath, ALU.subtract).then_inc(S["eT3"], 1)
                    a = At(t, u, q, 0)
                    if a.ok:
                        dve.wait_ge(S["pI1"], l * 64 + a.s + 1)
                        nc.vector.tensor_copy(Ai[a.par].rearrange("p (y k) -> p k y", k=2 * KX)[:, 8 * a.q:8 * a.q + 8],
                                              P[a.q % 2][:, :].rearrange("p (k y) -> p k y", y=SIDE)).then_inc(S["eI1"], 1)
                    a = At(t, u, q, 6)
                    if a.ok:
                        for h in range(2):
                            dve.wait_ge(S["eY"], l * 128 + a.s * 2 + h + 1)
                            so = stats.rearrange("p (t c) -> p t c", c=96)[:, a.t, a.par * 48 + (a.q * 2 + h) * 6:a.par * 48 + (a.q * 2 + h) * 6 + 6]
                            nc.vector.bn_stats(so, ybuf[a.q % 2][:, h * 512:h * 512 + 512]).then_inc(S["eS"], 1)
                over_steps(dve, step)
                dve.wait_ge(S["eS"], (l + 1) * 128)
                link(nc.vector.bn_aggr(mv, stats))
                link(nc.vector.tensor_copy(st2[:, 0:1], mv[:, 0:1]))
                link(nc.vector.tensor_tensor(e2, mv[:, 0:1], mv[:, 0:1], ALU.mult))
                nc.vector.tensor_tensor(st2[:, 1:2], mv[:, 1:2], e2, ALU.add).then_inc(S["sAggr"], 1)
                dve.wait_ge(S["pStat"], l + 2)
                link(nc.vector.tensor_copy(tmp, P[0][:, 0:2]))
                link(nc.vector.tensor_tensor(e2, tmp[:, 0:1], tmp[:, 0:1], ALU.mult))
                nc.vector.tensor_tensor(e2, tmp[:, 1:2], e2, ALU.subtract).then_inc(S["sVar"], 1)
                dve.wait_ge(S["sRstd"], l + 1)
                link(nc.vector.reciprocal(rstd, std))
                link(nc.vector.tensor_tensor(bsc, rstd, gam_c, ALU.mult))
                link(nc.vector.tensor_tensor(e2, tmp[:, 0:1], bsc, ALU.mult))
                link(nc.vector.tensor_tensor(bbi, bet_c, e2, ALU.subtract))
                leave(dve, "dve")

            def fwd(l):
                enter(dve, "dve", 3 * l)

                def step(t, u, q):
                    a = At(t, u, q, 2)
                    if a.ok:
                        for h in range(2):
                            dve.wait_ge(S["pT1"], (l - 1) * 128 + a.s * 2 + h + 1)
                            if h == 0:
                                wait(dve, "pF1", (l - 1) * 64 + a.s - 1)
                            nc.vector.tensor_copy(hT[a.q % 2][:, h * 512:h * 512 + 512], P[h][:, :]).then_inc(S["eT1"], 1)
                    a = At(t, u, q, 7)
                    if a.ok:
                        dve.wait_ge(S["pT2"], (l - 1) * 64 + a.s + 1)
                        wait(dve, "pF2", (l - 1) * 64 + a.s)
                        nc.vector.tensor_copy(hT2[a.q % 2], P[2][:, :]).then_inc(S["eT2"], 1)
                over_steps(dve, step)
                leave(dve, "dve")
            mix(0)
            inv(0, True)
            for l in range(1, layers):
                fwd(l)
                mix(l)
                inv(l, False)
ROWS = 96
PER = TOK // ROWS
HEADS = 8
HP = HEADS // 2
THIRD = TOK // 3
NT = 376
EXPERTS, HID = 16, 128


def attention_constants():
    h, t = np.arange(96) // 48, np.arange(96) % 48
    mask = (t[:, None] == np.arange(PER)[None]) * 1.0
    spread = (h[:, None] == (np.arange(128) // 64)[None]) * 1.0
    order = np.tile(np.arange(EXPERTS, dtype=np.float64), (96, 1))
    ident = np.eye(128)[0:96]
    return np.concatenate([mask, spread, order, ident], axis=1).astype(np.float32)


NACONST = PER + 128 + EXPERTS + 128


def over_pairs_steps(eng, body):
    for u in range(2):
        for q in range(4):
            body(0, u, q)
    with eng.Fori(1, PAIRS // 2) as t:
        for u in range(2):
            for q in range(4):
                body(t, u, q)
    for u in range(2):
        for q in range(4):
            body(PAIRS // 2, u, q)


class At:
    def __init__(self, t, u, q, lag):
        d = q - lag
        back, self.q = -(d // 4), d % 4
        self.par = (u - back) % 2
        self.t = t + (u - back) // 2
        self.pair = self.t * 2 + self.par
        self.s = self.pair * 4 + self.q
        self.ok = not isinstance(self.pair, int) or 0 <= self.pair < PAIRS


def build_head(nc, bsc, bbi, z_d, H_d, txt, fc1, fc1b, fc2, fc2b):
    f32, f32r = mybir.dt.float32, mybir.dt.float32r
    ALU, ACT = mybir.AluOpType, mybir.ActivationFunctionType
    ctx = ExitStack()
    with ctx:
        sb = lambda name, shape, dt=f32: ctx.enter_context(nc.sbuf_tensor(name, shape, dt))
        sem = lambda name: ctx.enter_context(nc.semaphore(name))
        zbuf = sb("hz", [128, 2, 4096])
        zhi, zlo = sb("hzh", [128, 2, 1024], f32r), sb("hzl", [128, 2, 1024], f32r)
        g = sb("hg", [128, 2, 4, 512])
        ghi, glo = sb("hgh", [128, 2, 4, 512], f32r), sb("hgl", [128, 2, 4, 512], f32r)
        f1 = sb("hf1", [128, 2, 128])
        f1hi, f1lo = sb("hf1h", [128, 2, 128], f32r), sb("hf1l", [128, 2, 128], f32r)
        fz = sb("hfz", [128, 127])
        fzr = sb("hfzr", [128, 127], f32r)
        bia = sb("hb", [128, 2])
        one = sb("h1", [128, 1])
        ob, ob2 = sb("hob", [32, 512]), sb("hob2", [32, 512])
        P = [ctx.enter_context(nc.psum_tensor(f"HP{i}", [128, 512], f32)) for i in range(8)]
        zeroed, params, text, parts, chain = sem("h_zeroed"), sem("h_params"), sem("h_text"), sem("h_parts"), sem("h_chain")
        z_in = [[sem(f"h_z{u}{q}") for q in range(4)] for u in range(2)]
        h_ready, z_hi, z_split, hid_done, g_ready, g_hi, g_split, out_done, ob_ready, stored = (
            sem("h_" + n) for n in ("ready", "zhi", "zsplit", "hid_done", "g_ready", "ghi", "gsplit", "out_done", "ob_ready", "stored"))
        half_sum = sem("h_half")
        z_q = z_d.rearrange("(t u) p (q n) -> t u p q n", u=2, q=4)
        H_i = H_d.rearrange("(h t u) n -> h t u n", h=2, u=2)

        def wait(eng, s, v):
            if not isinstance(v, int) or v > 0:
                eng.wait_ge(s, v)
        block = ctx.enter_context(nc.Block())

        @block.sync
        def _(sp):
            sp.dma_start(H_d[:, PX:], txt).then_inc(text, 16)
            sp.dma_start(bia[:, 0:1], fc1b).then_inc(params, 16)
            sp.dma_start(bia[0:32, 1:2], fc2b.broadcast_to([32, 1])).then_inc(params, 16)
            sp.wait_ge(zeroed, 1)
            for h in range(2):
                sp.dma_start(f1[h * 64:h * 64 + 64, h, :], fc1).then_inc(params, 16)
            sp.dma_start(fz[:, 63:64], fc2).then_inc(params, 16)

            def step(t, u, q):
                a = At(t, u, q, 0)
                if a.ok:
                    if not isinstance(a.pair, int):
                        sp.wait_ge(z_split, a.s - 7)
                    sp.dma_start(zbuf[:, u, q * 1024:q * 1024 + 1024], z_q[a.t, u, :, q]).then_inc(z_in[u][q], 16)
                a = At(t, u, q, 8)
                if a.ok and a.par == 1 and a.q == 3:
                    sp.wait_ge(ob_ready, a.t + 1)
                    for h in range(2):
                        for v in range(2):
                            sp.dma_start(H_i[h, a.t, v, 0:PX].rearrange("(c n) -> c n", n=512), ob[h * 16 + v * 8:h * 16 + v * 8 + 8, :]).then_inc(stored, 16)
            over_pairs_steps(sp, step)
            sp.wait_ge(stored, 8 * 64)
            sp.wait_ge(text, 16)

        @block.gpsimd
        def _(pool):
            nc.gpsimd.memset(f1[:, :, :], 0.0)
            nc.gpsimd.memset(one[:, :], 1.0)
            nc.gpsimd.memset(fz[:, :], 0.0).then_inc(zeroed, 1)
            pool.wait_ge(zeroed, 1)

            def step(t, u, q):
                a = At(t, u, q, 0)
                if a.ok:
                    wait(pool, hid_done, a.s * 4 - 4)
                    pool.wait_ge(h_ready, a.s + 1)
                    z = zbuf[:, a.par, a.q * 1024:a.q * 1024 + 1024]
                    nc.gpsimd.tensor_tensor(zhi[:, a.q % 2, :], z, one[:, :].broadcast_to([128, 1024]), ALU.mult).then_inc(z_hi, 1)
                    pool.wait_ge(z_hi, a.s + 1)
                    nc.gpsimd.tensor_tensor(zlo[:, a.q % 2, :], z, zhi[:, a.q % 2, :], ALU.subtract).then_inc(z_split, 1)
            over_pairs_steps(pool, step)

        @block.scalar
        def _(act):
            act.wait_ge(params, 80)

            def step(t, u, q):
                a = At(t, u, q, 0)
                if a.ok:
                    act.wait_ge(z_in[a.par][a.q], a.t * 16 + 16)
                    z = zbuf[:, a.par, a.q * 1024:a.q * 1024 + 1024]
                    nc.scalar.activation(z, z, ACT.Gelu, bias=bbi, scale=bsc).then_inc(h_ready, 1)
                a = At(t, u, q, 1)
                if a.ok:
                    wait(act, g_split, a.s * 4 - 4)
                    for k in range(4):
                        act.wait_ge(hid_done, a.s * 4 + k + 1)
                        nc.scalar.activation(g[:, a.q % 2, k, :], P[k][:, :], ACT.Gelu, bias=bia[:, 0:1]).then_inc(g_ready, 1)
            over_pairs_steps(act, step)

        @block.tensor
        def _(pe):
            pe.wait_ge(parts, 1)

            def step(t, u, q):
                a = At(t, u, q, 1)
                if a.ok:
                    pe.wait_ge(z_split, a.s + 1)
                    for k in range(4):
                        h, o = k // 2, (k % 2) * 512
                        hi, lo = zhi[:, a.q % 2, o:o + 512], zlo[:, a.q % 2, o:o + 512]
                        wait(pe, g_ready, a.s * 4 + k - 3)
                        nc.tensor.matmul(P[k][:, :], f1hi[:, h, :], hi, start=True, stop=False)
                        nc.tensor.matmul(P[k][:, :], f1lo[:, h, :], hi, start=False, stop=False)
                        nc.tensor.matmul(P[k][:, :], f1hi[:, h, :], lo, start=False, stop=True).then_inc(hid_done, 1)
                a = At(t, u, q, 3)
                if a.ok:
                    if a.par == 0 and a.q == 0:
                        wait(pe, ob_ready, a.t)
                    for k in range(4):
                        j = (k // 2) * 16 + a.par * 8 + a.q * 2 + k % 2
                        pe.wait_ge(g_split, a.s * 4 + k + 1)
                        nc.tensor.matmul(P[4][0:64, :], fzr[:, 63 - j:127 - j], ghi[:, a.q % 2, k, :],
                                         start=a.par == 0 and a.q == 0 and k == 0, stop=False)
                        last = nc.tensor.matmul(P[4][0:64, :], fzr[:, 63 - j:127 - j], glo[:, a.q % 2, k, :],
                                                start=False, stop=a.par == 1 and a.q == 3 and k == 3)
                    last.then_inc(out_done, 1)
            over_pairs_steps(pe, step)

        @block.vector
        def _(dve):
            chained = [0]

            def link(ins):
                chained[0] += 1
                ins.then_inc(chain, 1)
                dve.wait_ge(chain, chained[0])
            dve.wait_ge(params, 80)
            link(nc.vector.tensor_copy(f1hi[:, :, :], f1[:, :, :]))
            link(nc.vector.tensor_tensor(f1lo[:, :, :], f1[:, :, :], f1hi[:, :, :], ALU.subtract))
            link(nc.vector.tensor_copy(fzr[:, :], fz[:, :]))
            nc.vector.tensor_tensor(fzr[:, 95:96], fz[:, 63:64], fzr[:, 63:64], ALU.subtract).then_inc(parts, 1)

            def step(t, u, q):
                a = At(t, u, q, 1)
                if a.ok:
                    for k in range(4):
                        dve.wait_ge(g_ready, a.s * 4 + k + 1)
                        if k == 0:
                            wait(dve, out_done, a.s - 1)
                        nc.vector.tensor_copy(ghi[:, a.q % 2, k, :], g[:, a.q % 2, k, :]).then_inc(g_hi, 1)
                        dve.wait_ge(g_hi, a.s * 4 + k + 1)
                        nc.vector.tensor_tensor(glo[:, a.q % 2, k, :], g[:, a.q % 2, k, :], ghi[:, a.q % 2, k, :], ALU.subtract).then_inc(g_split, 1)
                a = At(t, u, q, 3)
                if a.ok and a.par == 1 and a.q == 3:
                    dve.wait_ge(out_done, a.t * 8 + 8)
                    wait(dve, stored, a.t * 64)
                    nc.vector.tensor_scalar(ob2[:, :], P[4][32:64, :], bia[0:32, 1:2], None, ALU.add).then_inc(half_sum, 1)
                    dve.wait_ge(half_sum, a.t + 1)
                    nc.vector.tensor_tensor(ob[:, :], P[4][0:32, :], ob2[:, :], ALU.add).then_inc(ob_ready, 1)
            over_pairs_steps(dve, step)


def layernorm(nc, ALU, AX, link, dve, act_sqrt, H, xn, stat, n=PER):
    mean, var, rstd = stat[:, 0:n], stat[:, n:2 * n], stat[:, 2 * n:3 * n]
    Hv = H.rearrange("p (j d) -> p j d", d=D)
    first, second = xn[:, :, 0:D], xn[:, :, D:2 * D]

    def over_d(x):
        return x.rearrange("p (j o) -> p j o", o=1).broadcast_to([ROWS, n, D])
    link(nc.vector.tensor_reduce(mean, Hv, axis=AX.X, op=ALU.add))
    link(nc.vector.tensor_scalar(mean, mean, 1.0 / D, None, ALU.mult))
    link(nc.vector.tensor_tensor(first, Hv, over_d(mean), ALU.subtract))
    link(nc.vector.tensor_tensor(second, first, first, ALU.mult))
    link(nc.vector.tensor_reduce(var, second, axis=AX.X, op=ALU.add))
    act_sqrt(var, rstd)
    link(nc.vector.reciprocal(rstd, rstd))
    link(nc.vector.tensor_tensor(first, first, over_d(rstd), ALU.mult))
    return nc.vector.tensor_copy(second, first)


def build_attention(nc, H, H_d, wqkv, bqkv, w0, b0, aconst):
    f32, f32r = mybir.dt.float32, mybir.dt.float32r
    ALU, ACT, AX = mybir.AluOpType, mybir.ActivationFunctionType, mybir.AxisListType
    ctx = ExitStack()
    with ctx:
        sb = lambda name, shape, dt=f32: ctx.enter_context(nc.sbuf_tensor(name, shape, dt))
        sem = lambda name: ctx.enter_context(nc.semaphore(name))
        cst = sb("ac", [96, NACONST])
        mask, spread, ident = cst[:, 0:PER], cst[:, PER:PER + 128], cst[:, PER + 128 + EXPERTS:]
        xT = sb("axT", [128, TOK], f32r)
        whi, wlo = sb("awh", [128, 12, 128], f32r), sb("awl", [128, 12, 128], f32r)
        bias = sb("ab", [128, 24])
        VT = sb("aV", [128, HP, TOK])
        QT, KT = sb("aQ", [128, TOK]), sb("aK", [128, TOK])
        KZ = sb("aKZ", [128, ROWS, 2, 48])
        w0s, b0s = sb("aw0", [128, HP, D]), sb("ab0", [D, 1])
        E = sb("aE", [96, 2, 3 * SEQ])
        nmax, sums = sb("am", [96, ROWS]), sb("as", [96, ROWS])
        stat = sb("ast", [96, 3 * PER + 1])
        wraw = QT[:, 0:12 * 128].rearrange("p (c m) -> p c m", c=12)
        xn = VT[0:96, 0:2, :].rearrange("p a n -> p (a n)")[:, 0:PER * 128].rearrange("p (j d) -> p j d", d=128)
        Dg = KT[0:96, :].rearrange("p (b c) -> p b c", c=PER)
        oT = QT[0:D, :]
        P = [ctx.enter_context(nc.psum_tensor(f"AP{i}", [128, 512], f32)) for i in range(8)]
        S = {n: sem("at_" + n) for n in ("h", "par", "chain", "var", "rstd", "xn", "tr", "xT", "zero", "qkv", "evA", "evD", "kz", "sc", "max", "exp", "diag", "norm", "sp", "av", "o", "oA", "ot", "done", "whi", "wready")}
        block = ctx.enter_context(nc.Block())
        EV = HP * 36 // 2

        def groups(hp):
            for x in (1, 0, 2):
                for s in range(3):
                    for r in range(4):
                        yield x, s, r

        @block.sync
        def _(sp):
            sp.dma_start(H, H_d.rearrange("i n -> (i n)").rearrange("(p n) -> p n", p=ROWS)).then_inc(S["h"], 16)
            sp.dma_start(cst[:, :], aconst).then_inc(S["par"], 16)
            for h in range(2):
                sp.dma_start(wraw[h * 64:h * 64 + 64], wqkv).then_inc(S["par"], 16)
            sp.dma_start(bias[:, 0:12], bqkv).then_inc(S["par"], 16)
            sp.dma_start(w0s[:, :, :], w0).then_inc(S["par"], 16)
            sp.dma_start(b0s[:, :], b0).then_inc(S["par"], 16)

        @block.gpsimd
        def _(pool):
            nc.gpsimd.memset(KZ[:, :, :, :], 0.0).then_inc(S["zero"], 1)
            for hp in range(HP):
                pool.wait_ge(S["evA"], hp * 18 + 6)
                pool.wait_ge(S["evD"], hp * 18 + 6)
                if hp:
                    pool.wait_ge(S["sc"], hp * IMG)
                else:
                    pool.wait_ge(S["zero"], 1)
                for h in range(2):
                    o = slice(h * 64, h * 64 + 64)
                    nc.gpsimd.tensor_copy(KZ[o, :, h, 0:PER], KT[o, :].rearrange("p (b c) -> p b c", c=PER)).then_inc(S["kz"], 1)
                pool.wait_ge(S["kz"], hp * 2 + 2)
                for b in range(IMG):
                    pool.wait_ge(S["exp"], hp * ROWS + b * 3 + 3)
                    blocks = E[:, b % 2, :].rearrange("p (k n) -> p k n", k=3)
                    for k in range(3):
                        last = nc.gpsimd.tensor_tensor(Dg[:, b * 3 + k, :], blocks[:, k, k * PER:k * PER + PER], mask, ALU.mult)
                    last.then_inc(S["diag"], 1)

        @block.tensor
        def _(pe):
            pe.wait_ge(S["par"], 96)
            pe.wait_ge(S["xn"], 1)
            for j in range(PER):
                if j >= 8 and j % 4 == 0:
                    pe.wait_ge(S["xT"], j // 4 - 1)
                last = nc.tensor.matmul(P[(j // 4) % 2][:, (j % 4) * 96:(j % 4) * 96 + 96], xn[:, j, :], ident[:, 0:96], start=True, stop=True, is_transpose=True)
                if j % 4 == 3 or j == PER - 1:
                    last.then_inc(S["tr"], 1)
            pe.wait_ge(S["xT"], 12)
            pe.wait_ge(S["wready"], 1)
            n = 0
            for hp in range(HP):
                for x, s, r in groups(hp):
                    if n >= 2:
                        pe.wait_ge(S["evA" if n % 2 == 0 else "evD"], n // 2)
                    rows = xT[:, x * THIRD + r * NT:x * THIRD + r * NT + NT]
                    nc.tensor.matmul(P[n % 2][:, 0:NT], whi[:, s * HP + hp, :], rows, start=True, stop=False)
                    nc.tensor.matmul(P[n % 2][:, 0:NT], wlo[:, s * HP + hp, :], rows, start=False, stop=True).then_inc(S["qkv"], 1)
                    n += 1
                pe.wait_ge(S["kz"], hp * 2 + 2)
                pe.wait_ge(S["evA"], hp * 18 + 12)
                pe.wait_ge(S["evD"], hp * 18 + 12)
                for b in range(IMG):
                    m = hp * IMG + b
                    if m >= 4:
                        pe.wait_ge(S["exp"], (m - 4) * 3 + 3)
                    for k in range(3):
                        last = nc.tensor.matmul(P[2 + m % 4][0:96, k * SEQ:k * SEQ + SEQ], KZ[:, b * 3 + k, :, :].rearrange("p h c -> p (h c)"), QT[:, b * SEQ:b * SEQ + SEQ], start=True, stop=True)
                    last.then_inc(S["sc"], 1)
                for i in range(12):
                    m = hp * 12 + i
                    pe.wait_ge(S["norm"], m + 1)
                    if m >= 2:
                        pe.wait_ge(S["av"], m - 1)
                    nc.tensor.matmul(P[6 + m % 2][:, 0:NT], spread, Dg[:, i * 8:i * 8 + 8, :].rearrange("p b c -> p (b c)"), start=True, stop=True).then_inc(S["sp"], 1)
            for i in range(12):
                pe.wait_ge(S["av"], 36 + i + 1)
                if i >= 2:
                    pe.wait_ge(S["oA"], i - 1)
                for hp in range(HP):
                    last = nc.tensor.matmul(P[i % 2][0:D, 0:NT], w0s[:, hp, :], VT[:, hp, i * NT:i * NT + NT], start=hp == 0, stop=hp == HP - 1)
                last.then_inc(S["o"], 1)
            pe.wait_ge(S["oA"], 12)
            for g in range(6):
                if g >= 2:
                    pe.wait_ge(S["done"], g - 1)
                js = range(g * 8, min(g * 8 + 8, PER))
                for j in js:
                    last = nc.tensor.matmul(P[2 + g % 2][0:96, (j - g * 8) * D:(j - g * 8) * D + D], oT[:, j:j + 1 + PER * 95:PER], ident[0:D, 0:D], start=True, stop=True, is_transpose=True)
                last.then_inc(S["ot"], 1)

        @block.scalar
        def _(act):
            act.wait_ge(S["var"], 1)
            nc.scalar.activation(stat[:, 2 * PER:3 * PER], stat[:, PER:2 * PER], ACT.Sqrt, bias=stat[:, 3 * PER:3 * PER + 1], scale=1.0 / D).then_inc(S["rstd"], 1)
            act.wait_ge(S["wready"], 1)
            n = 0
            for hp in range(HP):
                for x, s, r in groups(hp):
                    if n % 2 == 0:
                        act.wait_ge(S["qkv"], n + 1)
                        if hp and n % 36 == 0:
                            act.wait_ge(S["sp"], hp * 12)
                        if x == 0 and s == 0 and r == 0 and hp:
                            act.wait_ge(S["sc"], hp * IMG)
                        dst = (QT[:, :], KT[:, :], VT[:, hp, :])[x].rearrange("p (r s) -> p s r", s=3)[:, s, r * NT:r * NT + NT]
                        c = s * HP + hp + (12 if x == 0 else 0)
                        nc.scalar.activation(dst, P[n % 2][:, 0:NT], ACT.Identity, bias=bias[:, c:c + 1], scale=0.125 if x == 0 else 1.0).then_inc(S["evA"], 1)
                    n += 1
                for b in range(IMG):
                    m = hp * IMG + b
                    act.wait_ge(S["max"], m + 1)
                    if m >= 2:
                        act.wait_ge(S["diag"], m - 1)
                    for k in range(3):
                        c = b * 3 + k
                        nc.scalar.activation(E[:, b % 2, k * SEQ:k * SEQ + SEQ], P[2 + m % 4][0:96, k * SEQ:k * SEQ + SEQ], ACT.Exp, bias=nmax[:, c:c + 1], accum_out=sums[:, c:c + 1]).then_inc(S["exp"], 1)
            for i in range(12):
                act.wait_ge(S["o"], i + 1)
                nc.scalar.activation(oT[:, i * NT:i * NT + NT], P[i % 2][0:D, 0:NT], ACT.Identity, bias=b0s[:, :]).then_inc(S["oA"], 1)

        @block.vector
        def _(dve):
            chained = [0]

            def link(ins):
                chained[0] += 1
                ins.then_inc(S["chain"], 1)
                dve.wait_ge(S["chain"], chained[0])
            dve.wait_ge(S["h"], 16)
            link(nc.vector.memset(stat[:, 3 * PER:], EPS))

            def act_sqrt(var, rstd):
                link(nc.vector.tensor_copy(var, var)) if False else None
                nc.vector.nop().then_inc(S["var"], 1)
                dve.wait_ge(S["rstd"], 1)
            layernorm(nc, ALU, AX, link, dve, act_sqrt, H, xn, stat).then_inc(S["xn"], 1)
            dve.wait_ge(S["par"], 96)
            link(nc.vector.tensor_copy(whi[:, :, :], wraw))
            link(nc.vector.tensor_scalar(bias[:, 12:24], bias[:, 0:12], 0.125, None, ALU.mult))
            link(nc.vector.tensor_tensor(wlo[:, :, :], wraw, whi[:, :, :], ALU.subtract))
            dve.wait_ge(S["chain"], chained[0])
            nc.vector.nop().then_inc(S["wready"], 1)
            xv = xT[:, :].rearrange("d (p j) -> d j p", j=PER)
            for g in range(12):
                dve.wait_ge(S["tr"], g + 1)
                k = min(4, PER - 4 * g)
                src = P[g % 2][:, 0:k * 96].rearrange("d (j p) -> d j p", p=96)
                link(nc.vector.tensor_copy(xv[:, 4 * g:4 * g + k], src))
                nc.vector.tensor_tensor(xv[64:128, 4 * g:4 * g + k], src[64:128], xv[64:128, 4 * g:4 * g + k], ALU.subtract).then_inc(S["xT"], 1)
            n = 0
            for hp in range(HP):
                for x, s, r in groups(hp):
                    if n % 2 == 1:
                        dve.wait_ge(S["qkv"], n + 1)
                        if hp and n % 36 == 1:
                            dve.wait_ge(S["sp"], hp * 12)
                        if x == 0 and s == 0 and r == 1 and hp:
                            dve.wait_ge(S["sc"], hp * IMG)
                        dst = (QT[:, :], KT[:, :], VT[:, hp, :])[x].rearrange("p (r s) -> p s r", s=3)[:, s, r * NT:r * NT + NT]
                        c = s * HP + hp
                        nc.vector.tensor_scalar(dst, P[n % 2][:, 0:NT], bias[:, c:c + 1], 0.125 if x == 0 else 1.0, ALU.add, ALU.mult).then_inc(S["evD"], 1)
                    n += 1
                for b in range(IMG):
                    m = hp * IMG + b
                    dve.wait_ge(S["sc"], m + 1)
                    nc.vector.tensor_reduce(nmax[:, b * 3:b * 3 + 3], P[2 + m % 4][0:96, 0:3 * SEQ].rearrange("p (k n) -> p k n", k=3), axis=AX.X, op=ALU.max, negate=True).then_inc(S["max"], 1)
                dve.wait_ge(S["exp"], (hp + 1) * ROWS)
                dve.wait_ge(S["evA"], (hp + 1) * 18)
                link(nc.vector.reciprocal(sums[:, :], sums[:, :]))
                for i in range(12):
                    m = hp * 12 + i
                    dve.wait_ge(S["diag"], hp * IMG + (i * 8 + 7) // 3 + 1)
                    dd = Dg[:, i * 8:i * 8 + 8, :]
                    nc.vector.tensor_tensor(dd, dd, sums[:, i * 8:i * 8 + 8].rearrange("p (b o) -> p b o", o=1).broadcast_to([96, 8, PER]), ALU.mult).then_inc(S["norm"], 1)
                for i in range(12):
                    m = hp * 12 + i
                    dve.wait_ge(S["sp"], m + 1)
                    v = VT[:, hp, i * NT:i * NT + NT]
                    nc.vector.tensor_tensor(v, P[6 + m % 2][:, 0:NT], v, ALU.mult).then_inc(S["av"], 1)
            for g in range(6):
                dve.wait_ge(S["ot"], g + 1)
                k = min(8, PER - g * 8)
                h = H[:, g * 512:g * 512 + k * D]
                nc.vector.tensor_tensor(h, P[2 + g % 2][0:96, 0:k * D], h, ALU.add).then_inc(S["done"], 1)


def build_moe(nc, H, out, dT_d, gate, gateb, w12, w3, aconst):
    f32, f32r = mybir.dt.float32, mybir.dt.float32r
    ALU, ACT, AX = mybir.AluOpType, mybir.ActivationFunctionType, mybir.AxisListType
    ctx = ExitStack()
    with ctx:
        sb = lambda name, shape, dt=f32: ctx.enter_context(nc.sbuf_tensor(name, shape, dt))
        sem = lambda name: ctx.enter_context(nc.semaphore(name))
        cst = sb("mc", [96, NACONST])
        order, ident = cst[:, PER + 128:PER + 128 + EXPERTS], cst[:, PER + 128 + EXPERTS:]
        xT = sb("mxT", [128, TOK], f32r)
        whi, wlo = sb("mwh", [128, EXPERTS, 2 * HID], f32r), sb("mwl", [128, EXPERTS, 2 * HID], f32r)
        ghi = sb("mg", [128, 2 * EXPERTS], f32r)
        w3s = sb("mw3", [128, EXPERTS, D])
        scr = sb("mscr", [128, 8 * PER * EXPERTS])
        xn = sb("mxn", [96, PER, 128])
        disp = sb("mdisp", [96, PER, EXPERTS])
        dTs = sb("mdT", [EXPERTS, TOK])
        oT = dTs
        acc = sb("macc", [D, TOK])
        dB = sb("mdB", [128, 2, EXPERTS // 4, NT])
        s1 = sb("ms1", [128, 2, NT])
        hid = sb("mhid", [128, 3, NT])
        stat = sb("mst", [96, 3 * PER + 1])
        small = sb("msm", [96, 4 * PER])
        gb = sb("mgb", [96, EXPERTS])
        wraw = scr[:, 0:EXPERTS * 2 * HID].rearrange("p (e m) -> p e m", e=EXPERTS)
        graw = scr[:, EXPERTS * 2 * HID:EXPERTS * 2 * HID + EXPERTS]
        P = [ctx.enter_context(nc.psum_tensor(f"MP{i}", [128, 512], f32)) for i in range(8)]
        S = {n: sem("m_" + n) for n in ("par", "chain", "var", "rstd", "xn", "tr", "xT", "w", "lg", "lgd", "rt", "dt", "dte", "dst", "h", "silu", "prod", "hid", "acc", "accd", "ot", "fin", "st")}
        dbs = [sem(f"m_db{u}") for u in range(2)]
        block = ctx.enter_context(nc.Block())
        STEPS = 12 * EXPERTS
        QE = EXPERTS // 4

        @block.sync
        def _(sp):
            sp.dma_start(cst[:, :], aconst).then_inc(S["par"], 16)
            for h in range(2):
                sp.dma_start(wraw[h * 64:h * 64 + 64], w12).then_inc(S["par"], 16)
                sp.dma_start(graw[h * 64:h * 64 + 64, :], gate).then_inc(S["par"], 16)
            sp.dma_start(w3s[:, :, :], w3).then_inc(S["par"], 16)
            sp.dma_start(gb[:, :], gateb.broadcast_to([96, EXPERTS])).then_inc(S["par"], 16)
            sp.wait_ge(S["dte"], 12)
            sp.dma_start(dT_d, dTs[:, :]).then_inc(S["dst"], 16)
            sp.wait_ge(S["dst"], 16)
            for n in range(12 * 4):
                t, c = n // 4, n % 4
                if n >= 2:
                    sp.wait_ge(S["hid"], (n - 2) * QE + QE)
                src = dT_d[c * QE:c * QE + QE, t * NT:t * NT + NT].rearrange("(o e) n -> o e n", o=1).broadcast_to([128, QE, NT])
                sp.dma_start(dB[:, n % 2], src).then_inc(dbs[n % 2], 16)
            for g in range(6):
                sp.wait_ge(S["fin"], g + 1)
                k = min(8, PER - g * 8)
                sp.dma_start(out.rearrange("i n -> (i n)").rearrange("(p n) -> p n", p=ROWS)[:, g * 512:g * 512 + k * D], H[:, g * 512:g * 512 + k * D]).then_inc(S["st"], 16)
            sp.wait_ge(S["st"], 96)

        @block.gpsimd
        def _(pool):
            for n in range(STEPS):
                q = n // QE
                pool.wait_ge(S["prod"], n + 1)
                if n % QE == 0:
                    pool.wait_ge(dbs[q % 2], (q // 2 + 1) * 16)
                nc.gpsimd.tensor_tensor(hid[:, n % 3, :], hid[:, n % 3, :], dB[:, q % 2, n % QE, :], ALU.mult).then_inc(S["hid"], 1)

        @block.tensor
        def _(pe):
            pe.wait_ge(S["par"], 112)
            pe.wait_ge(S["xn"], 1)
            for j in range(PER):
                if j >= 8 and j % 4 == 0:
                    pe.wait_ge(S["xT"], j // 4 - 1)
                last = nc.tensor.matmul(P[(j // 4) % 2][:, (j % 4) * 96:(j % 4) * 96 + 96], xn[:, j, :], ident[:, 0:96], start=True, stop=True, is_transpose=True)
                if j % 4 == 3 or j == PER - 1:
                    last.then_inc(S["tr"], 1)
            pe.wait_ge(S["xT"], 12)
            pe.wait_ge(S["w"], 1)
            for j in range(PER):
                last = nc.tensor.matmul(P[2 + j // 16][0:96, (j % 16) * 32:(j % 16) * 32 + 32], xT[:, j:j + 1 + PER * 95:PER], ghi[:, :], start=True, stop=True)
            last.then_inc(S["lg"], 1)
            pe.wait_ge(S["rt"], 1)
            for g in range(12):
                if g >= 2:
                    pe.wait_ge(S["dte"], g - 1)
                k = min(4, PER - 4 * g)
                for i in range(k):
                    last = nc.tensor.matmul(P[5 + g % 2][0:EXPERTS, i * 96:i * 96 + 96], disp[:, 4 * g + i, :], ident[:, 0:96], start=True, stop=True, is_transpose=True)
                last.then_inc(S["dt"], 1)
            for n in range(STEPS + 3):
                if n < STEPS:
                    t, e = n // EXPERTS, n % EXPERTS
                    x = xT[:, t * NT:t * NT + NT]
                    if n >= 2:
                        pe.wait_ge(S["prod"], n - 1)
                    for k in range(2):
                        o = slice(k * HID, k * HID + HID)
                        nc.tensor.matmul(P[2 * k + n % 2][:, 0:NT], whi[:, e, o], x, start=True, stop=False)
                        nc.tensor.matmul(P[2 * k + n % 2][:, 0:NT], wlo[:, e, o], x, start=False, stop=True).then_inc(S["h"], 1)
                m = n - 3
                if m >= 0:
                    t, e = m // EXPERTS, m % EXPERTS
                    pe.wait_ge(S["hid"], m + 1)
                    if e == 0 and t >= 2:
                        pe.wait_ge(S["accd"], t - 1)
                    last = nc.tensor.matmul(P[4 + t % 2][0:D, 0:NT], w3s[:, e, :], hid[:, m % 3, :], start=e == 0, stop=e == EXPERTS - 1)
                    last.then_inc(S["acc"], 1)
            pe.wait_ge(S["accd"], 12)
            for g in range(6):
                if g >= 2:
                    pe.wait_ge(S["fin"], g - 1)
                for j in range(g * 8, min(g * 8 + 8, PER)):
                    last = nc.tensor.matmul(P[6 + g % 2][0:96, (j - g * 8) * D:(j - g * 8) * D + D], acc[:, j:j + 1 + PER * 95:PER], ident[0:D, 0:D], start=True, stop=True, is_transpose=True)
                last.then_inc(S["ot"], 1)

        @block.scalar
        def _(act):
            act.wait_ge(S["var"], 1)
            nc.scalar.activation(stat[:, 2 * PER:3 * PER], stat[:, PER:2 * PER], ACT.Sqrt, bias=stat[:, 3 * PER:3 * PER + 1], scale=1.0 / D).then_inc(S["rstd"], 1)
            act.wait_ge(S["lgd"], 1)
            lg = scr[0:96, 0:PER * EXPERTS]
            nc.scalar.activation(lg, lg, ACT.Exp).then_inc(S["lgd"], 1)
            for n in range(STEPS):
                t, e = n // EXPERTS, n % EXPERTS
                act.wait_ge(S["h"], 2 * n + 1)
                if n >= 2:
                    act.wait_ge(S["prod"], n - 1)
                nc.scalar.activation(s1[:, n % 2, :], P[n % 2][:, 0:NT], ACT.Silu).then_inc(S["silu"], 1)
                if e == 2 and t >= 1:
                    pass
                if e == 6 and t >= 1:
                    act.wait_ge(S["acc"], t * EXPERTS)
                    nc.scalar.activation(acc[:, (t - 1) * NT:t * NT], P[4 + (t - 1) % 2][0:D, 0:NT], ACT.Copy).then_inc(S["accd"], 1)
            act.wait_ge(S["acc"], 12 * EXPERTS)
            nc.scalar.activation(acc[:, 11 * NT:12 * NT], P[5][0:D, 0:NT], ACT.Copy).then_inc(S["accd"], 1)

        @block.vector
        def _(dve):
            chained = [0]

            def link(ins):
                chained[0] += 1
                ins.then_inc(S["chain"], 1)
                dve.wait_ge(S["chain"], chained[0])
            link(nc.vector.memset(stat[:, 3 * PER:], EPS))

            def act_sqrt(var, rstd):
                nc.vector.nop().then_inc(S["var"], 1)
                dve.wait_ge(S["rstd"], 1)
            layernorm(nc, ALU, AX, link, dve, act_sqrt, H, xn[:, :, :], stat).then_inc(S["xn"], 1)
            dve.wait_ge(S["par"], 112)
            link(nc.vector.tensor_copy(whi[:, :, :], wraw))
            link(nc.vector.tensor_tensor(wlo[:, :, :], wraw, whi[:, :, :], ALU.subtract))
            link(nc.vector.tensor_copy(ghi[:, 0:EXPERTS], graw))
            link(nc.vector.tensor_tensor(ghi[:, EXPERTS:], graw, ghi[:, 0:EXPERTS], ALU.subtract))
            nc.vector.nop().then_inc(S["w"], 1)
            xv = xT[:, :].rearrange("d (p j) -> d j p", j=PER)
            for g in range(12):
                dve.wait_ge(S["tr"], g + 1)
                k = min(4, PER - 4 * g)
                src = P[g % 2][:, 0:k * 96].rearrange("d (j p) -> d j p", p=96)
                link(nc.vector.tensor_copy(xv[:, 4 * g:4 * g + k], src))
                nc.vector.tensor_tensor(xv[64:128, 4 * g:4 * g + k], src[64:128], xv[64:128, 4 * g:4 * g + k], ALU.subtract).then_inc(S["xT"], 1)
            n, E_ = PER * EXPERTS, EXPERTS
            arr = [scr[0:96, i * n:i * n + n].rearrange("p (j e) -> p j e", e=E_) for i in range(8)]
            lg, pr, hit, idx, one1, one2, rest, tmp = arr
            cols = [small[:, i * PER:i * PER + PER] for i in range(4)]

            def over_e(x):
                return x.rearrange("p (j o) -> p j o", o=1).broadcast_to([ROWS, PER, E_])

            def over_j(x):
                return x.rearrange("p (o e) -> p o e", o=1).broadcast_to([ROWS, PER, E_])
            dve.wait_ge(S["lg"], 1)
            for b in range(3):
                k = min(16, PER - 16 * b)
                src = P[2 + b][0:96, 0:k * 32].rearrange("p (j w e) -> p j w e", w=2, e=E_)
                link(nc.vector.tensor_copy(lg[:, 16 * b:16 * b + k], src[:, :, 1]))
                link(nc.vector.tensor_tensor(lg[:, 16 * b:16 * b + k], src[:, :, 0], lg[:, 16 * b:16 * b + k], ALU.add))
            link(nc.vector.tensor_tensor(lg, lg, over_j(gb[:, :]), ALU.add))
            link(nc.vector.tensor_reduce(cols[0], lg, axis=AX.X, op=ALU.max))
            nc.vector.tensor_tensor(lg, lg, over_e(cols[0]), ALU.subtract).then_inc(S["lgd"], 1)
            dve.wait_ge(S["lgd"], 2)
            link(nc.vector.tensor_reduce(cols[0], lg, axis=AX.X, op=ALU.add))
            link(nc.vector.reciprocal(cols[0], cols[0]))
            link(nc.vector.tensor_tensor(pr, lg, over_e(cols[0]), ALU.mult))
            link(nc.vector.tensor_copy(rest, pr))
            for top, one in ((cols[1], one1), (cols[2], one2)):
                link(nc.vector.tensor_reduce(top, rest, axis=AX.X, op=ALU.max))
                link(nc.vector.tensor_tensor(hit, rest, over_e(top), ALU.is_equal))
                link(nc.vector.tensor_scalar(idx, hit, -float(E_), float(E_), ALU.mult, ALU.add))
                link(nc.vector.tensor_tensor(idx, idx, over_j(order), ALU.add))
                link(nc.vector.tensor_reduce(cols[3], idx, axis=AX.X, op=ALU.min))
                link(nc.vector.tensor_tensor(one, idx, over_e(cols[3]), ALU.is_equal))
                link(nc.vector.tensor_scalar(tmp, one, -2.0, None, ALU.mult))
                link(nc.vector.tensor_tensor(rest, rest, tmp, ALU.add))
            link(nc.vector.tensor_tensor(cols[1], cols[1], cols[2], ALU.add))
            link(nc.vector.reciprocal(cols[1], cols[1]))
            link(nc.vector.tensor_tensor(one1, one1, one2, ALU.add))
            link(nc.vector.tensor_tensor(pr, pr, one1, ALU.mult))
            nc.vector.tensor_tensor(disp[:, :, :], pr, over_e(cols[1]), ALU.mult).then_inc(S["rt"], 1)
            dv = dTs[:, :].rearrange("e (p j) -> e j p", j=PER)
            for g in range(12):
                dve.wait_ge(S["dt"], g + 1)
                k = min(4, PER - 4 * g)
                nc.vector.tensor_copy(dv[:, 4 * g:4 * g + k], P[5 + g % 2][0:EXPERTS, 0:k * 96].rearrange("e (j p) -> e j p", p=96)).then_inc(S["dte"], 1)
            for m in range(STEPS):
                dve.wait_ge(S["h"], 2 * m + 2)
                dve.wait_ge(S["silu"], m + 1)
                if m >= 3:
                    dve.wait_ge(S["acc"], m - 2)
                nc.vector.tensor_tensor(hid[:, m % 3, :], P[2 + m % 2][:, 0:NT], s1[:, m % 2, :], ALU.mult).then_inc(S["prod"], 1)
            for g in range(6):
                dve.wait_ge(S["ot"], g + 1)
                k = min(8, PER - g * 8)
                h = H[:, g * 512:g * 512 + k * D]
                nc.vector.tensor_tensor(h, P[6 + g % 2][0:96, 0:k * D], h, ALU.add).then_inc(S["fin"], 1)


def build(nc, a, out):
    f32 = mybir.dt.float32
    z_d = nc.dram_tensor("z_d", (PAIRS, 128, PX), f32).ap()
    X_d = nc.dram_tensor("X_d", (3, CHUNKS, WIDTH, IMG, CM), f32).ap()
    G_d = nc.dram_tensor("G_d", (IMG, 2, KY, KX * WIDTH), f32).ap()
    H_d = nc.dram_tensor("H_d", (IMG, SEQ * D), f32).ap()
    dT_d = nc.dram_tensor("dT_d", (EXPERTS, TOK), f32).ap()
    with ExitStack() as ctx:
        small = ctx.enter_context(nc.sbuf_tensor("small", [128, 64], f32))
        build_fno(nc, small, a["x6"], a["fc0"], a["fc0T"], a["fc0b"], a["wmix"], a["pwT"], a["pwb"], a["gamma"], a["beta"], a["consts"], z_d, X_d, G_d)
        build_head(nc, small[:, 12:13], small[:, 13:14], z_d, H_d, a["txt"], a["fc1"], a["fc1b"], a["fc2"], a["fc2b"])
        H = ctx.enter_context(nc.sbuf_tensor("H", [ROWS, PER * D], f32))
        build_attention(nc, H[:, :], H_d, a["wqkv"], a["bqkv"], a["w0"], a["b0"], a["aconst"])
        build_moe(nc, H[:, :], out, dT_d, a["gate"], a["gateb"], a["w12"], a["w3"], a["aconst"])


def kernel(**inputs):
    import numpy as _np
    import concourse.bacc as _bacc
    from concourse import mybir as _mybir
    from concourse.bass_utils import run_bass_kernel_spmd as _run

    d = {k: _np.asarray(v) for k, v in inputs.items()}
    f = {k[3:]: v for k, v in d.items() if k.startswith("L0_")}
    wr = _np.stack([f["tok_w1r"], f["tok_w2r"]], axis=1)
    wi = _np.stack([f["tok_w1i"], f["tok_w2i"]], axis=1)
    wmix = _np.stack([wr, wi], axis=2).reshape(LAYERS, 2, 128, WIDTH, 16, 16).transpose(0, 1, 4, 2, 5, 3)
    wqkv = f["attn_Wqkv"].reshape(D, 3, D, HEADS).transpose(0, 1, 3, 2)
    bqkv = f["attn_bqkv"].reshape(3, D, HEADS).transpose(2, 1, 0).reshape(HP, 128, 3).transpose(1, 2, 0)
    host = {
        "x6": d["x"].reshape(2, PAIRS, PX, CH).transpose(1, 0, 3, 2).reshape(PAIRS, 2 * CH, PX),
        "txt": d["txt"].reshape(IMG, TXT * D),
        "fc0": f["tok_fc0_w"], "fc0T": f["tok_fc0_w"].T, "fc0b": f["tok_fc0_b"].reshape(WIDTH, 1),
        "wmix": wmix.reshape(LAYERS, WP, 128, 16 * WIDTH),
        "pwT": f["tok_pw_w"].transpose(0, 2, 1),
        "pwb": f["tok_pw_b"].reshape(LAYERS, WIDTH, 1),
        "gamma": f["tok_gamma"].reshape(LAYERS, WIDTH, 1), "beta": f["tok_beta"].reshape(LAYERS, WIDTH, 1),
        "fc1": f["tok_fc1_w"], "fc1b": f["tok_fc1_b"].reshape(HIDDEN1, 1),
        "fc2": f["tok_fc2_w"], "fc2b": f["tok_fc2_b"].reshape(1, 1),
        "wqkv": wqkv.reshape(D, 12, 128), "bqkv": bqkv.reshape(128, 12),
        "w0": f["attn_W0"].reshape(D, HEADS, D).transpose(1, 0, 2).reshape(HP, 128, D).transpose(1, 0, 2),
        "b0": f["attn_b0"].reshape(D, 1),
        "gate": f["ffn_gate_w"], "gateb": f["ffn_gate_b"].reshape(1, EXPERTS),
        "w12": _np.concatenate([f["ffn_w1"], f["ffn_w2"]], axis=2).transpose(1, 0, 2),
        "w3": f["ffn_w3"].transpose(1, 0, 2),
        "consts": dft_constants(), "aconst": attention_constants(),
    }
    nc = _bacc.Bacc("TRN2", target_bir_lowering=False, num_devices=1)
    arrays, aps = {}, {}
    for name, value in host.items():
        value = _np.ascontiguousarray(value)
        arrays[f"in_{name}"] = value
        aps[name] = nc.dram_tensor(f"in_{name}", value.shape, _mybir.dt.from_np(value.dtype), kind="ExternalInput").ap()
    out = nc.dram_tensor("out_0", (IMG, SEQ * D), _mybir.dt.float32, kind="ExternalOutput").ap()
    build(nc, aps, out)
    r = _run(nc, [arrays], core_ids=[0])
    return r.results[0]["out_0"].reshape(IMG, SEQ, D)
```

```python
import numpy as np
import concourse.bass as bass
from concourse import mybir
from contextlib import ExitStack

IMG, SIDE, CH, WIDTH, LAYERS = 32, 64, 3, 64, 4
M1, M2 = 16, 16
PAIRS = IMG // 2
PX = SIDE * SIDE
KY, KX = 2 * M1, M2
MODES = KY * KX
CHUNKS = 8
CM = MODES // CHUNKS
WP = MODES // 16
W_LATE = 20
HIDDEN1 = 128
TXT, D = 77, 64
SEQ = SIDE + TXT
TOK = IMG * SEQ
EPS = 1e-5


def dft_constants():
    w = 2 * np.pi / SIDE
    pos, kx = np.arange(SIDE), np.arange(KX)
    ky = np.concatenate([np.arange(M1), np.arange(SIDE - M1, SIDE)])
    ident = np.eye(128)
    f1 = np.zeros((2, SIDE, 2, KX, 2))
    for r in range(2):
        f1[r, :, r, :, 0] = np.cos(w * np.outer(pos, kx))
        f1[r, :, r, :, 1] = -np.sin(w * np.outer(pos, kx))
    f2 = np.zeros((2, SIDE, 2, KY))
    c, s = np.cos(w * np.outer(pos, ky)), np.sin(w * np.outer(pos, ky))
    f2[0, :, 0], f2[1, :, 0], f2[0, :, 1], f2[1, :, 1] = c, s, -s, c
    i1 = np.kron(np.eye(2), np.block([[c.T, s.T], [-s.T, c.T]]))
    i2 = np.zeros((4, KX, 2, 4, SIDE))
    g = np.where(kx == 0, 1.0, 2.0)[:, None] / PX
    for r in range(4):
        i2[r, :, 0, r] = g * np.cos(w * np.outer(kx, pos))
        i2[r, :, 1, r] = -g * np.sin(w * np.outer(kx, pos))
    avg = (np.arange(128)[:, None] % 64 == np.arange(128)[None] % 64) * 0.5
    none = np.zeros((128, 64))
    parts = [ident, f1.reshape(128, 64), none, f2.reshape(128, 64), none, i1, avg, i2.reshape(128, 256)]
    return np.concatenate(parts, axis=1).astype(np.float32)


NCONST = 128 + 128 + 128 + 256 + 128 + 256


def build_fno(nc, small, x6, fc0, fc0T, fc0b, wmix, pwT, pwb, gamma, beta, consts, z_d, X_d, G_d, layers=LAYERS):
    f32, f32r = mybir.dt.float32, mybir.dt.float32r
    ALU, ACT, AX = mybir.AluOpType, mybir.ActivationFunctionType, mybir.AxisListType
    ctx = ExitStack()
    with ctx:
        def sb(name, shape, dt=f32):
            return ctx.enter_context(nc.sbuf_tensor(name, shape, dt))

        def sem(name):
            return ctx.enter_context(nc.semaphore(name))

        with ExitStack() as under:
            zparts = under.enter_context(nc.sbuf_tensor("zparts", [128, 2, 2, 1024], f32r))
            ATr = under.enter_context(nc.sbuf_tensor("ATr", [128, 2, 2, 512], f32r))
            i1h, i1l = (under.enter_context(nc.sbuf_tensor(name, [128, 256], f32r)) for name in ("i1h", "i1l"))
            Gr = under.enter_context(nc.sbuf_tensor("Gr", [128, 2, 2, 1024], f32r))
        W = sb("W", [128, WP, 1024])
        work = sb("work", [128, 18432])
        i2h, i2l = sb("i2h", [128, 256], f32r), sb("i2l", [128, 256], f32r)
        pwh, pwl = sb("pwh", [128, 128], f32r), sb("pwl", [128, 128], f32r)
        cst = sb("cst", [128, NCONST - 256])
        wbd = sb("wbd", [128, 128])
        wc6 = sb("wc6", [96, 128])
        P = [ctx.enter_context(nc.psum_tensor(f"P{i}", [128, 512], f32)) for i in range(8)]
        ident, f1r, f2r = cst[:, 0:128], cst[:, 128:256], cst[:, 256:384]
        i1r, avg = cst[:, 384:640], cst[:, 640:768]

        def part(off, n):
            return work[:, off:off + n]
        zbuf = [part(0, 4096), part(4096, 4096)]
        hT = [part(8192, 1024), part(9216, 1024)]
        hT2 = [part(10240, 512), part(10752, 512)]
        A1 = [part(11264, 2048), part(13312, 2048)]
        Xs = [part(15360, 1024), part(16384, 1024)]
        XM = [part(i * 4096, 4096) for i in range(4)]
        Gs = [part(16384, 1024), part(17408, 1024)]
        Ai = [part(8192, 2048), part(10240, 2048)]
        Gt = [part(14336, 1024), part(15360, 1024)]
        ybuf = [part(16384, 1024), part(17408, 1024)]
        stats = W[:, WP - 1, 0:768]
        xall = work[0:96, 0:4096]
        sel0 = work[0:96, 4096:6144]
        Xx = work[0:96, 6144:7168]
        Xs0 = Xs + [part(0, 1024), part(1024, 1024)]
        i2r = part(7168, 256)
        fc0Tbd = small[:, 16:22]
        fc0b_c, pwb_c, gam_c, bet_c = (small[:, i:i + 1] for i in range(4))
        bias0, mv, e2, st2 = small[:, 4:5], small[:, 6:8], small[:, 8:9], small[:, 10:12]
        bsc, bbi = small[:, 12:13], small[:, 13:14]
        rstd, std = small[:, 14:15], small[:, 15:16]
        fc0b4k = small[:, 24:25]
        tmp = small[:, 26:28]
        eps_c = small[:, 28:29]

        S = {n: sem(n) for n in (
            "s_const", "w_loaded", "z_zero", "sp_phase", "s_zero", "s_w0", "s_parload",
            "a0_pe", "a0_ev", "a0_mx", "a0_re", "a0_im", "a0_dc", "x_re", "x_im",
            "z_gelu", "pT1", "pF1", "pT2", "pF2", "eT1", "eF1", "eT2", "eF2",
            "pM", "eMd", "eMa",
            "pI1", "pT3", "pY", "eI1", "eT3", "eY", "eS", "z_gelu_c", "z_hi", "z_split", "g_hi", "g_split", "eT3h", "pw_hi", "pw_split",
            "pe_phase", "act_phase", "dve_phase", "pool_phase", "chain", "pStat", "eStat", "sAggr", "sVar", "sRstd",
            "x0_load")}
        zl = [[sem(f"zl{u}{q}") for q in range(4)] for u in range(2)]
        xl = [sem(f"xl{u}") for u in range(4)]
        gl = [sem(f"gl{u}") for u in range(2)]
        xst = [sem(f"xst{u}") for u in range(2)]
        x0st = [sem(f"x0st{u}") for u in range(4)]
        gst = [sem(f"gst{u}") for u in range(2)]
        yst = [sem(f"yst{u}") for u in range(2)]

        z_q = z_d.rearrange("(t u) p (q n) -> t u p q n", u=2, q=4)
        x6_q = x6.rearrange("(t u) p (q n) -> t u p q n", u=2, q=4)
        X_s = X_d.rearrange("k c (h t u) n -> t u h c k n", h=2, u=2)

        def mixed(c):
            return XM[c % 4].rearrange("p (i v m) -> p i v m", i=IMG, v=2)

        def plane(X, r):
            return X.rearrange("p (k r m) -> p r k m", r=2, m=CM)[:, r]

        def plane_by_kx(X, r, lo, n):
            return X.rearrange("p (k r y x) -> p r x k y", r=2, k=CHUNKS, x=KX)[:, r, lo:lo + n]
        G_s = G_d.rearrange("(h t u) r y (k v o) -> h t u (r y) k v o", h=2, u=2, v=2, o=WIDTH)
        W_t = W[:, :, :].rearrange("p (t w) n -> p t w n", w=4)
        G_w = G_d.rearrange("i r k n -> k (i r) n")

        def wait(eng, s, v):
            if not isinstance(v, int) or v > 0:
                eng.wait_ge(S[s] if isinstance(s, str) else s, v)

        A0 = [("T1", 0, 0), ("T1", 0, 1)]
        for g in range(4):
            A0 += ([("T1", g + 1, 0), ("T1", g + 1, 1)] if g < 3 else []) + [("F1", g, 0)]
        A0 += [("T2", 0, 0)]
        for g in range(4):
            A0 += ([("T2", g + 1, 0)] if g < 3 else []) + [("F2", g, 0)]

        def a0_count(kind, g, h=0):
            return A0.index((kind, g, h)) + 1

        class At:
            def __init__(self, t, u, q, lag):
                d = q - lag
                back, self.q = -(d // 4), d % 4
                self.par = (u - back) % 2
                self.t = t + (u - back) // 2
                self.pair = self.t * 2 + self.par
                self.s = self.pair * 4 + self.q
                self.ok = not isinstance(self.pair, int) or 0 <= self.pair < PAIRS

        def over_steps(eng, body, last=PAIRS // 2 + 1):
            for u in range(2):
                for q in range(4):
                    body(0, u, q)
            with eng.Fori(1, PAIRS // 2) as t:
                for u in range(2):
                    for q in range(4):
                        body(t, u, q)
            for u in range(2):
                for q in range(4):
                    body(PAIRS // 2, u, q)

        OTHERS = {"pe": "act dve pool sp", "act": "pe dve pool sp", "dve": "pe act pool sp", "pool": "pe act dve sp", "sp": "pe act dve pool"}

        def enter(eng, who, n):
            for o in OTHERS[who].split():
                eng.wait_ge(S[o + "_phase"], n)

        def leave(eng, who):
            eng.drain().then_inc(S[who + "_phase"], 1)

        def store_spectra(eng, t, u, X, stored):
            for h in range(2):
                eng.dma_start(X_s[t, u, h], X[h * 64:h * 64 + 64, :].rearrange("p (k n) -> p k n", k=CHUNKS)).then_inc(stored, 16)

        block = ctx.enter_context(nc.Block())

        @block.sync
        def _(sp):
            sp.dma_start(cst[:, :], consts[:, 0:NCONST - 256]).then_inc(S["s_const"], 16)
            sp.dma_start(i2r, consts[:, NCONST - 256:]).then_inc(S["s_const"], 16)
            sp.dma_start(xall, x6.rearrange("b p n -> (b p) n")).then_inc(S["x0_load"], 16)
            sp.dma_start(W[:, 0:W_LATE, :], wmix[0, 0:W_LATE].rearrange("w p n -> p w n")).then_inc(S["w_loaded"], 16)
            sp.wait_ge(S["s_zero"], 2)
            for b in range(PAIRS):
                for h in range(2):
                    r = b * 6 + h * 3
                    sp.dma_start(sel0[r:r + 3, b * 128 + h * 64:b * 128 + h * 64 + 64], fc0).then_inc(S["s_w0"], 16)
            for h in range(2):
                o = slice(h * 64, h * 64 + 64)
                sp.dma_start(fc0Tbd[o, h * 3:h * 3 + 3], fc0T).then_inc(S["s_w0"], 16)
                sp.dma_start(fc0b_c[o, :], fc0b).then_inc(S["s_w0"], 16)
            for b in range(PAIRS):
                sp.wait_ge(S["a0_dc"], b + 1)
                store_spectra(sp, b // 2, b % 2, Xs0[b % 4], x0st[b % 4])
            for u in range(4):
                sp.wait_ge(x0st[u], 4 * 32)
            leave(sp, "sp")

            def layer_parameters(l):
                for h in range(2):
                    o = slice(h * 64, h * 64 + 64)
                    sp.dma_start(wbd[o, o], pwT[l]).then_inc(S["s_parload"], 16)
                    for dst, src in ((pwb_c, pwb), (gam_c, gamma), (bet_c, beta)):
                        sp.dma_start(dst[o, :], src[l]).then_inc(S["s_parload"], 16)

            def mix_loads(l):
                enter(sp, "sp", 3 * l + 1)

                def xm(c):
                    if c >= 4:
                        sp.wait_ge(S["pM"], l * 64 + 8 * (c - 3))
                    sp.dma_start(XM[c % 4][0:64, :], X_d[c].rearrange("c i n -> c (i n)")).then_inc(xl[c % 4], 16)
                for c in range(3):
                    xm(c)
                for k in range(KY):
                    sp.wait_ge(S["eMd"], l * 32 + k + 1)
                    sp.wait_ge(S["eMa"], l * 32 + k + 1)
                    sp.dma_start(G_w[k], Gs[k % 2][0:64, :]).then_inc(gst[k % 2], 16)
                    if k % 4 == 0 and k // 4 + 3 < CHUNKS:
                        xm(k // 4 + 3)
                    if l == 0 and k % 2 == 1 and W_LATE + k - 1 < WP:
                        w = slice(W_LATE + k - 1, W_LATE + k + 1)
                        sp.dma_start(W[:, w, :], wmix[0, w].rearrange("w p n -> p w n")).then_inc(S["w_loaded"], 16)
                    if k == 10:
                        layer_parameters(l)
                for u in range(2):
                    sp.wait_ge(gst[u], (l + 1) * 16 * 16)
                leave(sp, "sp")

            def inv_loads(l, first):
                enter(sp, "sp", 3 * l + 2)
                if first:
                    sp.wait_ge(S["z_zero"], 1)

                def step(t, u, q):
                    a = At(t, u, q, 0)
                    inner = not isinstance(a.pair, int)
                    if q == 0 and a.ok:
                        if inner:
                            sp.wait_ge(S["g_split"], l * 64 + a.pair * 4 - 4)
                        for v in range(2):
                            for h in range(2):
                                dst = Gt[u][v * 64:v * 64 + 64, :].rearrange("p (k h o) -> p h k o", h=2, o=WIDTH)[:, h]
                                sp.dma_start(dst, G_s[h, a.t, u, :, :, v]).then_inc(gl[u], 16)
                    b = At(t, u, q, 8)
                    if b.ok:
                        sp.wait_ge(S["eY"], l * 128 + b.s * 2 + 2)
                        sp.dma_start(z_q[b.t, b.par, :, b.q], ybuf[b.q % 2]).then_inc(yst[b.q % 2], 16)
                    if not a.ok:
                        return
                    if inner:
                        sp.wait_ge(S["z_split"], l * 64 + a.s - 7)
                    o = slice(q * 1024, q * 1024 + 1024)
                    if first:
                        sp.dma_start(zbuf[u][0:6, o], x6_q[a.t, u, :, q]).then_inc(zl[u][q], 16)
                    else:
                        sp.dma_start(zbuf[u][:, o], z_q[a.t, u, :, q]).then_inc(zl[u][q], 16)
                over_steps(sp, step)
                for u in range(2):
                    sp.wait_ge(yst[u], (l + 1) * 32 * 16)
                leave(sp, "sp")

            def fwd_loads(l):
                def load(t, u, q):
                    sp.dma_start(zbuf[u][:, q * 1024:q * 1024 + 1024], z_q[t, u, :, q]).then_inc(zl[u][q], 16)
                sp.wait_ge(S["z_split"], l * 64)
                for u in range(2):
                    for q in range(4):
                        load(0, u, q)
                enter(sp, "sp", 3 * l)

                def step(t, u, q):
                    a = At(t, u, q, 0)
                    if not a.ok:
                        return
                    if not isinstance(a.pair, int):
                        sp.wait_ge(S["pT1"], (l - 1) * 128 + a.s * 2 - 14)
                        load(a.t, u, q)
                    if q % 2 == 1:
                        w = u * 2 + q // 2
                        sp.dma_start(W_t[:, a.t, w], wmix[l].rearrange("(t w) p n -> p t w n", w=4)[:, a.t, w]).then_inc(S["w_loaded"], 16)
                over_steps(sp, step)
                for u in range(2):
                    sp.wait_ge(xst[u], l * 8 * 32)
                leave(sp, "sp")
            mix_loads(0)
            inv_loads(0, True)
            for l in range(1, layers):
                fwd_loads(l)
                mix_loads(l)
                inv_loads(l, False)

        def z_loads_before(l, phase):
            return (l * 2 - 1 if phase == "A" else l * 2) * 8 * 16

        @block.gpsimd
        def _(pool):
            nc.gpsimd.memset(sel0, 0.0)
            nc.gpsimd.memset(small[:, :], 0.0)
            nc.gpsimd.memset(wc6[:, :], 0.0)
            nc.gpsimd.memset(wbd[:, :], 0.0).then_inc(S["s_zero"], 1)
            pool.wait_ge(S["s_zero"], 1)
            nc.gpsimd.memset(eps_c, EPS).then_inc(S["s_zero"], 1)
            pool.wait_ge(S["s_zero"], 2)

            leave(pool, "pool")
            enter(pool, "pool", 1)
            leave(pool, "pool")

            def inv(l, rows):
                enter(pool, "pool", 3 * l + 2)

                def step(t, u, q):
                    a = At(t, u, q, 4)
                    if a.ok:
                        pool.wait_ge(S["z_hi"], l * 64 + a.s + 1)
                        nc.gpsimd.tensor_tensor(zparts[0:rows, a.q % 2, 1, :], zbuf[a.par][0:rows, a.q * 1024:a.q * 1024 + 1024],
                                                zparts[0:rows, a.q % 2, 0, :], ALU.subtract).then_inc(S["z_split"], 1)
                over_steps(pool, step)
                leave(pool, "pool")
            inv(0, 96)
            for l in range(1, layers):
                for n in range(3 * l, 3 * l + 2):
                    enter(pool, "pool", n)
                    leave(pool, "pool")
                inv(l, 128)

        @block.tensor
        def _(pe):
            nc.tensor.nop().then_inc(S["pF2"], 1)
            pe.wait_ge(S["s_const"], 32)
            pe.wait_ge(S["x0_load"], 16)

            def tr(out, in_):
                n = in_.shape[0]
                return nc.tensor.matmul(out, in_, ident[0:n, 0:n], start=True, stop=True, is_transpose=True)

            for kind, g, h in A0:
                if kind == "T1":
                    if g:
                        pe.wait_ge(S["a0_ev"], a0_count("T1", g - 1, h))
                    for i in range(4):
                        o = g * 1024 + h * 512 + i * 128
                        last = tr(P[h][:, i * 128:i * 128 + 96], xall[:, o:o + 128])
                elif kind == "F1":
                    pe.wait_ge(S["a0_ev"], a0_count("T1", g, 1))
                    if g >= 2:
                        pe.wait_ge(S["a0_ev"], a0_count("F1", g - 2))
                    for i in range(8):
                        last = nc.tensor.matmul(P[3 + g % 2][0:96, i * 64:i * 64 + 64], hT[g % 2][:, i * 128:i * 128 + 96], f1r[:, 0:64], start=True, stop=True)
                elif kind == "T2":
                    pe.wait_ge(S["a0_ev"], a0_count("F1", 3) if g < 2 else a0_count("T2", g - 2))
                    for i in range(4):
                        last = tr(P[g % 2][:, i * 128:i * 128 + 96], A1[0][0:96, (4 * g + i) * 128:(4 * g + i) * 128 + 128])
                else:
                    pe.wait_ge(S["a0_ev"], a0_count("T2", g))
                    if g >= 2:
                        pe.wait_ge(S["a0_ev"], a0_count("F2", g - 2))
                    for i in range(4):
                        last = nc.tensor.matmul(P[3 + g % 2][0:96, i * 64:i * 64 + 64], hT2[g % 2][:, i * 128:i * 128 + 96], f2r[:, 0:64], start=True, stop=True)
                last.then_inc(S["a0_pe"], 1)
            pe.wait_ge(S["a0_ev"], len(A0))
            pe.wait_ge(S["s_w0"], 36 * 16)
            for b in range(PAIRS):
                if b >= 2:
                    pe.wait_ge(S["a0_re"], b - 1)
                    pe.wait_ge(S["a0_im"], b - 1)
                for r in range(2):
                    last = nc.tensor.matmul(P[2 * (b % 2) + r][:, :], sel0[:, b * 128:b * 128 + 128], Xx[:, r * 512:r * 512 + 512], start=True, stop=True)
                last.then_inc(S["a0_mx"], 1)
            leave(pe, "pe")

            def mix(l):
                enter(pe, "pe", 3 * l + 1)
                for n in range(64):
                    c, g = n // 8, n % 8
                    if n == 0:
                        pe.wait_ge(S["w_loaded"], 16 + (WP - W_LATE) // 2 * 16 + l * WP * 16 if l else 16)
                    if l == 0 and g == 0 and c * CM // 16 >= W_LATE:
                        pe.wait_ge(S["w_loaded"], 16 + (c * CM // 16 + CM // 16 - W_LATE) // 2 * 16)
                    if g == 0:
                        pe.wait_ge(S["x_re"], l * CHUNKS + c + 1)
                        pe.wait_ge(S["x_im"], l * CHUNKS + c + 1)
                    if n >= 4:
                        pe.wait_ge(S["eMd" if n % 2 == 0 else "eMa"], l * 32 + (n - 4) // 2 + 1)
                    xm = XM[c % 4].rearrange("p (i m) -> p i m", m=CM)
                    for i in range(8):
                        m = g * 8 + i
                        last = nc.tensor.matmul(P[n % 4][0:64, i * 64:i * 64 + 64], xm[:, :, m], W[:, (c * CM + m) // 16, (m % 16) * 64:(m % 16) * 64 + 64], start=True, stop=True)
                    last.then_inc(S["pM"], 1)
                leave(pe, "pe")

            def inv(l, first):
                enter(pe, "pe", 3 * l + 2)
                pe.wait_ge(S["s_parload"], (l + 1) * 128)
                if first:
                    nc.tensor.matmul(P[7][0:6, 0:128], fc0Tbd, wbd[:, :], start=True, stop=True)
                    nc.tensor.matmul(P[6][:, 0:1], wbd[:, :], fc0b_c, start=True, stop=True).then_inc(S["pStat"], 1)
                    pe.wait_ge(S["eStat"], 1)
                pe.wait_ge(S["pw_split"], l + 1)
                rows = 96 if first else 128

                def step(t, u, q):
                    a = At(t, u, q, 5)
                    if a.ok:
                        wait(pe, "eI1", l * 64 + a.pair * 4 + 4)
                        wait(pe, "eT3", l * 64 + a.s - 1 if not first or not isinstance(a.s, int) else a.s - 1)
                        for i in range(4):
                            j = 4 * a.q + i
                            last = tr(P[2 + a.q % 2][:, i * 128:i * 128 + 128], Ai[a.par][:, j * 128:j * 128 + 128])
                        last.then_inc(S["pT3"], 1)
                    a = At(t, u, q, 1)
                    if a.ok:
                        wait(pe, "g_split", l * 64 + a.s + 1)
                        wait(pe, "eI1", l * 64 + a.s - 1)
                        for i in range(2):
                            m = 2 * a.q + i
                            half = P[a.q % 2][:, i * 256:i * 256 + 256]
                            gh, glow = (Gr[:, a.par, part, m * 128:m * 128 + 128] for part in range(2))
                            nc.tensor.matmul(half, gh, i1h[:, :], start=True, stop=False)
                            nc.tensor.matmul(half, gh, i1l[:, :], start=False, stop=False)
                            last = nc.tensor.matmul(half, glow, i1h[:, :], start=False, stop=True)
                        last.then_inc(S["pI1"], 1)
                    a = At(t, u, q, 6)
                    if a.ok:
                        pe.wait_ge(S["z_split"], l * 64 + a.s + 1)
                        pe.wait_ge(S["eT3"], l * 64 + a.s + 1)
                        for h in range(2):
                            bank = P[4 + 2 * (a.q % 2) + h]
                            wait(pe, "eY", l * 128 + a.s * 2 + h - 3)
                            zh, zlow = (zparts[0:rows, a.q % 2, part, h * 512:h * 512 + 512] for part in range(2))
                            nc.tensor.matmul(bank[:, :], pwh[0:rows, :], zh, start=True, stop=False)
                            nc.tensor.matmul(bank[:, :], pwl[0:rows, :], zh, start=False, stop=False)
                            nc.tensor.matmul(bank[:, :], pwh[0:rows, :], zlow, start=False, stop=False)
                            for i in range(2):
                                half = bank[:, i * 256:i * 256 + 256]
                                ath, atl = (ATr[:, a.q % 2, part, (2 * h + i) * 128:(2 * h + i) * 128 + 128] for part in range(2))
                                nc.tensor.matmul(half, ath, i2h[:, :], start=False, stop=False)
                                nc.tensor.matmul(half, ath, i2l[:, :], start=False, stop=False)
                                last = nc.tensor.matmul(half, atl, i2h[:, :], start=False, stop=i == 1)
                            last.then_inc(S["pY"], 1)
                over_steps(pe, step)
                pe.wait_ge(S["sAggr"], l + 1)
                nc.tensor.matmul(P[0][:, 0:2], avg, st2, start=True, stop=True).then_inc(S["pStat"], 1)
                leave(pe, "pe")

            def fwd(l):
                enter(pe, "pe", 3 * l)

                def step(t, u, q):
                    a = At(t, u, q, 2)
                    if a.ok:
                        wait(pe, "z_gelu", (l - 1) * 64 + a.s + 1)
                        for h in range(2):
                            wait(pe, "eT1", (l - 1) * 128 + a.s * 2 + h - 1)
                            for i in range(4):
                                o = a.q * 1024 + h * 512 + i * 128
                                last = tr(P[h][:, i * 128:i * 128 + 128], zbuf[a.par][:, o:o + 128])
                            last.then_inc(S["pT1"], 1)
                    a = At(t, u, q, 8)
                    if a.ok:
                        wait(pe, "eT2", (l - 1) * 64 + a.s + 1)
                        if a.q % 2 == 0:
                            wait(pe, "eF2", (l - 1) * 32 + a.pair * 2 + a.q // 2 + 1)
                        for i in range(4):
                            m = (a.q % 2) * 4 + i
                            n = 96 if m < 7 else 64
                            last = nc.tensor.matmul(P[5 + a.q // 2][:, m * 64:m * 64 + n], hT2[a.q % 2][:, i * 128:i * 128 + 128], f2r[:, 0:n], start=True, stop=True)
                        last.then_inc(S["pF2"], 1)
                    a = At(t, u, q, 7)
                    if a.ok:
                        wait(pe, "eF1", (l - 1) * 64 + a.pair * 4 + 4)
                        wait(pe, "eT2", (l - 1) * 64 + a.s)
                        for i in range(4):
                            last = tr(P[2][:, i * 128:i * 128 + 128], A1[a.par][:, (4 * a.q + i) * 128:(4 * a.q + i) * 128 + 128])
                        last.then_inc(S["pT2"], 1)
                    a = At(t, u, q, 3)
                    if a.ok:
                        wait(pe, "eT1", (l - 1) * 128 + a.s * 2 + 2)
                        wait(pe, "eF1", (l - 1) * 64 + a.s - 1)
                        for i in range(8):
                            n = 96 if i < 7 else 64
                            last = nc.tensor.matmul(P[3 + a.q % 2][:, i * 64:i * 64 + n], hT[a.q % 2][:, i * 128:i * 128 + 128], f1r[:, 0:n], start=True, stop=True)
                        last.then_inc(S["pF1"], 1)
                over_steps(pe, step)
                leave(pe, "pe")
            mix(0)
            inv(0, True)
            for l in range(1, layers):
                fwd(l)
                mix(l)
                inv(l, False)

        @block.scalar
        def _(act):
            act.wait_ge(S["s_w0"], 36 * 16)
            for b in range(PAIRS):
                act.wait_ge(S["a0_mx"], b + 1)
                if b >= 4:
                    act.wait_ge(x0st[b % 4], 32 * (b // 4))
                nc.scalar.activation(plane(Xs0[b % 4], 0), P[2 * (b % 2)][:, :].rearrange("p (k m) -> p k m", m=CM), ACT.Copy).then_inc(S["a0_re"], 1)
            leave(act, "act")

            def mix(l):
                enter(act, "act", 3 * l + 1)

                def rotate(c):
                    act.wait_ge(xl[c % 4], (l * 2 + c // 4 + 1) * 16)
                    nc.scalar.activation(mixed(c)[64:128, :, 1], mixed(c)[0:64, :, 0], ACT.Copy).then_inc(S["x_re"], 1)
                rotate(0)
                for k in range(KY):
                    if k % 4 == 1 and k // 4 + 1 < CHUNKS:
                        rotate(k // 4 + 1)
                    n = 2 * k + 1
                    act.wait_ge(S["pM"], l * 64 + n + 1)
                    v = l * 256 + 16 * (k // 2)
                    wait(act, gst[k % 2], v if k >= 2 else 0)
                    nc.scalar.activation(Gs[k % 2][0:64, 512:1024], P[n % 4][0:64, :], ACT.Copy).then_inc(S["eMa"], 1)
                leave(act, "act")

            def inv(l, first):
                enter(act, "act", 3 * l + 2)

                def step(t, u, q):
                    c = At(t, u, q, 4)
                    z = zbuf[c.par][0:rows, c.q * 1024:c.q * 1024 + 1024]
                    if c.ok and not first:
                        wait(act, zl[c.par][c.q], z_loads_before(l, "C") + c.t * 16 + 16)
                        nc.scalar.activation(z, z, ACT.Gelu, bias=bbi, scale=bsc).then_inc(S["z_gelu_c"], 1)
                    a = At(t, u, q, 6)
                    if a.ok:
                        for h in range(2):
                            act.wait_ge(S["pY"], l * 128 + a.s * 2 + h + 1)
                            if h == 0:
                                wait(act, yst[a.q % 2], stores_waited(l, a))
                                wait(act, "eS", l * 128 + a.s * 2 - 2)
                            nc.scalar.activation(ybuf[a.q % 2][:, h * 512:h * 512 + 512], P[4 + 2 * (a.q % 2) + h][:, :], ACT.Identity, bias=bias0 if first else pwb_c).then_inc(S["eY"], 1)
                    if c.ok:
                        if first:
                            act.wait_ge(zl[c.par][c.q], c.t * 16 + 16)
                        else:
                            act.wait_ge(S["z_gelu_c"], (l - 1) * 64 + c.s + 1)
                        wait(act, "pY", l * 128 + c.s * 2 - 2)
                        nc.scalar.activation(zparts[0:rows, c.q % 2, 0, :], z, ACT.Copy).then_inc(S["z_hi"], 1)
                if first:
                    act.wait_ge(S["eStat"], 1)
                    act.wait_ge(S["z_zero"], 1)
                rows = 96 if first else 128
                act.wait_ge(S["s_parload"], (l + 1) * 128)
                over_steps(act, step)
                act.wait_ge(S["sVar"], l + 1)
                nc.scalar.activation(std, e2, ACT.Sqrt, bias=eps_c).then_inc(S["sRstd"], 1)
                leave(act, "act")

            def stores_waited(l, a):
                return l * 32 * 16 + (a.pair * 2 + a.q // 2) * 16 if not isinstance(a.pair, int) or a.s >= 2 else 0

            def fwd(l):
                enter(act, "act", 3 * l)

                def step(t, u, q):
                    a = At(t, u, q, 0)
                    if a.ok:
                        wait(act, zl[a.par][a.q], z_loads_before(l, "A") + a.t * 16 + 16)
                        o = slice(a.q * 1024, a.q * 1024 + 1024)
                        nc.scalar.activation(zbuf[a.par][:, o], zbuf[a.par][:, o], ACT.Gelu, bias=bbi, scale=bsc).then_inc(S["z_gelu"], 1)
                    a = At(t, u, q, 3)
                    if a.ok:
                        act.wait_ge(S["pF1"], (l - 1) * 64 + a.s + 1)
                        nc.scalar.activation(A1[a.par].rearrange("p (k y) -> p y k", y=SIDE)[:, 16 * a.q:16 * a.q + 16],
                                             P[3 + a.q % 2][:, :].rearrange("p (y k) -> p y k", k=2 * KX), ACT.Copy).then_inc(S["eF1"], 1)
                    a = At(t, u, q, 8)
                    if a.ok and a.q % 2 == 1:
                        g = a.q // 2
                        act.wait_ge(S["pF2"], (l - 1) * 64 + a.s + 2)
                        if g == 0 and (not isinstance(a.pair, int) or a.pair >= 2):
                            wait(act, xst[a.par], (l - 1) * 256 + a.t * 32)
                        F = P[5 + g][:, :].rearrange("p (x r k y) -> p r x k y", x=8, r=2, k=CHUNKS)
                        nc.scalar.activation(plane_by_kx(Xs[a.par], 0, 8 * g, 8), F[:, 0], ACT.Copy)
                        nc.scalar.activation(plane_by_kx(Xs[a.par], 1, 8 * g, 8), F[:, 1], ACT.Copy).then_inc(S["eF2"], 1)
                        if g == 1:
                            act.wait_ge(S["eF2"], (l - 1) * 32 + a.pair * 2 + 4)
                            store_spectra(act, a.t, a.par, Xs[a.par], xst[a.par])
                over_steps(act, step)
                leave(act, "act")
            mix(0)
            inv(0, True)
            for l in range(1, layers):
                fwd(l)
                mix(l)
                inv(l, False)

        @block.vector
        def _(dve):
            chained = [0]

            def link(ins):
                chained[0] += 1
                ins.then_inc(S["chain"], 1)
                dve.wait_ge(S["chain"], chained[0])
            dve.wait_ge(S["s_const"], 32)
            link(nc.vector.tensor_copy(i2h[:, :], i2r))
            link(nc.vector.tensor_tensor(i2l[:, :], i2r, i2h[:, :], ALU.subtract))
            nc.vector.nop().then_inc(S["eF2"], 2)
            for n, (kind, g, h) in enumerate(A0):
                dve.wait_ge(S["a0_pe"], n + 1)
                if g >= 2 and kind in ("T1", "T2"):
                    dve.wait_ge(S["a0_pe"], a0_count("F" + kind[1], g - 2))
                if kind == "T1":
                    dst = hT[g % 2][:, h * 512:h * 512 + 512].rearrange("p (i c) -> p i c", c=128)[:, :, 0:96]
                    src = P[h][:, :].rearrange("p (i c) -> p i c", c=128)[:, :, 0:96]
                elif kind == "F1":
                    dst = A1[0][0:96, :].rearrange("p (k y) -> p y k", y=SIDE)[:, 16 * g:16 * g + 16]
                    src = P[3 + g % 2][0:96, :].rearrange("p (y k) -> p y k", k=2 * KX)
                elif kind == "T2":
                    dst = hT2[g % 2][:, 0:512].rearrange("p (i c) -> p i c", c=128)[:, :, 0:96]
                    src = P[g % 2][:, :].rearrange("p (i c) -> p i c", c=128)[:, :, 0:96]
                else:
                    dst = Xx.rearrange("p (r y k) -> p k r y", r=2, k=KX)[:, 4 * g:4 * g + 4]
                    src = P[3 + g % 2][0:96, 0:256].rearrange("p (k r y) -> p k r y", k=4, r=2)
                nc.vector.tensor_copy(dst, src).then_inc(S["a0_ev"], 1)
            dve.wait_ge(S["s_w0"], 36 * 16)
            link(nc.vector.tensor_scalar(fc0b4k, fc0b_c, float(PX), None, ALU.mult))
            for b in range(PAIRS):
                dve.wait_ge(S["a0_mx"], b + 1)
                if b >= 4:
                    dve.wait_ge(x0st[b % 4], 32 * (b // 4))
                nc.vector.tensor_copy(plane(Xs0[b % 4], 1), P[2 * (b % 2) + 1][:, :].rearrange("p (k m) -> p k m", m=CM)).then_inc(S["a0_im"], 1)
                dve.wait_ge(S["a0_re"], b + 1)
                nc.vector.tensor_tensor(Xs0[b % 4][:, 0:1], Xs0[b % 4][:, 0:1], fc0b4k, ALU.add).then_inc(S["a0_dc"], 1)
            leave(dve, "dve")

            def mix(l):
                enter(dve, "dve", 3 * l + 1)

                def rotate(c):
                    dve.wait_ge(xl[c % 4], (l * 2 + c // 4 + 1) * 16)
                    nc.vector.tensor_scalar(mixed(c)[64:128, :, 0], mixed(c)[0:64, :, 1], -1.0, None, ALU.mult).then_inc(S["x_im"], 1)
                rotate(0)
                for k in range(KY):
                    if k % 4 == 1 and k // 4 + 1 < CHUNKS:
                        rotate(k // 4 + 1)
                    n = 2 * k
                    dve.wait_ge(S["pM"], l * 64 + n + 1)
                    wait(dve, gst[k % 2], l * 256 + 16 * (k // 2) if k >= 2 else 0)
                    nc.vector.tensor_copy(Gs[k % 2][0:64, 0:512], P[n % 4][0:64, :]).then_inc(S["eMd"], 1)
                leave(dve, "dve")

            def inv(l, first):
                enter(dve, "dve", 3 * l + 2)
                if first:
                    dve.wait_ge(S["pStat"], 1)
                    nc.vector.memset(work[0:96, 0:8192], 0.0).then_inc(S["z_zero"], 1)
                    dve.wait_ge(S["s_zero"], 2)
                    link(nc.vector.tensor_copy(wc6[0:6, :], P[7][0:6, 0:128]))
                dve.wait_ge(S["s_parload"], (l + 1) * 128)
                if first:
                    nc.vector.tensor_tensor(bias0, P[6][:, 0:1], pwb_c, ALU.add).then_inc(S["eStat"], 1)
                link(nc.vector.tensor_copy(i1h[:, :], i1r))
                link(nc.vector.tensor_tensor(i1l[:, :], i1r, i1h[:, :], ALU.subtract))
                rows, pw = (96, wc6[:, :]) if first else (128, wbd[:, :])
                nc.vector.tensor_copy(pwh[0:rows, :], pw).then_inc(S["pw_hi"], 1)
                dve.wait_ge(S["pw_hi"], l + 1)
                nc.vector.tensor_tensor(pwl[0:rows, :], pw, pwh[0:rows, :], ALU.subtract).then_inc(S["pw_split"], 1)

                def step(t, u, q):
                    a = At(t, u, q, 5)
                    if a.ok:
                        dve.wait_ge(S["pT3"], l * 64 + a.s + 1)
                        wait(dve, "pY", l * 128 + a.s * 2 - 2)
                        ath, atl = ATr[:, a.q % 2, 0, :], ATr[:, a.q % 2, 1, :]
                        nc.vector.tensor_copy(ath, P[2 + a.q % 2][:, :]).then_inc(S["eT3h"], 1)
                        dve.wait_ge(S["eT3h"], l * 64 + a.s + 1)
                        nc.vector.tensor_tensor(atl, P[2 + a.q % 2][:, :], ath, ALU.subtract).then_inc(S["eT3"], 1)
                    c = At(t, u, q, 0)
                    if c.ok:
                        o = slice(c.q * 256, c.q * 256 + 256)
                        dve.wait_ge(gl[c.par], l * 512 + c.t * 64 + 64)
                        wait(dve, "pI1", l * 64 + c.s - 7)
                        nc.vector.tensor_copy(Gr[:, c.par, 0, o], Gt[c.par][:, o]).then_inc(S["g_hi"], 1)
                    if c.ok:
                        dve.wait_ge(S["g_hi"], l * 64 + c.s + 1)
                        nc.vector.tensor_tensor(Gr[:, c.par, 1, o], Gt[c.par][:, o], Gr[:, c.par, 0, o], ALU.subtract).then_inc(S["g_split"], 1)
                    a = At(t, u, q, 1)
                    if a.ok:
                        dve.wait_ge(S["pI1"], l * 64 + a.s + 1)
                        nc.vector.tensor_copy(Ai[a.par].rearrange("p (y k) -> p k y", k=2 * KX)[:, 8 * a.q:8 * a.q + 8],
                                              P[a.q % 2][:, :].rearrange("p (k y) -> p k y", y=SIDE)).then_inc(S["eI1"], 1)
                    a = At(t, u, q, 7)
                    if a.ok:
                        for h in range(2):
                            dve.wait_ge(S["eY"], l * 128 + a.s * 2 + h + 1)
                            so = stats.rearrange("p (t c) -> p t c", c=96)[:, a.t, a.par * 48 + (a.q * 2 + h) * 6:a.par * 48 + (a.q * 2 + h) * 6 + 6]
                            nc.vector.bn_stats(so, ybuf[a.q % 2][:, h * 512:h * 512 + 512]).then_inc(S["eS"], 1)
                over_steps(dve, step)
                dve.wait_ge(S["eS"], (l + 1) * 128)
                link(nc.vector.bn_aggr(mv, stats))
                link(nc.vector.tensor_copy(st2[:, 0:1], mv[:, 0:1]))
                link(nc.vector.tensor_tensor(e2, mv[:, 0:1], mv[:, 0:1], ALU.mult))
                nc.vector.tensor_tensor(st2[:, 1:2], mv[:, 1:2], e2, ALU.add).then_inc(S["sAggr"], 1)
                dve.wait_ge(S["pStat"], l + 2)
                link(nc.vector.tensor_copy(tmp, P[0][:, 0:2]))
                link(nc.vector.tensor_tensor(e2, tmp[:, 0:1], tmp[:, 0:1], ALU.mult))
                nc.vector.tensor_tensor(e2, tmp[:, 1:2], e2, ALU.subtract).then_inc(S["sVar"], 1)
                dve.wait_ge(S["sRstd"], l + 1)
                link(nc.vector.reciprocal(rstd, std))
                link(nc.vector.tensor_tensor(bsc, rstd, gam_c, ALU.mult))
                link(nc.vector.tensor_tensor(e2, tmp[:, 0:1], bsc, ALU.mult))
                link(nc.vector.tensor_tensor(bbi, bet_c, e2, ALU.subtract))
                leave(dve, "dve")

            def fwd(l):
                enter(dve, "dve", 3 * l)

                def step(t, u, q):
                    a = At(t, u, q, 2)
                    if a.ok:
                        for h in range(2):
                            dve.wait_ge(S["pT1"], (l - 1) * 128 + a.s * 2 + h + 1)
                            if h == 0:
                                wait(dve, "pF1", (l - 1) * 64 + a.s - 1)
                            nc.vector.tensor_copy(hT[a.q % 2][:, h * 512:h * 512 + 512], P[h][:, :]).then_inc(S["eT1"], 1)
                    a = At(t, u, q, 7)
                    if a.ok:
                        dve.wait_ge(S["pT2"], (l - 1) * 64 + a.s + 1)
                        wait(dve, "pF2", (l - 1) * 64 + a.s)
                        nc.vector.tensor_copy(hT2[a.q % 2], P[2][:, :]).then_inc(S["eT2"], 1)
                over_steps(dve, step)
                leave(dve, "dve")
            mix(0)
            inv(0, True)
            for l in range(1, layers):
                fwd(l)
                mix(l)
                inv(l, False)
ROWS = 96
PER = TOK // ROWS
HEADS = 8
HP = HEADS // 2
THIRD = TOK // 3
NT = 376
EXPERTS, HID = 16, 128


def attention_constants():
    h, t = np.arange(96) // 48, np.arange(96) % 48
    mask = (t[:, None] == np.arange(PER)[None]) * 1.0
    spread = (h[:, None] == (np.arange(128) // 64)[None]) * 1.0
    order = np.tile(np.arange(EXPERTS, dtype=np.float64), (96, 1))
    ident = np.eye(128)[0:96]
    return np.concatenate([mask, spread, order, ident], axis=1).astype(np.float32)


NACONST = PER + 128 + EXPERTS + 128


def over_pairs_steps(eng, body):
    for u in range(2):
        for q in range(4):
            body(0, u, q)
    with eng.Fori(1, PAIRS // 2) as t:
        for u in range(2):
            for q in range(4):
                body(t, u, q)
    for u in range(2):
        for q in range(4):
            body(PAIRS // 2, u, q)


class At:
    def __init__(self, t, u, q, lag):
        d = q - lag
        back, self.q = -(d // 4), d % 4
        self.par = (u - back) % 2
        self.t = t + (u - back) // 2
        self.pair = self.t * 2 + self.par
        self.s = self.pair * 4 + self.q
        self.ok = not isinstance(self.pair, int) or 0 <= self.pair < PAIRS


def build_head(nc, bsc, bbi, z_d, H_d, txt, fc1, fc1b, fc2, fc2b):
    f32, f32r = mybir.dt.float32, mybir.dt.float32r
    ALU, ACT = mybir.AluOpType, mybir.ActivationFunctionType
    ctx = ExitStack()
    with ctx:
        sb = lambda name, shape, dt=f32: ctx.enter_context(nc.sbuf_tensor(name, shape, dt))
        sem = lambda name: ctx.enter_context(nc.semaphore(name))
        zbuf = sb("hz", [128, 2, 4096])
        zhi, zlo = sb("hzh", [128, 2, 1024], f32r), sb("hzl", [128, 2, 1024], f32r)
        g = sb("hg", [128, 2, 4, 512])
        ghi, glo = sb("hgh", [128, 2, 4, 512], f32r), sb("hgl", [128, 2, 4, 512], f32r)
        f1 = sb("hf1", [128, 2, 128])
        f1hi, f1lo = sb("hf1h", [128, 2, 128], f32r), sb("hf1l", [128, 2, 128], f32r)
        fz = sb("hfz", [128, 127])
        fzr = sb("hfzr", [128, 127], f32r)
        bia = sb("hb", [128, 2])
        one = sb("h1", [128, 1])
        ob, ob2 = sb("hob", [32, 2, 512]), sb("hob2", [32, 512])
        P = [ctx.enter_context(nc.psum_tensor(f"HP{i}", [128, 512], f32)) for i in range(8)]
        zeroed, params, text, parts, chain = sem("h_zeroed"), sem("h_params"), sem("h_text"), sem("h_parts"), sem("h_chain")
        z_in = [[sem(f"h_z{u}{q}") for q in range(4)] for u in range(2)]
        h_ready, z_hi, z_split, hid_done, g_ready, g_hi, g_split, out_done, ob_ready = (
            sem("h_" + n) for n in ("ready", "zhi", "zsplit", "hid_done", "g_ready", "ghi", "gsplit", "out_done", "ob_ready"))
        half_sum, stored = sem("h_half"), [sem(f"h_stored{u}") for u in range(2)]
        z_q = z_d.rearrange("(t u) p (q n) -> t u p q n", u=2, q=4)
        H_i = H_d.rearrange("(h t u) n -> h t u n", h=2, u=2)

        def wait(eng, s, v):
            if not isinstance(v, int) or v > 0:
                eng.wait_ge(s, v)
        block = ctx.enter_context(nc.Block())

        @block.sync
        def _(sp):
            sp.dma_start(H_d[:, PX:], txt).then_inc(text, 16)
            sp.dma_start(bia[:, 0:1], fc1b).then_inc(params, 16)
            sp.dma_start(bia[0:32, 1:2], fc2b.broadcast_to([32, 1])).then_inc(params, 16)
            sp.wait_ge(zeroed, 1)
            for h in range(2):
                sp.dma_start(f1[h * 64:h * 64 + 64, h, :], fc1).then_inc(params, 16)
            sp.dma_start(fz[:, 63:64], fc2).then_inc(params, 16)

            def step(t, u, q):
                a = At(t, u, q, 0)
                if a.ok:
                    if not isinstance(a.pair, int):
                        sp.wait_ge(z_split, a.s - 7)
                    sp.dma_start(zbuf[:, u, q * 1024:q * 1024 + 1024], z_q[a.t, u, :, q]).then_inc(z_in[u][q], 16)
                a = At(t, u, q, 8)
                if a.ok and a.q == 3:
                    sp.wait_ge(ob_ready, a.pair + 1)
                    for h in range(2):
                        sp.dma_start(H_i[h, a.t, a.par, 0:PX].rearrange("(c n) -> c n", n=512), ob[h * 8:h * 8 + 8, a.par, :]).then_inc(stored[a.par], 16)
            over_pairs_steps(sp, step)
            for u in range(2):
                sp.wait_ge(stored[u], 8 * 32)
            sp.wait_ge(text, 16)

        @block.gpsimd
        def _(pool):
            nc.gpsimd.memset(f1[:, :, :], 0.0)
            nc.gpsimd.memset(one[:, :], 1.0)
            nc.gpsimd.memset(fz[:, :], 0.0).then_inc(zeroed, 1)
            pool.wait_ge(zeroed, 1)

            def step(t, u, q):
                a = At(t, u, q, 0)
                if a.ok:
                    wait(pool, hid_done, a.s * 4 - 4)
                    pool.wait_ge(h_ready, a.s + 1)
                    z = zbuf[:, a.par, a.q * 1024:a.q * 1024 + 1024]
                    nc.gpsimd.tensor_tensor(zhi[:, a.q % 2, :], z, one[:, :].broadcast_to([128, 1024]), ALU.mult).then_inc(z_hi, 1)
                    pool.wait_ge(z_hi, a.s + 1)
                    nc.gpsimd.tensor_tensor(zlo[:, a.q % 2, :], z, zhi[:, a.q % 2, :], ALU.subtract).then_inc(z_split, 1)
            over_pairs_steps(pool, step)

        @block.scalar
        def _(act):
            act.wait_ge(params, 80)

            def step(t, u, q):
                a = At(t, u, q, 0)
                if a.ok:
                    act.wait_ge(z_in[a.par][a.q], a.t * 16 + 16)
                    z = zbuf[:, a.par, a.q * 1024:a.q * 1024 + 1024]
                    nc.scalar.activation(z, z, ACT.Gelu, bias=bbi, scale=bsc).then_inc(h_ready, 1)
                a = At(t, u, q, 1)
                if a.ok:
                    wait(act, g_split, a.s * 4 - 4)
                    for k in range(4):
                        act.wait_ge(hid_done, a.s * 4 + k + 1)
                        nc.scalar.activation(g[:, a.q % 2, k, :], P[k][:, :], ACT.Gelu, bias=bia[:, 0:1]).then_inc(g_ready, 1)
            over_pairs_steps(act, step)

        @block.tensor
        def _(pe):
            pe.wait_ge(parts, 1)

            def step(t, u, q):
                a = At(t, u, q, 1)
                if a.ok:
                    pe.wait_ge(z_split, a.s + 1)
                    for k in range(4):
                        h, o = k // 2, (k % 2) * 512
                        hi, lo = zhi[:, a.q % 2, o:o + 512], zlo[:, a.q % 2, o:o + 512]
                        wait(pe, g_ready, a.s * 4 + k - 3)
                        nc.tensor.matmul(P[k][:, :], f1hi[:, h, :], hi, start=True, stop=False)
                        nc.tensor.matmul(P[k][:, :], f1lo[:, h, :], hi, start=False, stop=False)
                        nc.tensor.matmul(P[k][:, :], f1hi[:, h, :], lo, start=False, stop=True).then_inc(hid_done, 1)
                a = At(t, u, q, 3)
                if a.ok:
                    if a.q == 0:
                        wait(pe, ob_ready, a.pair - 1)
                    for k in range(4):
                        j = (k // 2) * 8 + a.q * 2 + k % 2
                        pe.wait_ge(g_split, a.s * 4 + k + 1)
                        nc.tensor.matmul(P[4 + a.par][0:64, :], fzr[:, 63 - j:127 - j], ghi[:, a.q % 2, k, :],
                                         start=a.q == 0 and k == 0, stop=False)
                        last = nc.tensor.matmul(P[4 + a.par][0:64, :], fzr[:, 63 - j:127 - j], glo[:, a.q % 2, k, :],
                                                start=False, stop=a.q == 3 and k == 3)
                    last.then_inc(out_done, 1)
            over_pairs_steps(pe, step)

        @block.vector
        def _(dve):
            chained = [0]

            def link(ins):
                chained[0] += 1
                ins.then_inc(chain, 1)
                dve.wait_ge(chain, chained[0])
            dve.wait_ge(params, 80)
            link(nc.vector.tensor_copy(f1hi[:, :, :], f1[:, :, :]))
            link(nc.vector.tensor_tensor(f1lo[:, :, :], f1[:, :, :], f1hi[:, :, :], ALU.subtract))
            link(nc.vector.tensor_copy(fzr[:, :], fz[:, :]))
            nc.vector.tensor_tensor(fzr[:, 95:96], fz[:, 63:64], fzr[:, 63:64], ALU.subtract).then_inc(parts, 1)

            def step(t, u, q):
                a = At(t, u, q, 1)
                if a.ok:
                    for k in range(4):
                        dve.wait_ge(g_ready, a.s * 4 + k + 1)
                        if k == 0:
                            wait(dve, out_done, a.s - 1)
                        nc.vector.tensor_copy(ghi[:, a.q % 2, k, :], g[:, a.q % 2, k, :]).then_inc(g_hi, 1)
                        dve.wait_ge(g_hi, a.s * 4 + k + 1)
                        nc.vector.tensor_tensor(glo[:, a.q % 2, k, :], g[:, a.q % 2, k, :], ghi[:, a.q % 2, k, :], ALU.subtract).then_inc(g_split, 1)
                a = At(t, u, q, 3)
                if a.ok and a.q == 3:
                    dve.wait_ge(out_done, a.pair * 4 + 4)
                    wait(dve, stored[a.par], a.t * 32)
                    wait(dve, ob_ready, a.pair)
                    nc.vector.tensor_scalar(ob2[:, :], P[4 + a.par][32:64, :], bia[0:32, 1:2], None, ALU.add).then_inc(half_sum, 1)
                    dve.wait_ge(half_sum, a.pair + 1)
                    nc.vector.tensor_tensor(ob[:, a.par, :], P[4 + a.par][0:32, :], ob2[:, :], ALU.add).then_inc(ob_ready, 1)
            over_pairs_steps(dve, step)


def layernorm(nc, ALU, AX, link, dve, act_sqrt, H, xn, stat, n=PER):
    mean, var, rstd = stat[:, 0:n], stat[:, n:2 * n], stat[:, 2 * n:3 * n]
    Hv = H.rearrange("p (j d) -> p j d", d=D)
    first, second = xn[:, :, 0:D], xn[:, :, D:2 * D]

    def over_d(x):
        return x.rearrange("p (j o) -> p j o", o=1).broadcast_to([ROWS, n, D])
    link(nc.vector.tensor_reduce(mean, Hv, axis=AX.X, op=ALU.add))
    link(nc.vector.tensor_scalar(mean, mean, 1.0 / D, None, ALU.mult))
    link(nc.vector.tensor_tensor(first, Hv, over_d(mean), ALU.subtract))
    link(nc.vector.tensor_tensor(second, first, first, ALU.mult))
    link(nc.vector.tensor_reduce(var, second, axis=AX.X, op=ALU.add))
    act_sqrt(var, rstd)
    link(nc.vector.reciprocal(rstd, rstd))
    link(nc.vector.tensor_tensor(first, first, over_d(rstd), ALU.mult))
    return nc.vector.tensor_copy(second, first)


def build_attention(nc, H, H_d, wqkv, bqkv, w0, b0, aconst):
    f32, f32r = mybir.dt.float32, mybir.dt.float32r
    ALU, ACT, AX = mybir.AluOpType, mybir.ActivationFunctionType, mybir.AxisListType
    ctx = ExitStack()
    with ctx:
        sb = lambda name, shape, dt=f32: ctx.enter_context(nc.sbuf_tensor(name, shape, dt))
        sem = lambda name: ctx.enter_context(nc.semaphore(name))
        cst = sb("ac", [96, NACONST])
        mask, spread, ident = cst[:, 0:PER], cst[:, PER:PER + 128], cst[:, PER + 128 + EXPERTS:]
        xT = sb("axT", [128, TOK], f32r)
        whi, wlo = sb("awh", [128, 12, 128], f32r), sb("awl", [128, 12, 128], f32r)
        bias = sb("ab", [128, 24])
        VT = sb("aV", [128, HP, TOK])
        QT = sb("aQ", [128, TOK])
        KZ = sb("aKZ", [128, ROWS, 2, 48])
        KZv = KZ[:, :, :, :].rearrange("p (b s) h c -> p b s h c", s=3)
        w0s, b0s = sb("aw0", [128, HP, D]), sb("ab0", [D, 1])
        E = sb("aE", [96, 2, 3 * SEQ + 3])
        nmax, sums = sb("am", [96, ROWS]), sb("as", [96, ROWS])
        stat = sb("ast", [96, 3 * PER + 1])
        wraw = QT[:, 0:12 * 128].rearrange("p (c m) -> p c m", c=12)
        xn = VT[0:96, 0:2, :].rearrange("p a n -> p (a n)")[:, 0:PER * 128].rearrange("p (j d) -> p j d", d=128)
        Dg = sb("aD", [96, ROWS, PER])
        oT = QT[0:D, :]
        TILES = [(b, min(b + 9, ROWS)) for b in range(0, ROWS, 9)]
        NTI = len(TILES)
        P = [ctx.enter_context(nc.psum_tensor(f"AP{i}", [128, 512], f32)) for i in range(8)]
        S = {n: sem("at_" + n) for n in ("h", "par", "chain", "var", "rstd", "xn", "tr", "xT", "zero", "qkv", "evA", "evD", "sc", "max", "exp", "diag", "norm", "sp", "av", "o", "oA", "ot", "done", "whi", "wready")}
        block = ctx.enter_context(nc.Block())
        EV = HP * 36 // 2

        def groups(hp):
            for x in (1, 0, 2):
                for s in range(3):
                    for r in range(4):
                        yield x, s, r

        def tile_at(b, lag):
            i = (b - lag) // 3
            return i if (b - lag) % 3 == 0 and 0 <= i < NTI else None

        def dests(hp, x, s, r):
            if x == 0:
                yield slice(0, 128), QT[:, :].rearrange("p (r s) -> p s r", s=3)[:, s, r * NT:r * NT + NT]
            elif x == 1:
                for h in range(2):
                    o = slice(h * 64, h * 64 + 64)
                    yield o, KZv[o, r * 8:r * 8 + 8, s, h, 0:PER]
            else:
                yield slice(0, 128), VT[:, hp, :].rearrange("p (b s i) -> p b s i", s=3, i=PER)[:, r * 8:r * 8 + 8, s]

        def tiled(tile, x):
            return tile if x == 0 else tile.rearrange("p (b i) -> p b i", i=PER)

        @block.sync
        def _(sp):
            sp.dma_start(H, H_d.rearrange("i n -> (i n)").rearrange("(p n) -> p n", p=ROWS)).then_inc(S["h"], 16)
            sp.dma_start(cst[:, :], aconst).then_inc(S["par"], 16)
            for h in range(2):
                sp.dma_start(wraw[h * 64:h * 64 + 64], wqkv).then_inc(S["par"], 16)
            sp.dma_start(bias[:, 0:12], bqkv).then_inc(S["par"], 16)
            sp.dma_start(w0s[:, :, :], w0).then_inc(S["par"], 16)
            sp.dma_start(b0s[:, :], b0).then_inc(S["par"], 16)

        @block.gpsimd
        def _(pool):
            pool.wait_ge(S["par"], 96)
            nc.gpsimd.tensor_copy(whi[:, :, :], wraw).then_inc(S["whi"], 1)
            pool.wait_ge(S["whi"], 1)
            nc.gpsimd.tensor_tensor(wlo[:, :, :], wraw, whi[:, :, :], ALU.subtract).then_inc(S["wready"], 1)
            nc.gpsimd.memset(KZ[:, :, :, :], 0.0).then_inc(S["zero"], 1)
            for hp in range(HP):
                if hp:
                    pool.wait_ge(S["sp"], hp * NTI)
                for b in range(IMG):
                    pool.wait_ge(S["exp"], hp * ROWS + b * 3 + 3)
                    own = E[:, b % 2, :].rearrange("p (k n) -> p k n", k=3)[:, :, 0:3 * PER - 2:3]
                    nc.gpsimd.tensor_tensor(Dg[:, b * 3:b * 3 + 3, :], own, mask.rearrange("p (o c) -> p o c", o=1).broadcast_to([96, 3, PER]), ALU.mult).then_inc(S["diag"], 1)

        @block.tensor
        def _(pe):
            pe.wait_ge(S["par"], 96)
            pe.wait_ge(S["xn"], 1)
            for j in range(PER):
                if j >= 8 and j % 4 == 0:
                    pe.wait_ge(S["xT"], j // 4 - 1)
                last = nc.tensor.matmul(P[(j // 4) % 2][:, (j % 4) * 96:(j % 4) * 96 + 96], xn[:, j, :], ident[:, 0:96], start=True, stop=True, is_transpose=True)
                if j % 4 == 3 or j == PER - 1:
                    last.then_inc(S["tr"], 1)
            pe.wait_ge(S["xT"], 12)
            pe.wait_ge(S["wready"], 2)
            n = 0
            for hp in range(HP):
                for x, s, r in groups(hp):
                    if n >= 6:
                        pe.wait_ge(S["evA" if n % 2 == 0 else "evD"], n // 2 - 2)
                    rows = xT[:, x * THIRD + r * NT:x * THIRD + r * NT + NT]
                    nc.tensor.matmul(P[n % 6][:, 0:NT], whi[:, s * HP + hp, :], rows, start=True, stop=False)
                    nc.tensor.matmul(P[n % 6][:, 0:NT], wlo[:, s * HP + hp, :], rows, start=False, stop=True).then_inc(S["qkv"], 1)
                    n += 1
                pe.wait_ge(S["evA"], hp * 18 + 18)
                pe.wait_ge(S["evD"], hp * 18 + 18)
                for b in range(IMG + 6):
                    m = hp * IMG + b
                    if b < IMG:
                        if m >= 4:
                            pe.wait_ge(S["exp"], (m - 4) * 3 + 3)
                        for k in range(3):
                            last = nc.tensor.matmul(P[2 + m % 4][0:96, k * SEQ:k * SEQ + SEQ], KZ[:, b * 3 + k, :, :].rearrange("p h c -> p (h c)"), QT[:, b * SEQ:b * SEQ + SEQ], start=True, stop=True)
                        last.then_inc(S["sc"], 1)
                    i = tile_at(b, 6)
                    if i is not None:
                        (lo, hi), m = TILES[i], hp * NTI + i
                        pe.wait_ge(S["norm"], m + 1)
                        if m >= 2:
                            pe.wait_ge(S["av"], m - 1)
                        nc.tensor.matmul(P[6 + m % 2][:, 0:(hi - lo) * PER], spread, Dg[:, lo:hi, :].rearrange("p b c -> p (b c)"), start=True, stop=True).then_inc(S["sp"], 1)
            for i, (lo, hi) in enumerate(TILES):
                pe.wait_ge(S["av"], (HP - 1) * NTI + i + 1)
                if i >= 2:
                    pe.wait_ge(S["oA"], i - 1)
                for hp in range(HP):
                    last = nc.tensor.matmul(P[i % 2][0:D, 0:(hi - lo) * PER], w0s[:, hp, :], VT[:, hp, lo * PER:hi * PER], start=hp == 0, stop=hp == HP - 1)
                last.then_inc(S["o"], 1)
            pe.wait_ge(S["oA"], NTI)
            for g in range(6):
                if g >= 2:
                    pe.wait_ge(S["done"], g - 1)
                js = range(g * 8, min(g * 8 + 8, PER))
                for j in js:
                    last = nc.tensor.matmul(P[2 + g % 2][0:96, (j - g * 8) * D:(j - g * 8) * D + D], oT[:, j:j + 1 + PER * 95:PER], ident[0:D, 0:D], start=True, stop=True, is_transpose=True)
                last.then_inc(S["ot"], 1)

        @block.scalar
        def _(act):
            act.wait_ge(S["var"], 1)
            nc.scalar.activation(stat[:, 2 * PER:3 * PER], stat[:, PER:2 * PER], ACT.Sqrt, bias=stat[:, 3 * PER:3 * PER + 1], scale=1.0 / D).then_inc(S["rstd"], 1)
            act.wait_ge(S["wready"], 2)
            n = 0
            for hp in range(HP):
                for x, s, r in groups(hp):
                    if n % 2 == 0:
                        act.wait_ge(S["qkv"], n + 1)
                        if n % 36 == 0:
                            act.wait_ge(S["zero"], 1)
                            if hp:
                                act.wait_ge(S["sc"], hp * IMG)
                        c = s * HP + hp + (12 if x == 0 else 0)
                        for rows, dst in dests(hp, x, s, r):
                            last = nc.scalar.activation(dst, tiled(P[n % 6][rows, 0:NT], x), ACT.Identity, bias=bias[rows, c:c + 1], scale=0.125 if x == 0 else 1.0)
                        last.then_inc(S["evA"], 1)
                    n += 1
                for b in range(IMG):
                    m = hp * IMG + b
                    act.wait_ge(S["max"], m + 1)
                    if m >= 2:
                        act.wait_ge(S["diag"], m - 1)
                    for k in range(3):
                        c = b * 3 + k
                        nc.scalar.activation(E[:, b % 2, k * SEQ:k * SEQ + SEQ], P[2 + m % 4][0:96, k * SEQ:k * SEQ + SEQ], ACT.Exp, bias=nmax[:, c:c + 1], accum_out=sums[:, c:c + 1]).then_inc(S["exp"], 1)
            for i, (lo, hi) in enumerate(TILES):
                act.wait_ge(S["o"], i + 1)
                dst = oT.rearrange("d (b i s) -> d b s i", i=PER, s=3)[:, lo // 3:hi // 3]
                nc.scalar.activation(dst, P[i % 2][0:D, 0:(hi - lo) * PER].rearrange("d (b s i) -> d b s i", s=3, i=PER), ACT.Identity, bias=b0s[:, :]).then_inc(S["oA"], 1)

        @block.vector
        def _(dve):
            chained = [0]

            def link(ins):
                chained[0] += 1
                ins.then_inc(S["chain"], 1)
                dve.wait_ge(S["chain"], chained[0])
            dve.wait_ge(S["h"], 16)
            link(nc.vector.memset(stat[:, 3 * PER:], EPS))

            def act_sqrt(var, rstd):
                nc.vector.nop().then_inc(S["var"], 1)
                dve.wait_ge(S["rstd"], 1)
            layernorm(nc, ALU, AX, link, dve, act_sqrt, H, xn, stat).then_inc(S["xn"], 1)
            dve.wait_ge(S["par"], 96)
            link(nc.vector.tensor_scalar(bias[:, 12:24], bias[:, 0:12], 0.125, None, ALU.mult))
            nc.vector.nop().then_inc(S["wready"], 1)
            xv = xT[:, :].rearrange("d (p j) -> d j p", j=PER)
            for g in range(12):
                dve.wait_ge(S["tr"], g + 1)
                k = min(4, PER - 4 * g)
                src = P[g % 2][:, 0:k * 96].rearrange("d (j p) -> d j p", p=96)
                link(nc.vector.tensor_copy(xv[:, 4 * g:4 * g + k], src))
                nc.vector.tensor_tensor(xv[64:128, 4 * g:4 * g + k], src[64:128], xv[64:128, 4 * g:4 * g + k], ALU.subtract).then_inc(S["xT"], 1)
            n = 0
            for hp in range(HP):
                for x, s, r in groups(hp):
                    if n % 2 == 1:
                        dve.wait_ge(S["qkv"], n + 1)
                        if n % 36 == 1:
                            dve.wait_ge(S["zero"], 1)
                            if hp:
                                dve.wait_ge(S["sc"], hp * IMG)
                        c = s * HP + hp
                        for rows, dst in dests(hp, x, s, r):
                            last = nc.vector.tensor_scalar(dst, tiled(P[n % 6][rows, 0:NT], x), bias[rows, c:c + 1], 0.125 if x == 0 else 1.0, ALU.add, ALU.mult)
                        last.then_inc(S["evD"], 1)
                    n += 1
                for b in range(IMG + 6):
                    m = hp * IMG + b
                    if b < IMG:
                        dve.wait_ge(S["sc"], m + 1)
                        nc.vector.tensor_reduce(nmax[:, b * 3:b * 3 + 3], P[2 + m % 4][0:96, 0:3 * SEQ].rearrange("p (k n) -> p k n", k=3), axis=AX.X, op=ALU.max, negate=True).then_inc(S["max"], 1)
                    i = tile_at(b, 5)
                    if i is not None:
                        lo, hi = TILES[i]
                        dve.wait_ge(S["exp"], hp * ROWS + hi)
                        link(nc.vector.reciprocal(sums[:, lo:hi], sums[:, lo:hi]))
                        dve.wait_ge(S["diag"], hp * IMG + hi // 3)
                        dd = Dg[:, lo:hi, :]
                        nc.vector.tensor_tensor(dd, dd, sums[:, lo:hi].rearrange("p (b o) -> p b o", o=1).broadcast_to([96, hi - lo, PER]), ALU.mult).then_inc(S["norm"], 1)
                    i = tile_at(b, 7)
                    if i is not None:
                        (lo, hi), m = TILES[i], hp * NTI + i
                        dve.wait_ge(S["evA"], (hp + 1) * 18)
                        dve.wait_ge(S["sp"], m + 1)
                        v = VT[:, hp, lo * PER:hi * PER]
                        nc.vector.tensor_tensor(v, P[6 + m % 2][:, 0:(hi - lo) * PER], v, ALU.mult).then_inc(S["av"], 1)
            for g in range(6):
                dve.wait_ge(S["ot"], g + 1)
                k = min(8, PER - g * 8)
                h = H[:, g * 512:g * 512 + k * D]
                nc.vector.tensor_tensor(h, P[2 + g % 2][0:96, 0:k * D], h, ALU.add).then_inc(S["done"], 1)


def build_moe(nc, H, out, dT_d, gate, gateb, w12, w3, aconst):
    f32, f32r = mybir.dt.float32, mybir.dt.float32r
    ALU, ACT, AX = mybir.AluOpType, mybir.ActivationFunctionType, mybir.AxisListType
    ctx = ExitStack()
    with ctx:
        sb = lambda name, shape, dt=f32: ctx.enter_context(nc.sbuf_tensor(name, shape, dt))
        sem = lambda name: ctx.enter_context(nc.semaphore(name))
        cst = sb("mc", [96, NACONST])
        order, ident = cst[:, PER + 128:PER + 128 + EXPERTS], cst[:, PER + 128 + EXPERTS:]
        xT = sb("mxT", [128, TOK], f32r)
        whi, wlo = sb("mwh", [128, EXPERTS, 2 * HID], f32r), sb("mwl", [128, EXPERTS, 2 * HID], f32r)
        ghi = sb("mg", [128, 2 * EXPERTS], f32r)
        w3s = sb("mw3", [128, EXPERTS, D])
        w3r = sb("mw3r", [128, EXPERTS, 2, D], f32r)
        scr = sb("mscr", [128, 8 * PER * EXPERTS])
        xn = sb("mxn", [96, PER, 128])
        disp = sb("mdisp", [96, PER, EXPERTS])
        dTs = sb("mdT", [EXPERTS, TOK])
        oT = dTs
        acc = sb("macc", [D, TOK])
        dB = sb("mdB", [128, 2, EXPERTS // 4, NT])
        s1 = sb("ms1", [128, 3, NT])
        hid = sb("mhid", [128, 7, NT])
        hhi, hlo = sb("mhh", [128, 4, NT], f32r), sb("mhl", [128, 4, NT], f32r)
        acc2 = sb("macc2", [D, NT])
        stat = sb("mst", [96, 3 * PER + 1])
        small = sb("msm", [96, 4 * PER])
        gb = sb("mgb", [96, EXPERTS])
        wraw = scr[:, 0:EXPERTS * 2 * HID].rearrange("p (e m) -> p e m", e=EXPERTS)
        graw = scr[:, EXPERTS * 2 * HID:EXPERTS * 2 * HID + EXPERTS]
        P = [ctx.enter_context(nc.psum_tensor(f"MP{i}", [128, 512], f32)) for i in range(8)]
        S = {n: sem("m_" + n) for n in ("par", "chain", "var", "rstd", "xn", "tr", "xT", "w", "wh", "lg", "lgd", "rt", "dt", "dte", "dst", "h", "silu", "prod", "hid", "acc", "accd", "acch", "hi", "lo", "ot", "fin", "st")}
        dbs = [sem(f"m_db{u}") for u in range(2)]
        block = ctx.enter_context(nc.Block())
        STEPS = 12 * EXPERTS
        QE = EXPERTS // 4
        H_BANKS = ((0, 1, 6), (2, 3, 7))
        HI, LO, W3 = 4, 5, 7

        @block.sync
        def _(sp):
            sp.dma_start(cst[:, :], aconst).then_inc(S["par"], 16)
            for h in range(2):
                sp.dma_start(wraw[h * 64:h * 64 + 64], w12).then_inc(S["par"], 16)
                sp.dma_start(graw[h * 64:h * 64 + 64, :], gate).then_inc(S["par"], 16)
            sp.dma_start(w3s[:, :, :], w3).then_inc(S["par"], 16)
            sp.dma_start(gb[:, :], gateb.broadcast_to([96, EXPERTS])).then_inc(S["par"], 16)
            sp.wait_ge(S["dte"], 12)
            sp.dma_start(dT_d, dTs[:, :]).then_inc(S["dst"], 16)
            sp.wait_ge(S["dst"], 16)
            for n in range(12 * 4):
                t, c = n // 4, n % 4
                if n >= 2:
                    sp.wait_ge(S["hid"], (n - 2) * QE + QE)
                src = dT_d[c * QE:c * QE + QE, t * NT:t * NT + NT].rearrange("(o e) n -> o e n", o=1).broadcast_to([128, QE, NT])
                sp.dma_start(dB[:, n % 2], src).then_inc(dbs[n % 2], 16)
            for g in range(6):
                sp.wait_ge(S["fin"], g + 1)
                k = min(8, PER - g * 8)
                sp.dma_start(out.rearrange("i n -> (i n)").rearrange("(p n) -> p n", p=ROWS)[:, g * 512:g * 512 + k * D], H[:, g * 512:g * 512 + k * D]).then_inc(S["st"], 16)
            sp.wait_ge(S["st"], 96)

        @block.gpsimd
        def _(pool):
            pool.wait_ge(S["par"], 112)
            parts = ((graw, ghi[:, 0:EXPERTS], ghi[:, EXPERTS:]), (wraw, whi[:, :, :], wlo[:, :, :]), (w3s[:, :, :], w3r[:, :, 0], w3r[:, :, 1]))
            for i, (raw, hi, lo) in enumerate(parts):
                nc.gpsimd.tensor_copy(hi, raw).then_inc(S["wh"], 1)
                pool.wait_ge(S["wh"], i + 1)
                nc.gpsimd.tensor_tensor(lo, raw, hi, ALU.subtract).then_inc(S["w"], 1)
            for n in range(STEPS):
                q = n // QE
                pool.wait_ge(S["prod"], n + 1)
                if n % QE == 0:
                    pool.wait_ge(dbs[q % 2], (q // 2 + 1) * 16)
                nc.gpsimd.tensor_tensor(hid[:, n % 7, :], hid[:, n % 7, :], dB[:, q % 2, n % QE, :], ALU.mult).then_inc(S["hid"], 1)

        @block.tensor
        def _(pe):
            pe.wait_ge(S["par"], 112)
            pe.wait_ge(S["xn"], 1)
            for j in range(PER):
                if j >= 8 and j % 4 == 0:
                    pe.wait_ge(S["xT"], j // 4 - 1)
                last = nc.tensor.matmul(P[(j // 4) % 2][:, (j % 4) * 96:(j % 4) * 96 + 96], xn[:, j, :], ident[:, 0:96], start=True, stop=True, is_transpose=True)
                if j % 4 == 3 or j == PER - 1:
                    last.then_inc(S["tr"], 1)
            pe.wait_ge(S["xT"], 12)
            pe.wait_ge(S["w"], 1)
            for j in range(PER):
                last = nc.tensor.matmul(P[2 + j // 16][0:96, (j % 16) * 32:(j % 16) * 32 + 32], xT[:, j:j + 1 + PER * 95:PER], ghi[:, :], start=True, stop=True)
            last.then_inc(S["lg"], 1)
            pe.wait_ge(S["rt"], 1)
            for g in range(12):
                if g >= 2:
                    pe.wait_ge(S["dte"], g - 1)
                k = min(4, PER - 4 * g)
                for i in range(k):
                    last = nc.tensor.matmul(P[5 + g % 2][0:EXPERTS, i * 96:i * 96 + 96], disp[:, 4 * g + i, :], ident[:, 0:96], start=True, stop=True, is_transpose=True)
                last.then_inc(S["dt"], 1)
            pe.wait_ge(S["w"], 3)
            pe.wait_ge(S["dte"], 12)
            for n in range(STEPS + W3):
                if n < STEPS:
                    t, e = n // EXPERTS, n % EXPERTS
                    x = xT[:, t * NT:t * NT + NT]
                    if n >= 3:
                        pe.wait_ge(S["prod"], n - 2)
                    for k in range(2):
                        o, bank = slice(k * HID, k * HID + HID), P[H_BANKS[k][n % 3]]
                        nc.tensor.matmul(bank[:, 0:NT], whi[:, e, o], x, start=True, stop=False)
                        nc.tensor.matmul(bank[:, 0:NT], wlo[:, e, o], x, start=False, stop=True).then_inc(S["h"], 1)
                m = n - W3
                if m >= 0:
                    t, e = m // EXPERTS, m % EXPERTS
                    pe.wait_ge(S["lo"], m + 1)
                    if e == 0 and t >= 2:
                        pe.wait_ge(S["accd"], t - 1)
                    w = w3r[:, e, :, :].rearrange("p w d -> p (w d)")
                    nc.tensor.matmul(P[4 + t % 2][:, 0:NT], w, hhi[:, m % 4, :], start=e == 0, stop=False)
                    nc.tensor.matmul(P[4 + t % 2][:, 0:NT], w, hlo[:, m % 4, :], start=False, stop=e == EXPERTS - 1).then_inc(S["acc"], 1)
            pe.wait_ge(S["accd"], 12)
            for g in range(6):
                if g >= 2:
                    pe.wait_ge(S["fin"], g - 1)
                for j in range(g * 8, min(g * 8 + 8, PER)):
                    last = nc.tensor.matmul(P[6 + g % 2][0:96, (j - g * 8) * D:(j - g * 8) * D + D], acc[:, j:j + 1 + PER * 95:PER], ident[0:D, 0:D], start=True, stop=True, is_transpose=True)
                last.then_inc(S["ot"], 1)

        @block.scalar
        def _(act):
            def half_sum(t):
                act.wait_ge(S["acc"], (t + 1) * EXPERTS)
                if t:
                    act.wait_ge(S["accd"], t)
                nc.scalar.activation(acc2[:, :], P[4 + t % 2][D:2 * D, 0:NT], ACT.Copy).then_inc(S["acch"], 1)

            act.wait_ge(S["var"], 1)
            nc.scalar.activation(stat[:, 2 * PER:3 * PER], stat[:, PER:2 * PER], ACT.Sqrt, bias=stat[:, 3 * PER:3 * PER + 1], scale=1.0 / D).then_inc(S["rstd"], 1)
            act.wait_ge(S["lgd"], 1)
            lg = scr[0:96, 0:PER * EXPERTS]
            nc.scalar.activation(lg, lg, ACT.Exp).then_inc(S["lgd"], 1)
            for n in range(STEPS + LO):
                if n < STEPS:
                    act.wait_ge(S["h"], 2 * n + 1)
                    if n >= 3:
                        act.wait_ge(S["prod"], n - 2)
                    nc.scalar.activation(s1[:, n % 3, :], P[H_BANKS[0][n % 3]][:, 0:NT], ACT.Silu).then_inc(S["silu"], 1)
                m = n - HI
                if 0 <= m < STEPS:
                    act.wait_ge(S["hid"], m + 1)
                    if m >= 4:
                        act.wait_ge(S["acc"], m - 3)
                    nc.scalar.activation(hhi[:, m % 4, :], hid[:, m % 7, :], ACT.Copy).then_inc(S["hi"], 1)
                t, e = n // EXPERTS, n % EXPERTS
                if e == 7 and t >= 1:
                    half_sum(t - 1)
            half_sum(11)

        @block.vector
        def _(dve):
            chained = [0]

            def link(ins):
                chained[0] += 1
                ins.then_inc(S["chain"], 1)
                dve.wait_ge(S["chain"], chained[0])
            link(nc.vector.memset(stat[:, 3 * PER:], EPS))

            def act_sqrt(var, rstd):
                nc.vector.nop().then_inc(S["var"], 1)
                dve.wait_ge(S["rstd"], 1)
            layernorm(nc, ALU, AX, link, dve, act_sqrt, H, xn[:, :, :], stat).then_inc(S["xn"], 1)
            xv = xT[:, :].rearrange("d (p j) -> d j p", j=PER)
            for g in range(12):
                dve.wait_ge(S["tr"], g + 1)
                k = min(4, PER - 4 * g)
                src = P[g % 2][:, 0:k * 96].rearrange("d (j p) -> d j p", p=96)
                link(nc.vector.tensor_copy(xv[:, 4 * g:4 * g + k], src))
                nc.vector.tensor_tensor(xv[64:128, 4 * g:4 * g + k], src[64:128], xv[64:128, 4 * g:4 * g + k], ALU.subtract).then_inc(S["xT"], 1)
            n, E_ = PER * EXPERTS, EXPERTS
            arr = [scr[0:96, i * n:i * n + n].rearrange("p (j e) -> p j e", e=E_) for i in range(7)]
            lg, pr, hit, idx, one1, one2, rest = arr
            cols = [small[:, i * PER:i * PER + PER] for i in range(4)]

            def over_e(x):
                return x.rearrange("p (j o) -> p j o", o=1).broadcast_to([ROWS, PER, E_])

            def over_j(x):
                return x.rearrange("p (o e) -> p o e", o=1).broadcast_to([ROWS, PER, E_])
            dve.wait_ge(S["w"], 2)
            dve.wait_ge(S["lg"], 1)
            for b in range(3):
                k = min(16, PER - 16 * b)
                src = P[2 + b][0:96, 0:k * 32].rearrange("p (j w e) -> p j w e", w=2, e=E_)
                link(nc.vector.tensor_copy(lg[:, 16 * b:16 * b + k], src[:, :, 1]))
                link(nc.vector.tensor_tensor(lg[:, 16 * b:16 * b + k], src[:, :, 0], lg[:, 16 * b:16 * b + k], ALU.add))
            link(nc.vector.tensor_tensor(lg, lg, over_j(gb[:, :]), ALU.add))
            link(nc.vector.tensor_reduce(cols[0], lg, axis=AX.X, op=ALU.max))
            nc.vector.tensor_tensor(lg, lg, over_e(cols[0]), ALU.subtract).then_inc(S["lgd"], 1)
            dve.wait_ge(S["lgd"], 2)
            link(nc.vector.tensor_reduce(cols[0], lg, axis=AX.X, op=ALU.add))
            link(nc.vector.reciprocal(cols[0], cols[0]))
            link(nc.vector.tensor_tensor(pr, lg, over_e(cols[0]), ALU.mult))
            link(nc.vector.tensor_copy(rest, pr))
            for top, one in ((cols[1], one1), (cols[2], one2)):
                link(nc.vector.tensor_reduce(top, rest, axis=AX.X, op=ALU.max))
                link(nc.vector.tensor_tensor(hit, rest, over_e(top), ALU.is_equal))
                link(nc.vector.scalar_tensor_tensor(idx, hit, -float(E_), over_j(order), ALU.mult, ALU.add))
                link(nc.vector.tensor_reduce(cols[3], idx, axis=AX.X, op=ALU.min))
                link(nc.vector.tensor_tensor(one, idx, over_e(cols[3]), ALU.is_equal))
                if one is one1:
                    link(nc.vector.scalar_tensor_tensor(rest, one, -2.0, rest, ALU.mult, ALU.add))
            link(nc.vector.tensor_tensor(cols[1], cols[1], cols[2], ALU.add))
            link(nc.vector.reciprocal(cols[1], cols[1]))
            link(nc.vector.tensor_tensor(one1, one1, one2, ALU.add))
            link(nc.vector.tensor_tensor(pr, pr, one1, ALU.mult))
            nc.vector.tensor_tensor(disp[:, :, :], pr, over_e(cols[1]), ALU.mult).then_inc(S["rt"], 1)
            dv = dTs[:, :].rearrange("e (p j) -> e j p", j=PER)
            for g in range(12):
                dve.wait_ge(S["dt"], g + 1)
                k = min(4, PER - 4 * g)
                nc.vector.tensor_copy(dv[:, 4 * g:4 * g + k], P[5 + g % 2][0:EXPERTS, 0:k * 96].rearrange("e (j p) -> e j p", p=96)).then_inc(S["dte"], 1)
            def whole_sum(t):
                dve.wait_ge(S["acch"], t + 1)
                nc.vector.tensor_tensor(acc[:, t * NT:(t + 1) * NT], P[4 + t % 2][0:D, 0:NT], acc2[:, :], ALU.add).then_inc(S["accd"], 1)

            for n in range(STEPS + LO):
                if n < STEPS:
                    dve.wait_ge(S["h"], 2 * n + 2)
                    dve.wait_ge(S["silu"], n + 1)
                    if n >= 7:
                        dve.wait_ge(S["lo"], n - 6)
                    nc.vector.tensor_tensor(hid[:, n % 7, :], P[H_BANKS[1][n % 3]][:, 0:NT], s1[:, n % 3, :], ALU.mult).then_inc(S["prod"], 1)
                m = n - LO
                if m >= 0:
                    dve.wait_ge(S["hi"], m + 1)
                    nc.vector.tensor_tensor(hlo[:, m % 4, :], hid[:, m % 7, :], hhi[:, m % 4, :], ALU.subtract).then_inc(S["lo"], 1)
                t, e = n // EXPERTS, n % EXPERTS
                if e == 9 and t >= 1:
                    whole_sum(t - 1)
            whole_sum(11)
            for g in range(6):
                dve.wait_ge(S["ot"], g + 1)
                k = min(8, PER - g * 8)
                h = H[:, g * 512:g * 512 + k * D]
                nc.vector.tensor_tensor(h, P[6 + g % 2][0:96, 0:k * D], h, ALU.add).then_inc(S["fin"], 1)


def build(nc, a, out):
    f32 = mybir.dt.float32
    z_d = nc.dram_tensor("z_d", (PAIRS, 128, PX), f32).ap()
    X_d = nc.dram_tensor("X_d", (CHUNKS, WIDTH, IMG, 2 * CM), f32).ap()
    G_d = nc.dram_tensor("G_d", (IMG, 2, KY, KX * WIDTH), f32).ap()
    H_d = nc.dram_tensor("H_d", (IMG, SEQ * D), f32).ap()
    dT_d = nc.dram_tensor("dT_d", (EXPERTS, TOK), f32).ap()
    with ExitStack() as ctx:
        small = ctx.enter_context(nc.sbuf_tensor("small", [128, 64], f32))
        build_fno(nc, small, a["x6"], a["fc0"], a["fc0T"], a["fc0b"], a["wmix"], a["pwT"], a["pwb"], a["gamma"], a["beta"], a["consts"], z_d, X_d, G_d)
        build_head(nc, small[:, 12:13], small[:, 13:14], z_d, H_d, a["txt"], a["fc1"], a["fc1b"], a["fc2"], a["fc2b"])
        H = ctx.enter_context(nc.sbuf_tensor("H", [ROWS, PER * D], f32))
        build_attention(nc, H[:, :], H_d, a["wqkv"], a["bqkv"], a["w0"], a["b0"], a["aconst"])
        build_moe(nc, H[:, :], out, dT_d, a["gate"], a["gateb"], a["w12"], a["w3"], a["aconst"])


def kernel(**inputs):
    import numpy as _np
    import concourse.bacc as _bacc
    from concourse import mybir as _mybir
    from concourse.bass_utils import run_bass_kernel_spmd as _run

    d = {k: _np.asarray(v) for k, v in inputs.items()}
    f = {k[3:]: v for k, v in d.items() if k.startswith("L0_")}
    wr = _np.stack([f["tok_w1r"], f["tok_w2r"]], axis=1)
    wi = _np.stack([f["tok_w1i"], f["tok_w2i"]], axis=1)
    wmix = _np.stack([wr, wi], axis=2).reshape(LAYERS, 2, 128, WIDTH, 16, 16).transpose(0, 1, 4, 2, 5, 3)
    wqkv = f["attn_Wqkv"].reshape(D, 3, D, HEADS).transpose(0, 1, 3, 2)
    bqkv = f["attn_bqkv"].reshape(3, D, HEADS).transpose(2, 1, 0).reshape(HP, 128, 3).transpose(1, 2, 0)
    host = {
        "x6": d["x"].reshape(2, PAIRS, PX, CH).transpose(1, 0, 3, 2).reshape(PAIRS, 2 * CH, PX),
        "txt": d["txt"].reshape(IMG, TXT * D),
        "fc0": f["tok_fc0_w"], "fc0T": f["tok_fc0_w"].T, "fc0b": f["tok_fc0_b"].reshape(WIDTH, 1),
        "wmix": wmix.reshape(LAYERS, WP, 128, 16 * WIDTH),
        "pwT": f["tok_pw_w"].transpose(0, 2, 1),
        "pwb": f["tok_pw_b"].reshape(LAYERS, WIDTH, 1),
        "gamma": f["tok_gamma"].reshape(LAYERS, WIDTH, 1), "beta": f["tok_beta"].reshape(LAYERS, WIDTH, 1),
        "fc1": f["tok_fc1_w"], "fc1b": f["tok_fc1_b"].reshape(HIDDEN1, 1),
        "fc2": f["tok_fc2_w"], "fc2b": f["tok_fc2_b"].reshape(1, 1),
        "wqkv": wqkv.reshape(D, 12, 128), "bqkv": bqkv.reshape(128, 12),
        "w0": f["attn_W0"].reshape(D, HEADS, D).transpose(1, 0, 2).reshape(HP, 128, D).transpose(1, 0, 2),
        "b0": f["attn_b0"].reshape(D, 1),
        "gate": f["ffn_gate_w"], "gateb": f["ffn_gate_b"].reshape(1, EXPERTS),
        "w12": _np.concatenate([f["ffn_w1"], f["ffn_w2"]], axis=2).transpose(1, 0, 2),
        "w3": f["ffn_w3"].transpose(1, 0, 2),
        "consts": dft_constants(), "aconst": attention_constants(),
    }
    nc = _bacc.Bacc("TRN2", target_bir_lowering=False, num_devices=1)
    arrays, aps = {}, {}
    for name, value in host.items():
        value = _np.ascontiguousarray(value)
        arrays[f"in_{name}"] = value
        aps[name] = nc.dram_tensor(f"in_{name}", value.shape, _mybir.dt.from_np(value.dtype), kind="ExternalInput").ap()
    out = nc.dram_tensor("out_0", (IMG, SEQ * D), _mybir.dt.float32, kind="ExternalOutput").ap()
    build(nc, aps, out)
    r = _run(nc, [arrays], core_ids=[0])
    return r.results[0]["out_0"].reshape(IMG, SEQ, D)
```
